# Optimizing a Trainium2 kernel written in Bass

```python
import numpy as np
import jax
import jax.numpy as jnp

def _softmax(x, axis=-1):
    return jax.nn.softmax(x, axis=axis)

def _gelu(x):
    return jax.nn.gelu(x, approximate=True)

def _silu(x):
    return jax.nn.silu(x)

def _sigmoid(x):
    return jax.nn.sigmoid(x)

def _layernorm(x, axis=-1, eps=1e-05):
    m = jnp.mean(x, axis=axis, keepdims=True)
    v = jnp.var(x, axis=axis, keepdims=True)
    return (x - m) / jnp.sqrt(v + eps)

def _scatter_add(tgt, idx, src, axis=0):
    return tgt.at[idx].add(src)

def _segment_sum(src, seg, n):
    return jax.ops.segment_sum(src, seg, n)
kernel_name = 'mk_gnn_preln_d4_gnn_r8_3c915c'

def setup_inputs(seed: int=0):
    np.random.seed(seed)
    _w = jnp.asarray

    def _rec_inputs():
        import jax
        import jax.numpy as jnp
        _gk = jax.random.key(seed)
        x = -0.0009044 + 1 * jax.random.normal(jax.random.fold_in(_gk, 1), (12500, 16), jnp.float32)
        src = jax.random.randint(jax.random.fold_in(_gk, 2), (400000,), 0, 12500, jnp.int32)
        dst = jax.random.randint(jax.random.fold_in(_gk, 3), (400000,), 0, 12500, jnp.int32)
        _o = jnp.argsort(dst, stable=True)
        src = src[_o]
        dst = dst[_o]
        edge_attr_2 = 0.000411684 + 0.577418 * jax.random.normal(jax.random.fold_in(_gk, 12), (400000, 2), jnp.float32)
        edge_attr_8 = -5.3897e-05 + 0.999841 * jax.random.normal(jax.random.fold_in(_gk, 13), (400000, 8), jnp.float32)
        edge_type_8 = jax.random.randint(jax.random.fold_in(_gk, 15), (400000,), 0, 8, jnp.int32)
        edge_weight = -0.000107899 + 1.00008 * jax.random.normal(jax.random.fold_in(_gk, 16), (400000,), jnp.float32)
        node_vec1 = -0.00472126 + 0.997171 * jax.random.normal(jax.random.fold_in(_gk, 17), (12500, 1), jnp.float32)
        return (x, src, dst, edge_attr_2, edge_attr_8, edge_type_8, edge_weight, node_vec1)
    x, src, dst, edge_attr_2, edge_attr_8, edge_type_8, edge_weight, node_vec1 = _rec_inputs()

    def _L0_gnn_setup():
        import jax, jax.numpy as jnp
        import numpy as np
        N_NODES = 12500
        N_EDGES = 400000
        BATCH = 16
        LAYER_NUMBER = 4
        key = jax.random.key(seed)
        k1, k2, k3, k4 = jax.random.split(key, 4)
        x = jax.random.normal(k1, (N_NODES, BATCH), dtype=jnp.float32)
        weights = jax.random.normal(k2, (N_EDGES,), dtype=jnp.float32)
        row = jax.random.randint(k3, (N_EDGES,), 0, N_NODES, dtype=jnp.int64)
        col = jax.random.randint(k4, (N_EDGES,), 0, N_NODES, dtype=jnp.int64)
        return {'x': x, 'weights': weights, 'row': row, 'col': col}
    _L0_gnn_all = _L0_gnn_setup()
    _L0_gnn_in = {k: v for k, v in _L0_gnn_all.items() if k in ()}
    del _L0_gnn_all

    def _L1_gnn_setup():
        import jax, jax.numpy as jnp
        import numpy as np
        N_NODES = 12500
        N_EDGES = 200000
        F_IN = 16
        F_OUT = 16
        N_BASIS = 4

        def linear_basis(u, n):
            centers = jnp.linspace(-1.0, 1.0, n, dtype=u.dtype)
            dx = 2.0 / (n - 1)
            return jnp.maximum(0.0, 1.0 - jnp.abs(u[:, None] - centers[None, :]) / dx)
        key = jax.random.key(seed)
        k1, k2, k3, k4, k5 = jax.random.split(key, 5)
        x = jax.random.normal(k1, (N_NODES, F_IN), dtype=jnp.float32)
        edge_index = jax.random.randint(k2, (2, N_EDGES), 0, N_NODES, dtype=jnp.int64)
        edge_attr = jax.random.uniform(k3, (N_EDGES, 2), dtype=jnp.float32, minval=-1.0, maxval=1.0)
        weight = jax.random.uniform(k4, (N_BASIS, N_BASIS, F_IN, F_OUT), dtype=jnp.float32, minval=-0.05, maxval=0.05)
        return {'x': x, 'edge_index': edge_index, 'edge_attr': edge_attr, 'weight': weight}
    _L1_gnn_all = _L1_gnn_setup()
    _L1_gnn_in = {k: v for k, v in _L1_gnn_all.items() if k in ('weight',)}
    del _L1_gnn_all

    def _L2_gnn_setup():
        import jax, jax.numpy as jnp
        import numpy as np
        NUM_ENTITIES = 12500
        NUM_RELATIONS = 8
        NUM_CLASSES = 16
        HIDDEN = 16
        NUM_EDGES = 400000

        def rgcn_conv(x, src, dst, edge_type, W, root, bias):
            num_nodes = x.shape[0]
            x_src = x[src]
            msg = jnp.zeros((src.shape[0], W.shape[2]), x.dtype)
            for r in range(NUM_RELATIONS):
                msg = msg + jnp.where((edge_type == r)[:, None], x_src @ W[r], jnp.zeros((), x.dtype))
            cnt = jnp.zeros((num_nodes, NUM_RELATIONS), x.dtype).at[dst, edge_type].add(1.0)
            norm = 1.0 / jnp.maximum(cnt[dst, edge_type], 1.0)
            agg = jax.ops.segment_sum(msg * norm[:, None], dst, num_segments=num_nodes)
            return agg + x @ root + bias
        key = jax.random.key(seed)
        ks = jax.random.split(key, 9)
        s = 1.0 / np.sqrt(HIDDEN)
        edge_index = jax.random.randint(ks[0], (2, NUM_EDGES), 0, NUM_ENTITIES, dtype=jnp.int32)
        edge_type = jax.random.randint(ks[1], (NUM_EDGES,), 0, NUM_RELATIONS, dtype=jnp.int32)
        return {'embed': jax.random.normal(ks[2], (NUM_ENTITIES, HIDDEN), jnp.float32), 'W1': jax.random.normal(ks[3], (NUM_RELATIONS, HIDDEN, HIDDEN), jnp.float32) * s, 'root1': jax.random.normal(ks[4], (HIDDEN, HIDDEN), jnp.float32) * s, 'b1': jnp.zeros((HIDDEN,), jnp.float32), 'W2': jax.random.normal(ks[5], (NUM_RELATIONS, HIDDEN, NUM_CLASSES), jnp.float32) * s, 'root2': jax.random.normal(ks[6], (HIDDEN, NUM_CLASSES), jnp.float32) * s, 'b2': jnp.zeros((NUM_CLASSES,), jnp.float32), 'edge_index': edge_index, 'edge_type': edge_type}
    _L2_gnn_all = _L2_gnn_setup()
    _L2_gnn_in = {k: v for k, v in _L2_gnn_all.items() if k in ('W1', 'root1', 'b1', 'W2', 'root2', 'b2')}
    del _L2_gnn_all

    def _L3_gnn_setup():
        import jax, jax.numpy as jnp
        import numpy as np
        N_NODES = 12500
        N_EDGES = 400000
        D_NODE = 16
        D_EDGE = 8
        D_HIDDEN = 16
        key = jax.random.key(seed)
        ks = jax.random.split(key, 8)
        node_features = jax.random.normal(ks[0], (N_NODES, D_NODE), dtype=jnp.float32)
        edge_attr_e3nn = jax.random.normal(ks[1], (N_EDGES, D_EDGE), dtype=jnp.float32)
        node_attr_scalar_raw = jax.random.normal(ks[2], (N_NODES, 1), dtype=jnp.float32)
        W_msg_tp = jax.random.normal(ks[3], (D_NODE, D_EDGE, D_HIDDEN), dtype=jnp.float32)
        W_msg_lin = jax.random.normal(ks[4], (D_HIDDEN, D_HIDDEN), dtype=jnp.float32)
        W_upd_tp = jax.random.normal(ks[5], (D_NODE, D_HIDDEN, D_HIDDEN), dtype=jnp.float32)
        W_upd_lin = jax.random.normal(ks[6], (D_HIDDEN, D_NODE), dtype=jnp.float32)
        edge_index = jax.random.randint(ks[7], (2, N_EDGES), 0, N_NODES, dtype=jnp.int64)
        return {'node_features': node_features, 'edge_attr_e3nn': edge_attr_e3nn, 'node_attr_scalar_raw': node_attr_scalar_raw, 'W_msg_tp': W_msg_tp, 'W_msg_lin': W_msg_lin, 'W_upd_tp': W_upd_tp, 'W_upd_lin': W_upd_lin, 'edge_index': edge_index}
    _L3_gnn_all = _L3_gnn_setup()
    _L3_gnn_in = {k: v for k, v in _L3_gnn_all.items() if k in ('W_msg_tp', 'W_msg_lin', 'W_upd_tp', 'W_upd_lin')}
    del _L3_gnn_all
    return {'x': x, 'src': src, 'dst': dst, 'edge_attr_2': edge_attr_2, 'edge_attr_8': edge_attr_8, 'edge_type_8': edge_type_8, 'edge_weight': edge_weight, 'node_vec1': node_vec1, 'L1_gnn_weight': _L1_gnn_in['weight'], 'L2_gnn_W1': _L2_gnn_in['W1'], 'L2_gnn_root1': _L2_gnn_in['root1'], 'L2_gnn_b1': _L2_gnn_in['b1'], 'L2_gnn_W2': _L2_gnn_in['W2'], 'L2_gnn_root2': _L2_gnn_in['root2'], 'L2_gnn_b2': _L2_gnn_in['b2'], 'L3_gnn_W_msg_tp': _L3_gnn_in['W_msg_tp'], 'L3_gnn_W_msg_lin': _L3_gnn_in['W_msg_lin'], 'L3_gnn_W_upd_tp': _L3_gnn_in['W_upd_tp'], 'L3_gnn_W_upd_lin': _L3_gnn_in['W_upd_lin']}

def reference(x, src, dst, edge_attr_2, edge_attr_8, edge_type_8, edge_weight, node_vec1, L1_gnn_weight, L2_gnn_W1, L2_gnn_root1, L2_gnn_b1, L2_gnn_W2, L2_gnn_root2, L2_gnn_b2, L3_gnn_W_msg_tp, L3_gnn_W_msg_lin, L3_gnn_W_upd_tp, L3_gnn_W_upd_lin):
    import jax
    import jax.numpy as jnp

    def _L0_gnn_ref(x, weights, row, col):
        import jax, jax.numpy as jnp
        import numpy as np
        N_NODES = 12500
        N_EDGES = 400000
        BATCH = 16
        LAYER_NUMBER = 4

        def step(y, _):
            msg = weights[:, None] * y[col]
            y_new = jax.ops.segment_sum(msg, row, num_segments=N_NODES)
            return (y_new, None)
        y, _ = jax.lax.scan(step, x, None, length=LAYER_NUMBER)
        return y

    def _L1_gnn_ref(x, edge_index, edge_attr, weight):
        import jax, jax.numpy as jnp
        import numpy as np
        N_NODES = 12500
        N_EDGES = 200000
        F_IN = 16
        F_OUT = 16
        N_BASIS = 4

        def linear_basis(u, n):
            centers = jnp.linspace(-1.0, 1.0, n, dtype=u.dtype)
            dx = 2.0 / (n - 1)
            return jnp.maximum(0.0, 1.0 - jnp.abs(u[:, None] - centers[None, :]) / dx)
        "BasisConvLayer forward, mode='conv', linear basis, no bias/activations.\n\n            For each edge e=(i<-j): msg_e = sum_{u,v} b_u(dx) b_v(dy) * (x_j @ W[u,v]);\n            out[i] = sum over incoming edges of msg_e.\n            "
        row, col = (edge_index[0], edge_index[1])
        x_j = x[col]
        bx = linear_basis(edge_attr[:, 0], N_BASIS)
        by = linear_basis(edge_attr[:, 1], N_BASIS)
        t = (bx[:, :, None] * by[:, None, :]).reshape(-1, N_BASIS * N_BASIS)
        w_flat = weight.reshape(N_BASIS * N_BASIS, F_IN, F_OUT)
        msg = jnp.zeros((x_j.shape[0], F_OUT), dtype=x.dtype)
        for k in range(N_BASIS * N_BASIS):
            msg = msg + t[:, k, None] * (x_j @ w_flat[k])
        out = jax.ops.segment_sum(msg, row, num_segments=N_NODES)
        return out

    def _L2_gnn_ref(embed, W1, root1, b1, W2, root2, b2, edge_index, edge_type):
        import jax, jax.numpy as jnp
        import numpy as np
        NUM_ENTITIES = 12500
        NUM_RELATIONS = 8
        NUM_CLASSES = 16
        HIDDEN = 16
        NUM_EDGES = 400000

        def rgcn_conv(x, src, dst, edge_type, W, root, bias):
            num_nodes = x.shape[0]
            x_src = x[src]
            msg = jnp.zeros((src.shape[0], W.shape[2]), x.dtype)
            for r in range(NUM_RELATIONS):
                msg = msg + jnp.where((edge_type == r)[:, None], x_src @ W[r], jnp.zeros((), x.dtype))
            cnt = jnp.zeros((num_nodes, NUM_RELATIONS), x.dtype).at[dst, edge_type].add(1.0)
            norm = 1.0 / jnp.maximum(cnt[dst, edge_type], 1.0)
            agg = jax.ops.segment_sum(msg * norm[:, None], dst, num_segments=num_nodes)
            return agg + x @ root + bias
        src, dst = (edge_index[0], edge_index[1])
        h = rgcn_conv(embed, src, dst, edge_type, W1, root1, b1)
        h = jax.nn.relu(h)
        h = rgcn_conv(h, src, dst, edge_type, W2, root2, b2)
        return jax.nn.log_softmax(h, axis=1)

    def _L3_gnn_ref(node_features, edge_attr_e3nn, node_attr_scalar_raw, W_msg_tp, W_msg_lin, W_upd_tp, W_upd_lin, edge_index):
        import jax, jax.numpy as jnp
        import numpy as np
        N_NODES = 12500
        N_EDGES = 400000
        D_NODE = 16
        D_EDGE = 8
        D_HIDDEN = 16
        n_nodes = node_features.shape[0]
        row = edge_index[0]
        col = edge_index[1]
        norm_msg_tp = 1.0 / np.float32(np.sqrt(D_NODE * D_EDGE))
        norm_upd_tp = 1.0 / np.float32(np.sqrt(D_NODE * D_HIDDEN))
        norm_lin = 1.0 / np.float32(np.sqrt(D_HIDDEN))
        x_j = node_features[col]
        m = jnp.einsum('ei,ej,ijh->eh', x_j, edge_attr_e3nn, W_msg_tp) * norm_msg_tp
        m = jax.nn.silu(m)
        m = m @ W_msg_lin * norm_lin
        agg = jax.ops.segment_sum(m, row, num_segments=n_nodes)
        u = jnp.einsum('ni,nh,ihk->nk', node_features, agg, W_upd_tp) * norm_upd_tp
        u = jax.nn.silu(u)
        u = u @ W_upd_lin * norm_lin
        return node_features + u
    edge_index = jnp.stack([src, dst])
    h = jnp.maximum(_layernorm(x, axis=-1), 0.0)
    x = x + _L0_gnn_ref(h, edge_weight, src, dst)
    h = jnp.maximum(_layernorm(x, axis=-1), 0.0)
    x = x + _L1_gnn_ref(h, edge_index, edge_attr_2, L1_gnn_weight)
    h = jnp.maximum(_layernorm(x, axis=-1), 0.0)
    x = x + _L2_gnn_ref(h, L2_gnn_W1, L2_gnn_root1, L2_gnn_b1, L2_gnn_W2, L2_gnn_root2, L2_gnn_b2, edge_index, edge_type_8)
    h = jnp.maximum(_layernorm(x, axis=-1), 0.0)
    x = x + _L3_gnn_ref(h, edge_attr_8, node_vec1, L3_gnn_W_msg_tp, L3_gnn_W_msg_lin, L3_gnn_W_upd_tp, L3_gnn_W_upd_lin, edge_index)
    return x

_drawn_inputs = setup_inputs


def setup_inputs(seed=0):
    import zlib

    import numpy as np

    out = dict(_drawn_inputs(seed))
    spreads = {'L2_gnn_b1': (0.0, 0.1), 'L2_gnn_b2': (0.0, 0.1)}
    factors = {}
    for name, (base, spread) in spreads.items():
        noise = np.random.default_rng([zlib.crc32(name.encode()), seed]).standard_normal(out[name].shape)
        drawn = base * np.exp(spread * noise) if base else spread * noise
        out[name] = jnp.asarray(drawn.astype(out[name].dtype))
    for name, factor in factors.items():
        out[name] = (out[name] * factor).astype(out[name].dtype)
    return out
```

```python
from contextlib import ExitStack

import concourse.bass as bass
from concourse import mybir

F32 = mybir.dt.float32
BF16 = mybir.dt.bfloat16
I32 = mybir.dt.int32
ALU = mybir.AluOpType
ACT = mybir.ActivationFunctionType
AX = mybir.AxisListType

P = 128
N_NODES = 12500
N_EDGES = 400000
D = 16
COLS = N_EDGES // P
HI = -(-N_NODES // P)
ROWS = P * HI
FULL = N_NODES // P
REST = N_NODES - FULL * P
TILES = 5
SLOTS = 5
TURN = TILES * SLOTS
TURNS = COLS // TURN
assert COLS == TURNS * TURN and P * COLS == N_EDGES and HI * TILES <= 512

REC_BY_SRC = 16
REC_BY_DST = 8


def loop(eng, turns, body):
    body(0, True)
    with eng.Fori(1, turns) as turn:
        body(turn, False)


class Line:

    def __init__(self, eng, sem):
        self.eng, self.sem, self.count = eng, sem, 0

    def do(self, ins):
        self.count += 1
        ins.then_inc(self.sem, 1)
        self.eng.wait_ge(self.sem, self.count)


class Scope:

    def __init__(self, nc, name):
        self.nc, self.name, self.stack, self.taken = nc, name, ExitStack(), []

    def __enter__(self):
        self.stack.__enter__()
        return self

    def __exit__(self, *e):
        self.stack.__exit__(*e)
        if self.taken:
            self.nc.clear_and_free_semaphores(self.taken)
            self.nc.all_engine_barrier()

    def sb(self, name, shape, dt=F32):
        return self.stack.enter_context(self.nc.sbuf_tensor(f"{self.name}_{name}", shape, dt))

    def ps(self, name, shape, dt=F32):
        return self.stack.enter_context(self.nc.psum_tensor(f"{self.name}_{name}", shape, dt))

    def sem(self, name):
        self.taken.append(self.nc.alloc_semaphore(f"{self.name}_{name}"))
        return self.taken[-1]

    def sems(self, name, n):
        return [self.sem(f"{name}{i}") for i in range(n)]

    def block(self):
        return self.stack.enter_context(self.nc.Block())


def constants(nc, c, x, X):
    with Scope(nc, "const") as s:
        iota_i = s.sb("iota_i", [P, P], I32)
        lane_i = s.sb("lane_i", [P, 1], I32)
        made, iotas, zeroed, x_in = s.sem("made"), s.sem("iotas"), s.sem("zeroed"), s.sem("x_in")
        block = s.block()

        @block.gpsimd
        def _(pool):
            pool.iota(iota_i[:], pattern=[[1, P]], base=0, channel_multiplier=0).then_inc(iotas, 1)
            pool.iota(lane_i[:], pattern=[[0, 1]], base=0, channel_multiplier=1).then_inc(iotas, 1)

        @block.vector
        def _(dve):
            line = Line(dve, made)
            dve.memset(X[:], 0.0).then_inc(zeroed, 1)
            dve.wait_ge(iotas, 2)
            line.do(dve.tensor_copy(c.free[:], iota_i[:]))
            line.do(dve.tensor_copy(c.free_b[:], iota_i[:]))
            line.do(dve.tensor_copy(c.lane[:], lane_i[:]))
            line.do(dve.tensor_scalar(c.ident[:], c.free[:], c.lane[:, 0:1], None, ALU.is_equal))
            line.do(dve.tensor_copy(c.ident_b[:], c.ident[:]))
            line.do(dve.tensor_scalar(c.above[:], c.free[:], c.lane[:, 0:1], None, ALU.is_gt))
            line.do(dve.tensor_copy(c.above_b[:], c.above[:]))
            line.do(dve.tensor_scalar(c.down[:], c.free[:], -1.0, c.lane[:, 0:1], ALU.add, ALU.is_equal))
            line.do(dve.tensor_scalar(c.up[:], c.free[:], 1.0, c.lane[:, 0:1], ALU.add, ALU.is_equal))

        @block.sync
        def _(sp):
            sp.wait_ge(zeroed, 1)
            sp.dma_start(X[:, 0:FULL, :], x[0:FULL * P, :].rearrange("(h p) d -> p h d", p=P)).then_inc(x_in, 16)
            sp.dma_start(X[0:REST, FULL, :], x[FULL * P:N_NODES, :]).then_inc(x_in, 16)
            sp.wait_ge(x_in, 32)


def digits(nc, c, key, name, lo_b, hi_b, row):
    with Scope(nc, f"digits_{name}") as s:
        ids = s.sb("ids", [P, COLS], I32)
        lo_i = s.sb("lo_i", [P, COLS], I32)
        hi_i = s.sb("hi_i", [P, COLS], I32)
        turned = s.sb("turned", [125, 25, P], BF16)
        flipped = s.ps("flipped", [P, 2, 1024], BF16)
        loaded, line_sem = s.sem("loaded"), s.sem("line")
        lows, flips, copied, stored = s.sem("lows"), s.sem("flips"), s.sem("copied"), s.sem("stored")
        low_rows = nc.dram_tensor(f"low_rows_{name}", (COLS, P), BF16).ap()
        block = s.block()

        @block.sync
        def _(sp):
            sp.dma_start(ids[:], key.rearrange("(p c) -> p c", p=P)).then_inc(loaded, 16)
            sp.wait_ge(copied, 25)
            sp.dma_start(low_rows.rearrange("(j k) e -> j (k e)", k=25),
                         turned[:].rearrange("j k e -> j (k e)")).then_inc(stored, 16)
            sp.wait_ge(stored, 16)

        @block.vector
        def _(dve):
            line = Line(dve, line_sem)
            dve.wait_ge(loaded, 16)
            line.do(dve.tensor_scalar(lo_i[:], ids[:], 127, None, ALU.bitwise_and))
            line.do(dve.tensor_scalar(hi_i[:], ids[:], 7, None, ALU.arith_shift_right))
            dve.tensor_copy(lo_b[:], lo_i[:]).then_inc(lows, 1)
            line.do(dve.tensor_copy(hi_b[:], hi_i[:]))
            dve.wait_ge(lows, 1)
            line.do(dve.scalar_tensor_tensor(out=row[:], in0=lo_b[:], scalar=float(HI), in1=hi_b[:],
                                             op0=ALU.mult, op1=ALU.add))

        @block.tensor
        def _(pe):
            pe.wait_ge(lows, 1)
            for k in range(25):
                if k >= 2:
                    pe.wait_ge(copied, k - 1)
                pe.transpose(flipped[0:125, k % 2, 0:P], lo_b[:, k::25], c.ident_b[:]).then_inc(flips, 1)

        @block.scalar
        def _(act):
            for k in range(25):
                act.wait_ge(flips, k + 1)
                act.copy(turned[:, k, :], flipped[0:125, k % 2, 0:P]).then_inc(copied, 1)
    return low_rows


def one_hots(dve, c, lo_b, hi_b, cols, lo_hot, hi_hot, done):
    dve.tensor_tensor(lo_hot, lo_b[:, cols].unsqueeze(2).to_broadcast([P, TILES, P]),
                      c.free_b[:, 0:P].unsqueeze(1).to_broadcast([P, TILES, P]), ALU.is_equal)
    dve.tensor_tensor(hi_hot, hi_b[:, cols].unsqueeze(2).to_broadcast([P, TILES, HI]),
                      c.free_b[:, 0:HI].unsqueeze(1).to_broadcast([P, TILES, HI]), ALU.is_equal).then_inc(done, 1)


def count(nc, c, name, lo_b, hi_b, info):
    with Scope(nc, f"count_{name}") as s:
        lo_hot = s.sb("lo_hot", [P, SLOTS, TILES, P], BF16)
        hi_hot = s.sb("hi_hot", [P, SLOTS, TILES, HI], BF16)
        zeros = s.sb("zeros", [P, P], BF16)
        total = s.sb("total", [P, 1])
        run = s.sb("run", [P, HI])
        pc = s.ps("counts", [P, 512])
        po = s.ps("offsets", [P, 512])
        hot, counted, line_sem = s.sem("hot"), s.sem("counted"), s.sem("line")
        zeroed, totals, offs = s.sem("zeroed"), s.sem("totals"), s.sem("offs")
        block = s.block()

        @block.vector
        def _(dve):
            dve.memset(zeros[:], 0.0).then_inc(zeroed, 1)

            def body(turn, first):
                for k in range(SLOTS):
                    if not first:
                        dve.wait_ge(counted, (turn - 1) * SLOTS + k + 1)
                    one_hots(dve, c, lo_b, hi_b, bass.ds(turn * TURN + k * TILES, TILES),
                             lo_hot[:, k], hi_hot[:, k], hot)

            loop(dve, TURNS, body)
            line = Line(dve, line_sem)
            dve.wait_ge(counted, TURNS * SLOTS)
            line.do(dve.tensor_copy(info.cnt[:], pc[:, 0:HI]))
            line.do(dve.memset(run[:], 1.0))
            line.do(dve.tensor_tensor_scan(info.start[:], run[:], info.cnt[:], 0.0, ALU.mult, ALU.add))
            dve.tensor_copy(total[:], info.start[:, HI - 1:HI]).then_inc(totals, 1)
            line.do(dve.tensor_tensor(run[:], info.start[:], info.cnt[:], ALU.subtract))
            dve.wait_ge(offs, 1)
            line.do(dve.tensor_scalar(info.start[:], run[:], po[:, 0:1], None, ALU.add))
            line.do(dve.tensor_tensor(run[:], info.start[:], info.cnt[:], ALU.add))
            line.do(dve.tensor_scalar(run[:], run[:], -1.0, 0.0, ALU.add, ALU.max))
            line.do(dve.tensor_copy(info.end_i[:], run[:]))
            line.do(dve.tensor_scalar(info.used[:], info.cnt[:], 1.0, None, ALU.min))

        @block.tensor
        def _(pe):
            pe.wait_ge(zeroed, 1)
            pe.matmul(pc[:, 0:HI], zeros[:], zeros[:, 0:HI], start=True, stop=True)

            def body(turn, first):
                for k in range(SLOTS):
                    pe.wait_ge(hot, turn * SLOTS + k + 1)
                    for j in range(TILES):
                        mm = pe.matmul(pc[:, 0:HI], lo_hot[:, k, j, :], hi_hot[:, k, j, :],
                                       start=False, stop=True, skip_group_check=True)
                    mm.then_inc(counted, 1)

            loop(pe, TURNS, body)
            pe.wait_ge(totals, 1)
            pe.matmul(po[:, 0:1], c.above[:], total[:], start=True, stop=True).then_inc(offs, 1)


def sort_edges(nc, c, name, lo_b, hi_b, low_rows, info, words, columns, parts, rec):
    with Scope(nc, f"sort_{name}") as s:
        lo_hot = s.sb("lo_hot", [P, SLOTS, TILES, P], BF16)
        hi_hot = s.sb("hi_hot", [P, SLOTS, TILES, HI], BF16)
        lo_row = s.sb("lo_row", [P, SLOTS, TILES * P], BF16)
        lo_hot_t = s.sb("lo_hot_t", [P, SLOTS, TILES, P])
        before = s.sb("before", [P, SLOTS, TILES, P], BF16)
        place = s.sb("place", [P, TILES, P])
        picked = s.sb("picked", [P, TILES, HI])
        pos_f = s.sb("pos_f", [P, TILES])
        pos_i = s.sb("pos_i", [P, SLOTS, TILES], I32)
        record = s.sb("record", [P, SLOTS, TILES, words])
        staged = [s.sb(f"staged{w}", [P, SLOTS, TILES * n]) for w, n, _ in parts]
        pcount = s.ps("pcount", [P, 512])
        pread = s.ps("pread", [P, SLOTS, 512])
        hot, rows_in, parts_in = s.sem("hot"), s.sems("rows_in", SLOTS), s.sems("parts_in", SLOTS)
        hot_t, counter, added = s.sem("hot_t"), s.sem("counter"), s.sem("added")
        read, pick, pos, posd = s.sem("read"), s.sem("pick"), s.sem("pos"), s.sem("posd")
        built, scattered, zeroed, gate = s.sem("built"), s.sems("scattered", SLOTS), s.sem("zeroed"), s.sem("gate")
        block = s.block()

        @block.sync
        def _(sp):
            def body(turn, first):
                for k in range(SLOTS):
                    if not first:
                        sp.wait_ge(hot_t, (turn - 1) * SLOTS + k + 1)
                        sp.wait_ge(built, (turn - 1) * SLOTS + k + 1)
                    src = low_rows[bass.ds(turn * TURN + k * TILES, TILES), :]
                    sp.dma_start(lo_row[:, k, :], src.rearrange("t e -> (t e)").unsqueeze(0).to_broadcast([P, TILES * P])
                                 ).then_inc(rows_in[k], 16)
                    for (w, n, dram), st in zip(parts, staged):
                        sp.dma_start(st[:, k, :], dram.rearrange("(p c) w -> p (c w)", p=P)
                                     [:, bass.ds((turn * TURN + k * TILES) * n, TILES * n)]).then_inc(parts_in[k], 16)

            loop(sp, TURNS, body)

        @block.vector
        def _(dve):
            if words > columns[-1][0] + 1:
                dve.memset(record[:], 0.0)
            dve.memset(picked[:], 0.0).then_inc(zeroed, 1)

            def prepare(turn, first, k):
                if not first:
                    dve.wait_ge(read, (turn - 1) * SLOTS + k + 1)
                cols = bass.ds(turn * TURN + k * TILES, TILES)
                one_hots(dve, c, lo_b, hi_b, cols, lo_hot[:, k], hi_hot[:, k], hot)
                dve.wait_ge(rows_in[k], turn * 16 + 16)
                dve.tensor_scalar(lo_hot_t[:, k].rearrange("p t e -> p (t e)"), lo_row[:, k, :],
                                  c.lane[:, 0:1], None, ALU.is_equal)
                for j in range(TILES):
                    ins = dve.scalar_tensor_tensor(
                        out=before[:, k, j, :], in0=lo_row[:, k, j * P:(j + 1) * P],
                        scalar=lo_b[:, bass.ds(turn * TURN + k * TILES + j, 1)], in1=c.above_b[:],
                        op0=ALU.is_equal, op1=ALU.mult)
                ins.then_inc(hot_t, 1)

            def finish(turn, first, k):
                n = turn * SLOTS + k
                dve.wait_ge(read, n + 1)
                dve.tensor_tensor(picked[:], pread[:, k, 0:TILES * HI].rearrange("p (t h) -> p t h", t=TILES),
                                  hi_hot[:, k], ALU.mult).then_inc(pick, 1)
                dve.wait_ge(pick, n + 1)
                dve.tensor_reduce(pos_f[:], picked[:], AX.X, ALU.add).then_inc(pos, 1)
                dve.wait_ge(pos, n + 1)
                if not first:
                    dve.wait_ge(scattered[k], turn * (16 * TILES))
                dve.tensor_copy(pos_i[:, k, :], pos_f[:]).then_inc(posd, 1)

            def body(turn, first):
                for k in range(SLOTS):
                    prepare(turn, first, k)
                    if k >= 1:
                        finish(turn, first, k - 1)
                finish(turn, first, SLOTS - 1)

            loop(dve, TURNS, body)

        @block.tensor
        def _(pe):
            pe.matmul(pcount[:, 0:HI], c.ident[:], info.start[:], start=True, stop=True).then_inc(added, 1)

            def body(turn, first):
                for k in range(SLOTS):
                    pe.wait_ge(hot_t, turn * SLOTS + k + 1)
                    if not first:
                        pe.wait_ge(pick, (turn - 1) * SLOTS + k + 1)
                    for j in range(TILES):
                        tile = turn * TURN + k * TILES + j
                        pe.wait_ge(counter, tile + 1)
                        pe.matmul(pcount[:, 0:HI], lo_hot[:, k, j, :], hi_hot[:, k, j, :],
                                  start=False, stop=True, skip_group_check=True).then_inc(added, 1)
                        out = pread[:, k, j * HI:(j + 1) * HI]
                        pe.matmul(out, before[:, k, j, :], hi_hot[:, k, j, :], start=True, stop=False,
                                  skip_group_check=True)
                        mm = pe.matmul(out, lo_hot_t[:, k, j, :], place[:, j, 0:HI], start=False, stop=True,
                                       skip_group_check=True)
                    mm.then_inc(read, 1)

            loop(pe, TURNS, body)

        @block.scalar
        def _(act):
            act.wait_ge(zeroed, 1)
            act.wait_ge(added, 1)
            act.copy(place[:, 0, 0:HI], pcount[:, 0:HI]).then_inc(counter, 1)

            def build(turn, first, k):
                if not first:
                    act.wait_ge(scattered[k], turn * (16 * TILES))
                cols = bass.ds(turn * TURN + k * TILES, TILES)
                if parts:
                    act.wait_ge(parts_in[k], (turn + 1) * (16 * len(parts)))
                for (w, n, _), st in zip(parts, staged):
                    act.copy(record[:, k, :, w:w + n], st[:, k, :].rearrange("p (t n) -> p t n", n=n))
                for w, col in columns:
                    ins = act.copy(record[:, k, :, w], col[:, cols])
                ins.then_inc(built, 1)

            def body(turn, first):
                for k in range(SLOTS):
                    build(turn, first, k)
                    for j in range(TILES):
                        act.wait_ge(added, turn * TURN + k * TILES + j + 2)
                        act.copy(place[:, (j + 1) % TILES, 0:HI], pcount[:, 0:HI]).then_inc(counter, 1)

            loop(act, TURNS, body)

        @block.gpsimd
        def _(pool):
            def body(turn, first):
                for k in range(SLOTS):
                    pool.wait_ge(posd, turn * SLOTS + k + 1)
                    pool.sem_inc(gate, 1)
                    pool.wait_ge(built, turn * SLOTS + k + 1)
                    pool.sem_inc(gate, 1)
                    for j in range(TILES):
                        pool.indirect_dma_start(rec, bass.IndirectOffsetOnAxis(pos_i[:, k, j:j + 1], 0),
                                                record[:, k, j, :], None).then_inc(scattered[k], 16)

            loop(pool, TURNS, body)
            for k in range(SLOTS):
                pool.wait_ge(scattered[k], TURNS * 16 * TILES)


class Info:

    def __init__(self, sb, name):
        self.cnt, self.start, self.used = (sb(f"{name}_{n}", [P, HI]) for n in ("cnt", "start", "used"))
        self.end_i = sb(f"{name}_end", [P, HI], I32)


class Constants:
    def __init__(self, sb):
        self.free, self.ident, self.above, self.down, self.up = (
            sb(n, [P, P]) for n in ("free", "ident", "above", "down", "up"))
        self.free_b, self.ident_b, self.above_b = (sb(n, [P, P], BF16) for n in ("free_b", "ident_b", "above_b"))
        self.lane = sb("lane", [P, 1])

COLS_SLOT = 25
PASS_TURNS = COLS // (COLS_SLOT * SLOTS)
PAD = COLS_SLOT * SLOTS
BLOCK = 7
BLOCKS = HI // BLOCK
PIECE = 512
assert BLOCKS * BLOCK == HI and PASS_TURNS * COLS_SLOT * SLOTS == COLS


class Runs:

    def __init__(self, sb, name, info):
        self.info = info
        self.index = sb(f"{name}_index", [P, COLS + PAD], I32)
        self.weight = sb(f"{name}_weight", [P, COLS])
        self.goes_on = sb(f"{name}_goes_on", [P, COLS])
        self.first_lo = sb(f"{name}_first_lo", [P, P])
        self.first_hi = sb(f"{name}_first_hi", [P, HI])
        self.first_row = sb(f"{name}_first_row", [P, 1], I32)
        self.through = sb(f"{name}_through", [D, P])


def load_runs(nc, c, name, rec, words, runs, by_src):
    with Scope(nc, f"runs_{name}") as s:
        recs = s.sb("recs", [P, SLOTS, COLS_SLOT, words])
        row = s.sb("row", [P, COLS])
        firsts = s.sb("firsts", [P, words])
        tmp = s.sb("tmp", [P, 8])
        alive = s.sb("alive", [P, D])
        psh = s.ps("shifted", [P, 512])
        landed, taken_a, taken_v = s.sems("landed", SLOTS), s.sem("taken_a"), s.sem("taken_v")
        first_in, line_sem, ends, shifted = s.sem("first_in"), s.sem("line"), s.sem("ends"), s.sem("shifted")
        block = s.block()
        view = rec.rearrange("(p c) w -> p (c w)", p=P)

        @block.sync
        def _(sp):
            sp.dma_start(firsts[:], view[:, 0:words]).then_inc(first_in, 16)

            def body(turn, first):
                for k in range(SLOTS):
                    if not first:
                        sp.wait_ge(taken_a, (turn - 1) * SLOTS + k + 1)
                        sp.wait_ge(taken_v, (turn - 1) * SLOTS + k + 1)
                    at = (turn * SLOTS + k) * COLS_SLOT
                    sp.dma_start(recs[:, k].rearrange("p c w -> p (c w)"),
                                 view[:, bass.ds(at * words, COLS_SLOT * words)]).then_inc(landed[k], 16)

            loop(sp, PASS_TURNS, body)

        @block.scalar
        def _(act):
            def body(turn, first):
                for k in range(SLOTS):
                    act.wait_ge(landed[k], turn * 16 + 16)
                    act.copy(runs.weight[:, bass.ds((turn * SLOTS + k) * COLS_SLOT, COLS_SLOT)],
                             recs[:, k, :, 0]).then_inc(taken_a, 1)

            loop(act, PASS_TURNS, body)

        @block.vector
        def _(dve):
            def body(turn, first):
                for k in range(SLOTS):
                    cols = bass.ds((turn * SLOTS + k) * COLS_SLOT, COLS_SLOT)
                    dve.wait_ge(landed[k], turn * 16 + 16)
                    if by_src:
                        dve.tensor_copy(runs.index[:, cols], recs[:, k, :, 11])
                        ins = dve.tensor_copy(row[:, cols], recs[:, k, :, 12])
                    else:
                        dve.scalar_tensor_tensor(out=runs.index[:, cols], in0=recs[:, k, :, 1], scalar=8.0,
                                                 in1=recs[:, k, :, 0], op0=ALU.mult, op1=ALU.add)
                        ins = dve.tensor_copy(row[:, cols], recs[:, k, :, 2])
                    ins.then_inc(taken_v, 1)

            loop(dve, PASS_TURNS, body)
            at = 12 if by_src else 2
            line = Line(dve, line_sem)
            dve.wait_ge(taken_v, PASS_TURNS * SLOTS)
            line.do(dve.tensor_copy(runs.index[:, COLS:COLS + PAD], runs.index[:, 0:PAD]))
            line.do(dve.tensor_tensor(runs.goes_on[:, 1:COLS], row[:, 1:COLS], row[:, 0:COLS - 1], ALU.is_equal))
            dve.tensor_scalar(tmp[:, 0:1], row[:, COLS - 1:COLS], 1.0, None, ALU.add).then_inc(ends, 1)
            line.do(dve.tensor_scalar(tmp[:, 1:2], row[:, 0:1], 1.0, None, ALU.add))
            dve.wait_ge(shifted, 1)
            line.do(dve.tensor_tensor(runs.goes_on[:, 0:1], tmp[:, 1:2], psh[:, 0:1], ALU.is_equal))
            dve.tensor_copy(tmp[:, 2:3], runs.goes_on[:, 0:1]).then_inc(ends, 1)
            line.do(dve.tensor_reduce(tmp[:, 3:4], runs.goes_on[:], AX.X, ALU.min))
            dve.tensor_copy(alive[:], tmp[:, 3:4].to_broadcast([P, D])).then_inc(ends, 1)
            dve.wait_ge(shifted, 3)
            line.do(dve.tensor_copy(runs.through[:], psh[0:D, 128:256]))
            line.do(dve.tensor_tensor(tmp[:, 4:5], tmp[:, 3:4], psh[:, 1:2], ALU.mult))
            line.do(dve.tensor_scalar(tmp[:, 5:6], tmp[:, 4:5], -1.0, 1.0, ALU.mult, ALU.add))
            line.do(dve.tensor_tensor(tmp[:, 6:7], tmp[:, 5:6], tmp[:, 2:3], ALU.mult))
            dve.wait_ge(first_in, 16)
            line.do(dve.tensor_copy(runs.first_row[:], firsts[:, at:at + 1]))
            line.do(dve.tensor_scalar(runs.first_lo[:], c.free[:], firsts[:, at + 1:at + 2], None, ALU.is_equal))
            line.do(dve.tensor_scalar(runs.first_hi[:], c.free[:, 0:HI], firsts[:, at + 2:at + 3], tmp[:, 6:7],
                                      ALU.is_equal, ALU.mult))

        @block.tensor
        def _(pe):
            pe.wait_ge(ends, 1)
            pe.matmul(psh[:, 0:1], c.down[:], tmp[:, 0:1], start=True, stop=True).then_inc(shifted, 1)
            pe.wait_ge(ends, 2)
            pe.matmul(psh[:, 1:2], c.up[:], tmp[:, 2:3], start=True, stop=True).then_inc(shifted, 1)
            pe.wait_ge(ends, 3)
            pe.matmul(psh[0:D, 128:256], alive[:], c.ident[:], start=True, stop=True).then_inc(shifted, 1)


class Carry:

    def __init__(self, s, width):
        self.width = width
        self.last = s.sb("last", [P, width])
        self.rows = s.sb("rows", [width, P + 1])
        self.spread = s.sb("spread", [P, HI, width])
        self.pt = s.ps("last_rows", [P, 512])
        self.fix = s.ps("fix", [P, 4 * PIECE])
        self.last_done, self.turned, self.scanned, self.back, self.laid, self.fixed = (
            s.sem(n) for n in ("last_done", "turned", "carry_scanned", "back", "laid", "fixed"))

    def tensor(self, pe, c, runs, r):
        w = self.width
        pe.wait_ge(self.last_done, r + 1)
        pe.transpose(self.pt[0:w, 0:P], self.last[:], c.ident[:]).then_inc(self.turned, 1)
        pe.wait_ge(self.scanned, r + 1)
        pe.matmul(self.pt[:, P:P + w], self.rows[:, 0:P], c.ident[0:w, 0:w], start=True, stop=True
                  ).then_inc(self.back, 1)
        pe.wait_ge(self.laid, r + 1)
        flat = self.spread[:].rearrange("p h f -> p (h f)")
        for at in range(0, HI * w, PIECE):
            to = min(at + PIECE, HI * w)
            mm = pe.matmul(self.fix[:, at:to], runs.first_lo[:], flat[:, at:to], start=True, stop=True)
        mm.then_inc(self.fixed, 1)

    def vector(self, dve, runs, r):
        w = self.width
        dve.wait_ge(self.turned, r + 1)
        dve.tensor_tensor_scan(self.rows[:, 1:P + 1], runs.through[0:w, :], self.pt[0:w, 0:P], 0.0,
                               ALU.mult, ALU.add).then_inc(self.scanned, 1)
        dve.wait_ge(self.back, r + 1)
        dve.tensor_tensor(self.spread[:], runs.first_hi[:].unsqueeze(2).to_broadcast([P, HI, w]),
                          self.pt[:, P:P + w].unsqueeze(1).to_broadcast([P, HI, w]), ALU.mult
                          ).then_inc(self.laid, 1)

    def add(self, dve, runs, r, ends, out, masked, done):
        w = self.width
        dve.tensor_tensor(out, ends, runs.info.used[:].unsqueeze(2).to_broadcast([P, HI, w]), ALU.mult
                          ).then_inc(masked, 1)
        dve.wait_ge(masked, r + 1)
        dve.wait_ge(self.fixed, r + 1)
        dve.tensor_tensor(out, out, self.fix[:, 0:HI * w].rearrange("p (h f) -> p h f", f=w), ALU.add
                          ).then_inc(done, 1)


def gather_ends(pool, runs, sums, ends, ends_in):
    for h in range(HI):
        pool.indirect_dma_start(ends[:, h, :], None, sums,
                                bass.IndirectOffsetOnAxis(runs.info.end_i[:, h:h + 1], 0)).then_inc(ends_in, 16)


def weighted_sums(nc, c, name, runs, table, sums, Y, rounds, table_from=None):
    with Scope(nc, name) as s:
        picked = s.sb("picked", [P, SLOTS, COLS_SLOT, D])
        staged = s.sb("staged", [P, SLOTS, COLS_SLOT], I32)
        message = s.sb("message", [P, COLS_SLOT, D])
        running = s.sb("running", [P, SLOTS, COLS_SLOT, D])
        ends = s.sb("ends", [P, HI, D])
        carry = Carry(s, D)
        staged_done, gathered = s.sems("staged_done", SLOTS), s.sems("gathered", SLOTS)
        weighed, scanned, kept, stored, free = (s.sem(n) for n in ("weighed", "scanned", "kept", "stored", "free"))
        ends_in, masked, y_done, table_in, gate = (
            s.sem(n) for n in ("ends_in", "masked", "y_done", "table_in", "gate"))
        block = s.block()
        slots = PASS_TURNS * SLOTS
        flat = sums.rearrange("(p c) f -> p (c f)", p=P)
        stores = table_from is not None
        table_rows = table.rearrange("(p h) d -> p (h d)", p=P) if stores else None

        def each_round(eng, body):
            if rounds == 1:
                body(0)
            else:
                with eng.Fori(0, rounds) as r:
                    body(r)

        @block.sync
        def _(sp):
            if stores:
                sp.dma_start(table_rows, table_from[:].rearrange("p h d -> p (h d)")).then_inc(table_in, 16)
            sp.sem_inc(free, SLOTS)

            def one(r):
                with sp.Fori(0, PASS_TURNS) as turn:
                    for k in range(SLOTS):
                        n = r * slots + turn * SLOTS + k
                        sp.wait_ge(scanned, n + 1)
                        sp.dma_start(flat[:, bass.ds((turn * SLOTS + k) * (COLS_SLOT * D), COLS_SLOT * D)],
                                     running[:, k].rearrange("p c f -> p (c f)")).then_inc(stored, 16)
                        sp.wait_ge(stored, n * 16 + 16)
                        sp.sem_inc(free, 1)
                if stores:
                    sp.wait_ge(y_done, r + 1)
                    sp.dma_start(table_rows, Y[:].rearrange("p h d -> p (h d)")).then_inc(table_in, 16)

            each_round(sp, one)
            if stores:
                sp.wait_ge(table_in, 16 * (rounds + 1))

        @block.gpsimd
        def _(pool):
            def one(r):
                if stores:
                    pool.wait_ge(table_in, r * 16 + 16)
                    pool.sem_inc(gate, 1)
                with pool.Fori(0, PASS_TURNS) as turn:
                    for k in range(SLOTS):
                        pool.wait_ge(staged_done[k], r * PASS_TURNS + turn + 1)
                        pool.sem_inc(gate, 1)
                        for j in range(COLS_SLOT):
                            pool.indirect_dma_start(picked[:, k, j, :], None, table,
                                                    bass.IndirectOffsetOnAxis(staged[:, k, j:j + 1], 0)
                                                    ).then_inc(gathered[k], 16)
                pool.wait_ge(stored, (r + 1) * (16 * slots))
                pool.sem_inc(gate, 1)
                gather_ends(pool, runs, sums, ends, ends_in)

            each_round(pool, one)

        @block.vector
        def _(dve):
            dve.memset(carry.rows[:], 0.0)
            for k in range(SLOTS):
                dve.tensor_copy(staged[:, k, :], runs.index[:, k * COLS_SLOT:(k + 1) * COLS_SLOT]
                                ).then_inc(staged_done[k], 1)

            def one(r):
                dve.memset(carry.last[:], 0.0).then_inc(kept, 1)
                with dve.Fori(0, PASS_TURNS) as turn:
                    for k in range(SLOTS):
                        n = r * slots + turn * SLOTS + k
                        at = (turn * SLOTS + k) * COLS_SLOT
                        dve.wait_ge(gathered[k], (r * PASS_TURNS + turn + 1) * (16 * COLS_SLOT))
                        dve.tensor_tensor(message[:], picked[:, k],
                                          runs.weight[:, bass.ds(at, COLS_SLOT)].unsqueeze(2)
                                          .to_broadcast([P, COLS_SLOT, D]), ALU.mult).then_inc(weighed, 1)
                        dve.wait_ge(weighed, n + 1)
                        dve.tensor_copy(staged[:, k, :], runs.index[:, bass.ds(at + PAD, COLS_SLOT)]
                                        ).then_inc(staged_done[k], 1)
                        dve.wait_ge(kept, n + r + 1)
                        dve.wait_ge(free, n + 1)
                        for f in range(D):
                            ins = dve.tensor_tensor_scan(running[:, k, :, f], runs.goes_on[:, bass.ds(at, COLS_SLOT)],
                                                         message[:, :, f], carry.last[:, f:f + 1], ALU.mult, ALU.add)
                        ins.then_inc(scanned, 1)
                        dve.wait_ge(scanned, n + 1)
                        dve.tensor_copy(carry.last[:], running[:, k, COLS_SLOT - 1, :]).then_inc(kept, 1)
                dve.wait_ge(kept, (r + 1) * (slots + 1))
                dve.sem_inc(carry.last_done, 1)
                carry.vector(dve, runs, r)
                dve.wait_ge(ends_in, (r + 1) * (16 * HI))
                if stores:
                    dve.wait_ge(table_in, r * 16 + 16)
                carry.add(dve, runs, r, ends[:], Y[:], masked, y_done)
                dve.wait_ge(y_done, r + 1)

            each_round(dve, one)

        @block.tensor
        def _(pe):
            each_round(pe, lambda r: carry.tensor(pe, c, runs, r))


def contracted_sums(nc, c, name, runs, table, rec, sums, Y, width, hats=False, silu_scale=None):
    with Scope(nc, name) as s:
        picked = s.sb("picked", [P, SLOTS, TILES, width, D])
        staged = s.sb("staged", [P, SLOTS, TILES], I32)
        recs = s.sb("recs", [P, SLOTS, TILES, REC_BY_SRC])
        product = s.sb("product", [P, TILES, width, D])
        message = s.sb("message", [P, SLOTS, TILES, D])
        active = s.sb("active", [P, SLOTS, TILES, D]) if silu_scale is not None else message
        running = s.sb("running", [P, TURN, D])
        ends = s.sb("ends", [P, HI, D])
        if hats:
            centers = s.sb("centers", [P, 5])
            far = s.sb("far", [P, TILES, 2, 4])
            hat = s.sb("hat", [P, SLOTS, TILES, 2, 4])
            coef = s.sb("coef", [P, TILES, 4, 4])
        carry = Carry(s, D)
        staged_done, gathered, recs_in = s.sems("staged_done", SLOTS), s.sems("gathered", SLOTS), s.sems("recs_in", SLOTS)
        times, summed, activated, scanned, kept, stored, free = (
            s.sem(n) for n in ("times", "summed", "activated", "scanned", "kept", "stored", "free"))
        ends_in, masked, y_done, gate, set_up, farther, hatted, coefs = (
            s.sem(n) for n in ("ends_in", "masked", "y_done", "gate", "set_up", "farther", "hatted", "coefs"))
        block = s.block()
        flat = sums.rearrange("(p c) f -> p (c f)", p=P)
        rec_flat = rec.rearrange("(p c) w -> p (c w)", p=P)

        @block.sync
        def _(sp):
            sp.sem_inc(free, 1)

            def body(turn, first):
                for k in range(SLOTS):
                    if not first:
                        sp.wait_ge(summed, (turn - 1) * SLOTS + k + 1)
                        if hats:
                            sp.wait_ge(hatted, (turn - 1) * SLOTS + k + 1)
                    at = turn * TURN + k * TILES
                    sp.dma_start(recs[:, k].rearrange("p c w -> p (c w)"),
                                 rec_flat[:, bass.ds(at * REC_BY_SRC, TILES * REC_BY_SRC)]).then_inc(recs_in[k], 16)

            loop(sp, TURNS, body)

        @block.gpsimd
        def _(pool):
            with pool.Fori(0, TURNS) as turn:
                for k in range(SLOTS):
                    pool.wait_ge(staged_done[k], turn + 1)
                    pool.sem_inc(gate, 1)
                    for j in range(TILES):
                        pool.indirect_dma_start(picked[:, k, j].rearrange("p w d -> p (w d)"), None, table,
                                                bass.IndirectOffsetOnAxis(staged[:, k, j:j + 1], 0)
                                                ).then_inc(gathered[k], 16)
            pool.wait_ge(stored, 16 * TURNS)
            pool.sem_inc(gate, 1)
            gather_ends(pool, runs, sums, ends, ends_in)

        @block.scalar
        def _(act):
            if hats:
                act.wait_ge(set_up, 1)

            def store(turn):
                act.wait_ge(scanned, turn + 1)
                act.dma_start(flat[:, bass.ds(turn * (TURN * D), TURN * D)],
                              running[:].rearrange("p c f -> p (c f)")).then_inc(stored, 16)
                act.wait_ge(stored, turn * 16 + 16)
                act.sem_inc(free, 1)

            def body(turn, first):
                for k in range(SLOTS):
                    n = turn * SLOTS + k
                    if hats:
                        act.wait_ge(recs_in[k], turn * 16 + 16)
                        if not first:
                            act.wait_ge(coefs, (turn - 1) * SLOTS + k + 1)
                        if not first or k:
                            act.wait_ge(hatted, n)
                        for v in range(4):
                            ins = act.activation(far[:, :, :, v], recs[:, k, :, 1:3], ACT.Abs,
                                                 bias=centers[:, v:v + 1], scale=1.5)
                        ins.then_inc(farther, 1)
                        act.wait_ge(farther, n + 1)
                        act.activation(hat[:, k], far[:], ACT.Relu, bias=centers[:, 4:5], scale=-1.0
                                       ).then_inc(hatted, 1)
                    if silu_scale is not None:
                        act.wait_ge(summed, n + 1)
                        act.activation(active[:, k], message[:, k], ACT.Silu, scale=silu_scale
                                       ).then_inc(activated, 1)
                if not first:
                    store(turn - 1)

            loop(act, TURNS, body)
            store(TURNS - 1)

        @block.vector
        def _(dve):
            if hats:
                for v, at in enumerate((1.5, 0.5, -0.5, -1.5, 1.0)):
                    ins = dve.memset(centers[:, v:v + 1], at)
                ins.then_inc(set_up, 1)
            dve.memset(carry.rows[:], 0.0)
            dve.memset(carry.last[:], 0.0).then_inc(kept, 1)
            for k in range(SLOTS):
                dve.tensor_copy(staged[:, k, :], runs.index[:, k * TILES:(k + 1) * TILES]).then_inc(staged_done[k], 1)

            def body(turn, first):
                for k in range(SLOTS):
                    n = turn * SLOTS + k
                    dve.wait_ge(recs_in[k], turn * 16 + 16)
                    if hats:
                        dve.wait_ge(hatted, n + 1)
                        dve.tensor_tensor(coef[:], hat[:, k, :, 0, :].unsqueeze(3).to_broadcast([P, TILES, 4, 4]),
                                          hat[:, k, :, 1, :].unsqueeze(2).to_broadcast([P, TILES, 4, 4]),
                                          ALU.mult).then_inc(coefs, 1)
                        dve.wait_ge(coefs, n + 1)
                        co = coef[:].rearrange("p t a b -> p t (a b)")
                    else:
                        co = recs[:, k, :, 3:3 + width]
                    dve.wait_ge(gathered[k], (turn + 1) * (16 * TILES))
                    if not first or k:
                        dve.wait_ge(summed, n)
                    dve.tensor_tensor(product[:], picked[:, k], co.unsqueeze(3).to_broadcast([P, TILES, width, D]),
                                      ALU.mult).then_inc(times, 1)
                    dve.wait_ge(times, n + 1)
                    dve.tensor_copy(staged[:, k, :], runs.index[:, bass.ds(turn * TURN + k * TILES + TURN, TILES)]
                                    ).then_inc(staged_done[k], 1)
                    if silu_scale is not None and not first:
                        dve.wait_ge(activated, (turn - 1) * SLOTS + k + 1)
                    dve.tensor_reduce(message[:, k], product[:].rearrange("p t w d -> p t d w"), AX.X, ALU.add
                                      ).then_inc(summed, 1)
                dve.wait_ge(summed if silu_scale is None else activated, (turn + 1) * SLOTS)
                dve.wait_ge(kept, turn + 1)
                dve.wait_ge(free, turn + 1)
                values = active[:].rearrange("p k t d -> p (k t) d")
                for f in range(D):
                    ins = dve.tensor_tensor_scan(running[:, :, f], runs.goes_on[:, bass.ds(turn * TURN, TURN)],
                                                 values[:, :, f], carry.last[:, f:f + 1], ALU.mult, ALU.add)
                ins.then_inc(scanned, 1)
                dve.wait_ge(scanned, turn + 1)
                dve.tensor_copy(carry.last[:], running[:, TURN - 1, :]).then_inc(kept, 1)

            loop(dve, TURNS, body)
            dve.wait_ge(kept, TURNS + 1)
            dve.sem_inc(carry.last_done, 1)
            carry.vector(dve, runs, 0)
            dve.wait_ge(ends_in, 16 * HI)
            carry.add(dve, runs, 0, ends[:], Y[:], masked, y_done)
            dve.wait_ge(y_done, 1)

        @block.tensor
        def _(pe):
            carry.tensor(pe, c, runs, 0)


def relation_norms(nc, c, runs, filled, sums):
    T = 8
    inverse_rows = nc.dram_tensor("inverse_rows", (ROWS, T), F32).ap()
    with Scope(nc, "norm") as s:
        hot = s.sb("hot", [P, COLS_SLOT, T])
        running = s.sb("running", [P, SLOTS, COLS_SLOT, T])
        ends = s.sb("ends", [P, HI, T])
        inverse = s.sb("inverse", [P, HI, T])
        to_f, to_i = s.sb("to_f", [P, 3, HI]), s.sb("to_i", [P, HI], I32)
        zeros = s.sb("zeros", [P, 1000])
        carry = Carry(s, T)
        hotted, scanned, kept, stored, free, ends_in, masked, counted, gate, line_sem, zeroed, cleared, inverted, out = (
            s.sem(n) for n in ("hotted", "scanned", "kept", "stored", "free", "ends_in", "masked", "counted", "gate",
                               "line", "zeroed", "cleared", "inverted", "out"))
        block = s.block()
        flat = sums.rearrange("(p c) f -> p (c f)", p=P)
        fill_flat = filled[0:N_EDGES, :].rearrange("(p c) f -> p (c f)", p=P)

        @block.sync
        def _(sp):
            sp.sem_inc(free, SLOTS)
            with sp.Fori(0, PASS_TURNS) as turn:
                for k in range(SLOTS):
                    n = turn * SLOTS + k
                    sp.wait_ge(scanned, n + 1)
                    sp.dma_start(flat[:, bass.ds(n * (COLS_SLOT * T), COLS_SLOT * T)],
                                 running[:, k].rearrange("p c f -> p (c f)")).then_inc(stored, 16)
                    sp.wait_ge(stored, n * 16 + 16)
                    sp.sem_inc(free, 1)

        @block.scalar
        def _(act):
            act.wait_ge(zeroed, 1)
            for i in range(COLS * T // 1000):
                act.dma_start(fill_flat[:, i * 1000:(i + 1) * 1000], zeros[:]).then_inc(cleared, 16)
            act.wait_ge(inverted, 1)
            act.dma_start(inverse_rows.rearrange("(p h) t -> p (h t)", p=P),
                          inverse[:].rearrange("p h t -> p (h t)")).then_inc(out, 16)
            act.wait_ge(out, 16)

        @block.gpsimd
        def _(pool):
            pool.wait_ge(stored, 16 * PASS_TURNS * SLOTS)
            pool.sem_inc(gate, 1)
            gather_ends(pool, runs, sums, ends, ends_in)
            pool.wait_ge(cleared, 16 * (COLS * T // 1000))
            pool.sem_inc(gate, 1)
            pool.wait_ge(inverted, 1)
            pool.sem_inc(gate, 1)
            for h in range(HI):
                pool.indirect_dma_start(filled, bass.IndirectOffsetOnAxis(to_i[:, h:h + 1], 0),
                                        inverse[:, h, :], None).then_inc(ends_in, 16)
            pool.wait_ge(ends_in, 16 * 2 * HI)

        @block.vector
        def _(dve):
            line = Line(dve, line_sem)
            dve.memset(zeros[:], 0.0).then_inc(zeroed, 1)
            line.do(dve.memset(carry.rows[:], 0.0))
            line.do(dve.tensor_scalar(to_f[:, 0, :], c.lane[:].to_broadcast([P, HI]), float(HI), float(N_EDGES),
                                      ALU.mult, ALU.add))
            line.do(dve.tensor_tensor(to_f[:, 1, :], to_f[:, 0, :], c.free[:, 0:HI], ALU.add))
            line.do(dve.tensor_tensor(to_f[:, 2, :], runs.info.start[:], to_f[:, 1, :], ALU.subtract))
            line.do(dve.tensor_tensor(to_f[:, 0, :], to_f[:, 2, :], runs.info.used[:], ALU.mult))
            line.do(dve.tensor_tensor(to_i[:], to_f[:, 0, :], to_f[:, 1, :], ALU.add))
            dve.memset(carry.last[:], 0.0).then_inc(kept, 1)
            with dve.Fori(0, PASS_TURNS) as turn:
                for k in range(SLOTS):
                    n = turn * SLOTS + k
                    cols = bass.ds(n * COLS_SLOT, COLS_SLOT)
                    dve.tensor_tensor(hot[:], runs.weight[:, cols].unsqueeze(2).to_broadcast([P, COLS_SLOT, T]),
                                      c.free[:, 0:T].unsqueeze(1).to_broadcast([P, COLS_SLOT, T]), ALU.is_equal
                                      ).then_inc(hotted, 1)
                    dve.wait_ge(hotted, n + 1)
                    dve.wait_ge(kept, n + 1)
                    dve.wait_ge(free, n + 1)
                    for f in range(T):
                        ins = dve.tensor_tensor_scan(running[:, k, :, f], runs.goes_on[:, cols], hot[:, :, f],
                                                     carry.last[:, f:f + 1], ALU.mult, ALU.add)
                    ins.then_inc(scanned, 1)
                    dve.wait_ge(scanned, n + 1)
                    dve.tensor_copy(carry.last[:], running[:, k, COLS_SLOT - 1, :]).then_inc(kept, 1)
            dve.wait_ge(kept, PASS_TURNS * SLOTS + 1)
            dve.sem_inc(carry.last_done, 1)
            carry.vector(dve, runs, 0)
            dve.wait_ge(ends_in, 16 * HI)
            carry.add(dve, runs, 0, ends[:], inverse[:], masked, counted)
            dve.wait_ge(counted, 1)
            line.do(dve.tensor_scalar(inverse[:], inverse[:], 1.0, None, ALU.max))
            dve.reciprocal(inverse[:], inverse[:]).then_inc(inverted, 1)

        @block.tensor
        def _(pe):
            carry.tensor(pe, c, runs, 0)

    with Scope(nc, "fill") as s:
        given = s.sb("given", [P, SLOTS, COLS_SLOT, T])
        along = s.sb("along", [P, COLS_SLOT, T])
        hot = s.sb("hot", [P, COLS_SLOT, T])
        own = s.sb("own", [P, COLS_SLOT, T])
        norm = s.sb("norm", [P, COLS_SLOT])
        last = s.sb("last", [P, T])
        written = s.sem("written")
        landed = s.sems("landed", SLOTS)
        first_in, scanned, kept, hotted, used = (s.sem(n) for n in ("first_in", "scanned", "kept", "hotted", "used"))
        block = s.block()
        fill_flat = filled[0:N_EDGES, :].rearrange("(p c) f -> p (c f)", p=P)

        @block.gpsimd
        def _(pool):
            pool.indirect_dma_start(last[:], None, inverse_rows,
                                    bass.IndirectOffsetOnAxis(runs.first_row[:, 0:1], 0)).then_inc(first_in, 16)

        @block.sync
        def _(sp):
            def body(turn, first):
                for k in range(SLOTS):
                    if not first:
                        sp.wait_ge(scanned, (turn - 1) * SLOTS + k + 1)
                    n = turn * SLOTS + k
                    sp.dma_start(given[:, k].rearrange("p c f -> p (c f)"),
                                 fill_flat[:, bass.ds(n * (COLS_SLOT * T), COLS_SLOT * T)]).then_inc(landed[k], 16)

            loop(sp, PASS_TURNS, body)

        @block.vector
        def _(dve):
            dve.wait_ge(first_in, 16)
            dve.sem_inc(kept, 1)
            with dve.Fori(0, PASS_TURNS) as turn:
                for k in range(SLOTS):
                    n = turn * SLOTS + k
                    cols = bass.ds(n * COLS_SLOT, COLS_SLOT)
                    dve.wait_ge(landed[k], turn * 16 + 16)
                    dve.tensor_tensor(hot[:], runs.weight[:, cols].unsqueeze(2).to_broadcast([P, COLS_SLOT, T]),
                                      c.free[:, 0:T].unsqueeze(1).to_broadcast([P, COLS_SLOT, T]), ALU.is_equal)
                    dve.wait_ge(kept, n + 1)
                    for f in range(T):
                        ins = dve.tensor_tensor_scan(along[:, :, f], runs.goes_on[:, cols], given[:, k, :, f],
                                                     last[:, f:f + 1], ALU.mult, ALU.add)
                    ins.then_inc(scanned, 1)
                    dve.wait_ge(scanned, n + 1)
                    dve.tensor_copy(last[:], along[:, COLS_SLOT - 1, :]).then_inc(kept, 1)
                    dve.tensor_tensor(own[:], along[:], hot[:], ALU.mult).then_inc(hotted, 1)
                    dve.wait_ge(hotted, n + 1)
                    dve.tensor_reduce(norm[:], own[:], AX.X, ALU.add).then_inc(used, 1)
                    dve.wait_ge(used, n + 1)
                    dve.tensor_scalar(runs.weight[:, cols], norm[:], 1.0, None, ALU.mult).then_inc(written, 1)
                    dve.wait_ge(written, n + 1)


def project(nc, c, name, src, weight, width, out=None, table=None):
    wide = BLOCK * width
    with Scope(nc, name) as s:
        diag = s.sb("diag", [BLOCK * D, BLOCK, width])
        turned = s.sb("turned", [BLOCK * D, 2, P])
        rows = s.sb("rows", [P, 2, wide]) if out is None else None
        pt = s.ps("turned_ps", [P, 2, PIECE])
        pp = s.ps("product", [P, 4, PIECE])
        zeroed, weights_in, flipped, copied, made, moved = (
            s.sem(n) for n in ("zeroed", "weights_in", "flipped", "copied", "made", "moved"))
        stored = s.sems("stored", 2)
        block = s.block()
        pieces = [(b, at, min(at + PIECE, wide)) for b in range(BLOCKS) for at in range(0, wide, PIECE)]
        per = len(pieces) // BLOCKS

        @block.sync
        def _(sp):
            sp.wait_ge(zeroed, 1)
            for j in range(BLOCK):
                to = diag[j * D:(j + 1) * D, j, :]
                if len(weight.shape) == 3:
                    to = to.rearrange("p (a d) -> p a d", d=D)
                sp.dma_start(to, weight).then_inc(weights_in, 16)
            if out is None:
                view = table.rearrange("(p h) w -> p (h w)", p=P)
                for b in range(BLOCKS):
                    sp.wait_ge(moved, (b + 1) * per)
                    sp.dma_start(view[:, b * wide:(b + 1) * wide], rows[:, b % 2, :]).then_inc(stored[b % 2], 16)
                for half in stored:
                    sp.wait_ge(half, 16 * (BLOCKS // 2))

        @block.vector
        def _(dve):
            dve.memset(diag[:], 0.0).then_inc(zeroed, 1)
            for b in range(BLOCKS):
                dve.wait_ge(flipped, b + 1)
                if b >= 2:
                    dve.wait_ge(made, (b - 1) * per)
                dve.tensor_copy(turned[:, b % 2, :], pt[0:BLOCK * D, b % 2, 0:P]).then_inc(copied, 1)

        @block.tensor
        def _(pe):
            def turn(b):
                if b >= 2:
                    pe.wait_ge(copied, b - 1)
                pe.transpose(pt[0:BLOCK * D, b % 2, 0:P],
                             src[:, b * BLOCK:(b + 1) * BLOCK, :].rearrange("p h d -> p (h d)"),
                             c.ident[:]).then_inc(flipped, 1)

            turn(0)
            pe.wait_ge(weights_in, 16 * BLOCK)
            flat = diag[:].rearrange("p h w -> p (h w)")
            for n, (b, at, to) in enumerate(pieces):
                if at == 0:
                    if b + 1 < BLOCKS:
                        turn(b + 1)
                    pe.wait_ge(copied, b + 1)
                if n >= 4:
                    pe.wait_ge(moved, n - 3)
                pe.matmul(pp[:, n % 4, 0:to - at], turned[:, b % 2, :], flat[:, at:to],
                          start=True, stop=True).then_inc(made, 1)

        @block.scalar
        def _(act):
            for n, (b, at, to) in enumerate(pieces):
                act.wait_ge(made, n + 1)
                if out is None:
                    if b >= 2 and at == 0:
                        act.wait_ge(stored[b % 2], 16 * (b // 2))
                    dest = rows[:, b % 2, at:to]
                else:
                    dest = out[:, b * BLOCK:(b + 1) * BLOCK, :].rearrange("p h w -> p (h w)")[:, at:to]
                act.copy(dest, pp[:, n % 4, 0:to - at]).then_inc(moved, 1)


def by_node(a):
    return a.unsqueeze(2).to_broadcast([P, HI, D])


def layernorm(nc, name, X, H):
    with Scope(nc, name) as s:
        mean, var, dev, inv = (s.sb(n, [P, HI]) for n in ("mean", "var", "dev", "inv"))
        square = s.sb("square", [P, HI, D])
        line_sem, spread, rooted = s.sem("line"), s.sem("spread"), s.sem("rooted")
        block = s.block()

        @block.vector
        def _(dve):
            line = Line(dve, line_sem)
            line.do(dve.tensor_reduce(mean[:], X[:], AX.X, ALU.add))
            line.do(dve.tensor_scalar(mean[:], mean[:], 1.0 / D, None, ALU.mult))
            line.do(dve.tensor_tensor(H[:], X[:], by_node(mean[:]), ALU.subtract))
            line.do(dve.tensor_tensor(square[:], H[:], H[:], ALU.mult))
            line.do(dve.tensor_reduce(var[:], square[:], AX.X, ALU.add))
            dve.tensor_scalar(var[:], var[:], 1.0 / D, 1e-5, ALU.mult, ALU.add).then_inc(spread, 1)
            dve.wait_ge(rooted, 1)
            line.do(dve.reciprocal(inv[:], dev[:]))
            line.do(dve.tensor_tensor(H[:], H[:], by_node(inv[:]), ALU.mult))
            line.do(dve.tensor_scalar(H[:], H[:], 0.0, None, ALU.max))

        @block.scalar
        def _(act):
            act.wait_ge(spread, 1)
            act.activation(dev[:], var[:], ACT.Sqrt).then_inc(rooted, 1)


def add_nodes(nc, name, out, terms, bias=None, relu=False):
    with Scope(nc, name) as s:
        wide = s.sb("wide", [P, D])
        bias_in, line_sem = s.sem("bias_in"), s.sem("line")
        block = s.block()

        @block.sync
        def _(sp):
            if bias is not None:
                sp.dma_start(wide[:], bias.unsqueeze(0).to_broadcast([P, D])).then_inc(bias_in, 16)
                sp.wait_ge(bias_in, 16)

        @block.vector
        def _(dve):
            line = Line(dve, line_sem)
            line.do(dve.tensor_tensor(out[:], terms[0][:], terms[1][:], ALU.add))
            for term in terms[2:]:
                line.do(dve.tensor_tensor(out[:], out[:], term[:], ALU.add))
            if bias is not None:
                dve.wait_ge(bias_in, 16)
                line.do(dve.tensor_tensor(out[:], out[:], wide[:].unsqueeze(1).to_broadcast([P, HI, D]), ALU.add))
            if relu:
                line.do(dve.tensor_scalar(out[:], out[:], 0.0, None, ALU.max))


def add_log_softmax(nc, name, X, Z):
    with Scope(nc, name) as s:
        top, total, log = (s.sb(n, [P, HI]) for n in ("top", "total", "log"))
        powers = s.sb("powers", [P, HI, D])
        line_sem, lowered, raised, totals, logs = (s.sem(n) for n in ("line", "lowered", "raised", "totals", "logs"))
        block = s.block()

        @block.vector
        def _(dve):
            line = Line(dve, line_sem)
            line.do(dve.tensor_reduce(top[:], Z[:], AX.X, ALU.max))
            dve.tensor_tensor(Z[:], Z[:], by_node(top[:]), ALU.subtract).then_inc(lowered, 1)
            dve.wait_ge(raised, 1)
            dve.tensor_reduce(total[:], powers[:], AX.X, ALU.add).then_inc(totals, 1)
            dve.wait_ge(logs, 1)
            line.do(dve.tensor_tensor(Z[:], Z[:], by_node(log[:]), ALU.subtract))
            line.do(dve.tensor_tensor(X[:], X[:], Z[:], ALU.add))

        @block.scalar
        def _(act):
            act.wait_ge(lowered, 1)
            act.activation(powers[:], Z[:], ACT.Exp).then_inc(raised, 1)
            act.wait_ge(totals, 1)
            act.activation(log[:], total[:], ACT.Ln).then_inc(logs, 1)


def update(nc, name, V, agg, U, scale):
    with Scope(nc, name) as s:
        line_sem, summed = s.sem("line"), s.sem("summed")
        block = s.block()

        @block.vector
        def _(dve):
            line = Line(dve, line_sem)
            v = V[:].rearrange("p n (h k) -> p (n h) k", k=D)
            a = agg[:].rearrange("p n h -> p (n h)").unsqueeze(2).to_broadcast([P, HI * D, D])
            line.do(dve.tensor_tensor(v, v, a, ALU.mult))
            dve.tensor_reduce(U[:], V[:].rearrange("p n (h k) -> p n k h", k=D), AX.X, ALU.add).then_inc(summed, 1)

        @block.scalar
        def _(act):
            act.wait_ge(summed, 1)
            act.activation(U[:], U[:], ACT.Silu, scale=scale).then_inc(line_sem, 1)


def finish(nc, X, H, U, scale, out):
    with Scope(nc, "finish") as s:
        line_sem, ready, stored = s.sem("line"), s.sem("ready"), s.sem("stored")
        block = s.block()

        @block.vector
        def _(dve):
            line = Line(dve, line_sem)
            line.do(dve.tensor_tensor(X[:], X[:], H[:], ALU.add))
            dve.scalar_tensor_tensor(out=X[:], in0=U[:], scalar=scale, in1=X[:], op0=ALU.mult, op1=ALU.add
                                     ).then_inc(ready, 1)

        @block.sync
        def _(sp):
            sp.wait_ge(ready, 1)
            sp.dma_start(out[0:FULL * P, :].rearrange("(h p) d -> p h d", p=P), X[:, 0:FULL, :]).then_inc(stored, 16)
            sp.dma_start(out[FULL * P:N_NODES, :], X[0:REST, FULL, :]).then_inc(stored, 16)
            sp.wait_ge(stored, 32)


def gnn_kernel(nc, x, src, dst, edge_attr_2, edge_attr_8, edge_type_8, edge_weight, L1_gnn_weight, L2_gnn_W1,
               L2_gnn_root1, L2_gnn_b1, L2_gnn_W2, L2_gnn_root2, L2_gnn_b2, L3_gnn_W_msg_tp, L3_gnn_W_msg_lin,
               L3_gnn_W_upd_tp, L3_gnn_W_upd_lin, out):
    def dram(name, shape):
        return nc.dram_tensor(name, shape, F32).ap()

    with ExitStack() as ctx:
        def sb(name, shape, dt=F32):
            return ctx.enter_context(nc.sbuf_tensor(name, shape, dt))

        c = Constants(sb)
        X, H, Y, R = (sb(n, [P, HI, D]) for n in "XHYR")
        info_src, info_dst = Info(sb, "by_src"), Info(sb, "by_dst")
        rec_src, rec_dst = dram("rec_src", (N_EDGES, REC_BY_SRC)), dram("rec_dst", (N_EDGES, REC_BY_DST))
        sums = dram("sums", (N_EDGES, D))
        constants(nc, c, x, X)

        with Scope(nc, "keys") as s:
            src_lo, src_hi, dst_lo, dst_hi = (s.sb(n, [P, COLS], BF16) for n in ("src_lo", "src_hi", "dst_lo", "dst_hi"))
            src_row, dst_row = s.sb("src_row", [P, COLS]), s.sb("dst_row", [P, COLS])
            weight, kind = s.sb("weight", [P, COLS]), s.sb("kind", [P, COLS], I32)
            src_lows = digits(nc, c, src, "src", src_lo, src_hi, src_row)
            dst_lows = digits(nc, c, dst, "dst", dst_lo, dst_hi, dst_row)
            with Scope(nc, "load") as ld:
                loaded = ld.sem("loaded")
                block = ld.block()

                @block.sync
                def _(sp):
                    sp.dma_start(weight[:], edge_weight.rearrange("(p c) -> p c", p=P)).then_inc(loaded, 16)
                    sp.dma_start(kind[:], edge_type_8.rearrange("(p c) -> p c", p=P)).then_inc(loaded, 16)
                    sp.wait_ge(loaded, 32)

            count(nc, c, "src", src_lo, src_hi, info_src)
            sort_edges(nc, c, "src", src_lo, src_hi, src_lows, info_src, REC_BY_SRC,
                       [(0, weight), (11, dst_row), (12, src_row), (13, src_lo), (14, src_hi)],
                       [(1, 2, edge_attr_2), (3, 8, edge_attr_8)], rec_src)
            count(nc, c, "dst", dst_lo, dst_hi, info_dst)
            sort_edges(nc, c, "dst", dst_lo, dst_hi, dst_lows, info_dst, REC_BY_DST,
                       [(0, kind), (1, src_row), (2, dst_row), (3, dst_lo), (4, dst_hi)], [], rec_dst)

        runs_src = Runs(sb, "src", info_src)
        load_runs(nc, c, "src", rec_src, REC_BY_SRC, runs_src, True)

        layernorm(nc, "ln0", X, H)
        weighted_sums(nc, c, "power", runs_src, dram("y_rows", (ROWS, D)), sums, Y, 4, table_from=H)
        add_nodes(nc, "add0", X, [X, Y])

        layernorm(nc, "ln1", X, H)
        basis_rows = dram("L1_rows", (ROWS, 16 * D))
        project(nc, c, "basis", H, L1_gnn_weight.rearrange("u v i o -> i (u v) o"), 16 * D, table=basis_rows)
        contracted_sums(nc, c, "conv", runs_src, basis_rows, rec_src, sums, Y, 16, hats=True)
        add_nodes(nc, "add1", X, [X, Y])

        layernorm(nc, "ln2", X, H)
        with Scope(nc, "l2") as s:
            runs_dst = Runs(s.sb, "dst", info_dst)
            load_runs(nc, c, "dst", rec_dst, REC_BY_DST, runs_dst, False)
            relation_norms(nc, c, runs_dst, dram("filled", (N_EDGES + ROWS, 8)), dram("type_sums", (N_EDGES, 8)))
            typed_rows = dram("L2_rows", (ROWS, 8 * D))
            by_type = typed_rows.rearrange("n (r d) -> (n r) d", r=8)
            for n, (W, root, b) in enumerate(((L2_gnn_W1, L2_gnn_root1, L2_gnn_b1), (L2_gnn_W2, L2_gnn_root2, L2_gnn_b2))):
                project(nc, c, f"typed{n}", H, W.rearrange("r i o -> i r o"), 8 * D, table=typed_rows)
                project(nc, c, f"root{n}", H, root, D, out=R)
                weighted_sums(nc, c, f"relate{n}", runs_dst, by_type, sums, Y, 1)
                add_nodes(nc, f"add2{n}", H, [Y, R], bias=b, relu=n == 0)
        add_log_softmax(nc, "softmax", X, H)

        layernorm(nc, "ln3", X, H)
        message_rows = dram("L3_rows", (ROWS, 8 * D))
        project(nc, c, "bilinear", H, L3_gnn_W_msg_tp, 8 * D, table=message_rows)
        contracted_sums(nc, c, "message", runs_src, message_rows, rec_src, sums, Y, 8, silu_scale=(8 * D) ** -0.5)
        project(nc, c, "mix", Y, L3_gnn_W_msg_lin, D, out=R)
        with Scope(nc, "l3") as s:
            V = s.sb("V", [P, HI, D * D])
            project(nc, c, "upd", H, L3_gnn_W_upd_tp, D * D, out=V)
            update(nc, "update", V, R, Y, D ** -0.5 / D)
        project(nc, c, "last", Y, L3_gnn_W_upd_lin, D, out=R)
        finish(nc, X, H, R, D ** -0.5, out)

_INS = ['x', 'src', 'dst', 'edge_attr_2', 'edge_attr_8', 'edge_type_8', 'edge_weight', 'node_vec1',
        'L1_gnn_weight', 'L2_gnn_W1', 'L2_gnn_root1', 'L2_gnn_b1', 'L2_gnn_W2', 'L2_gnn_root2', 'L2_gnn_b2',
        'L3_gnn_W_msg_tp', 'L3_gnn_W_msg_lin', 'L3_gnn_W_upd_tp', 'L3_gnn_W_upd_lin']


def kernel(**inputs):
    import numpy as _np
    import concourse.bacc as _bacc
    from concourse import mybir as _mybir
    from concourse.bass_utils import run_bass_kernel_spmd as _run

    nc = _bacc.Bacc("TRN2", target_bir_lowering=False, num_devices=1)
    arrays, args = {}, {}
    for name in _INS:
        if name == 'node_vec1':
            continue
        a = _np.ascontiguousarray(inputs[name])
        arrays[f"in_{name}"] = a
        args[name] = nc.dram_tensor(f"in_{name}", a.shape, _mybir.dt.from_np(a.dtype), kind="ExternalInput").ap()
    out = nc.dram_tensor("out_x", (N_NODES, D), F32, kind="ExternalOutput").ap()
    gnn_kernel(nc, out=out, **args)
    r = _run(nc, [arrays], core_ids=[0])
    return r.results[0]["out_x"]
```

```python
from contextlib import ExitStack

import concourse.bass as bass
from concourse import mybir

F32 = mybir.dt.float32
BF16 = mybir.dt.bfloat16
I32 = mybir.dt.int32
ALU = mybir.AluOpType
ACT = mybir.ActivationFunctionType
AX = mybir.AxisListType

P = 128
N_NODES = 12500
N_EDGES = 400000
D = 16
COLS = N_EDGES // P
HI = -(-N_NODES // P)
ROWS = P * HI
FULL = N_NODES // P
REST = N_NODES - FULL * P
TILES = 5
SLOTS = 5
TURN = TILES * SLOTS
TURNS = COLS // TURN
assert COLS == TURNS * TURN and P * COLS == N_EDGES and HI * TILES <= 512

WEIGHT, ATTR2, ATTR8, SOURCE, DST_ROW, DST_LO, DST_HI, KIND, WORDS = 0, 1, 3, 11, 12, 13, 14, 15, 16
WINDOW = 256
GROUPS = -(-N_NODES // (8 * WINDOW))
G_TURNS = TURNS + GROUPS
G_COLS = G_TURNS * TURN
PLACES = P * TURN
B_ALL = ROWS // 8
B_BLOCKS = -(-B_ALL // P)


def loop(eng, turns, body):
    body(0, True)
    with eng.Fori(1, turns) as turn:
        body(turn, False)


class Line:

    def __init__(self, eng, sem):
        self.eng, self.sem, self.count = eng, sem, 0

    def do(self, ins):
        self.count += 1
        ins.then_inc(self.sem, 1)
        self.eng.wait_ge(self.sem, self.count)


class Scope:

    def __init__(self, nc, name):
        self.nc, self.name, self.stack, self.taken = nc, name, ExitStack(), []

    def __enter__(self):
        self.stack.__enter__()
        return self

    def __exit__(self, *e):
        self.stack.__exit__(*e)
        if self.taken:
            self.nc.clear_and_free_semaphores(self.taken)
            self.nc.all_engine_barrier()

    def sb(self, name, shape, dt=F32):
        return self.stack.enter_context(self.nc.sbuf_tensor(f"{self.name}_{name}", shape, dt))

    def ps(self, name, shape, dt=F32):
        return self.stack.enter_context(self.nc.psum_tensor(f"{self.name}_{name}", shape, dt))

    def sem(self, name):
        self.taken.append(self.nc.alloc_semaphore(f"{self.name}_{name}"))
        return self.taken[-1]

    def sems(self, name, n):
        return [self.sem(f"{name}{i}") for i in range(n)]

    def block(self):
        return self.stack.enter_context(self.nc.Block())


def constants(nc, c, x, X):
    with Scope(nc, "const") as s:
        iota_i = s.sb("iota_i", [P, WINDOW], I32)
        lane_i = s.sb("lane_i", [P, 1], I32)
        made, iotas, zeroed, x_in = s.sem("made"), s.sem("iotas"), s.sem("zeroed"), s.sem("x_in")
        block = s.block()

        @block.gpsimd
        def _(pool):
            pool.iota(iota_i[:], pattern=[[1, WINDOW]], base=0, channel_multiplier=0).then_inc(iotas, 1)
            pool.iota(lane_i[:], pattern=[[0, 1]], base=0, channel_multiplier=1).then_inc(iotas, 1)

        @block.vector
        def _(dve):
            line = Line(dve, made)
            dve.memset(X[:], 0.0).then_inc(zeroed, 1)
            dve.wait_ge(iotas, 2)
            line.do(dve.tensor_copy(c.free[:], iota_i[:, 0:P]))
            line.do(dve.tensor_copy(c.free_b[:], iota_i[:, 0:P]))
            line.do(dve.tensor_copy(c.wide[:], iota_i[:]))
            line.do(dve.tensor_copy(c.lane[:], lane_i[:]))
            line.do(dve.tensor_scalar(c.ident[:], c.free[:], c.lane[:, 0:1], None, ALU.is_equal))
            line.do(dve.tensor_copy(c.ident_b[:], c.ident[:]))
            line.do(dve.memset(c.ones[:], 1.0))
            line.do(dve.tensor_scalar(c.above[:], c.free[:], c.lane[:, 0:1], None, ALU.is_gt))
            line.do(dve.tensor_copy(c.above_b[:], c.above[:]))
            line.do(dve.tensor_scalar(c.down[:], c.free[:], -1.0, c.lane[:, 0:1], ALU.add, ALU.is_equal))
            line.do(dve.tensor_scalar(c.up[:], c.free[:], 1.0, c.lane[:, 0:1], ALU.add, ALU.is_equal))

        @block.sync
        def _(sp):
            sp.wait_ge(zeroed, 1)
            sp.dma_start(X[:, 0:FULL, :], x[0:FULL * P, :].rearrange("(h p) d -> p h d", p=P)).then_inc(x_in, 16)
            sp.dma_start(X[0:REST, FULL, :], x[FULL * P:N_NODES, :]).then_inc(x_in, 16)
            sp.wait_ge(x_in, 32)


def digits(nc, c, src, dst, weight, kind, k):
    with Scope(nc, "digits") as s:
        raw_s, raw_d = s.sb("raw_s", [P, COLS], I32), s.sb("raw_d", [P, COLS], I32)
        lo_i, hi_i = s.sb("lo_i", [P, COLS], I32), s.sb("hi_i", [P, COLS], I32)
        step = s.sb("step", [P, COLS])
        edge = s.sb("edge", [P, 4])
        least = s.sb("least", [1, 2])
        pe_out = s.ps("pe_out", [P, PIECE])
        loaded, line_sem, asked, shifted = (s.sem(n) for n in ("loaded", "line", "asked", "shifted"))
        block = s.block()

        def flat(dram):
            return dram.rearrange("(p c) -> p c", p=P)

        @block.sync
        def _(sp):
            sp.dma_start(raw_s[:], flat(src)).then_inc(loaded, 16)
            sp.dma_start(raw_d[:], flat(dst)).then_inc(loaded, 16)
            sp.dma_start(k.weight[:], flat(weight)).then_inc(loaded, 16)
            sp.dma_start(k.kind[:], flat(kind)).then_inc(loaded, 16)

        @block.vector
        def _(dve):
            line = Line(dve, line_sem)
            dve.wait_ge(loaded, 64)
            line.do(dve.tensor_scalar(k.source[:], raw_s[:], 1.0, None, ALU.add))
            line.do(dve.tensor_scalar(lo_i[:], raw_d[:], 127, None, ALU.bitwise_and))
            line.do(dve.tensor_scalar(hi_i[:], raw_d[:], 7, None, ALU.arith_shift_right))
            line.do(dve.tensor_copy(k.lo[:], lo_i[:]))
            line.do(dve.tensor_copy(k.hi[:], hi_i[:]))
            line.do(dve.scalar_tensor_tensor(out=k.row[:], in0=k.lo[:], scalar=float(HI), in1=k.hi[:],
                                             op0=ALU.mult, op1=ALU.add))
            line.do(dve.tensor_tensor(step[:, 0:COLS - 1], raw_d[:, 1:COLS], raw_d[:, 0:COLS - 1], ALU.subtract))
            dve.tensor_copy(edge[:, 0:1], raw_d[:, COLS - 1:COLS]).then_inc(asked, 1)
            dve.wait_ge(shifted, 1)
            line.do(dve.tensor_tensor(step[:, COLS - 1:COLS], raw_d[:, 0:1], pe_out[:, 0:1], ALU.subtract))
            line.do(dve.tensor_reduce(edge[:, 1:2], step[:], AX.X, ALU.min))
            dve.tensor_scalar(edge[:, 2:3], edge[:, 1:2], 0.0, None, ALU.is_ge).then_inc(asked, 1)
            dve.wait_ge(shifted, 2)
            line.do(dve.tensor_reduce(least[:, 0:1], pe_out[0:1, P:2 * P], AX.X, ALU.min))
            line.do(dve.tensor_copy(k.ordered[:], least[:, 0:1]))

        @block.tensor
        def _(pe):
            pe.wait_ge(asked, 1)
            pe.matmul(pe_out[:, 0:1], c.down[:], edge[:, 0:1], start=True, stop=True).then_inc(shifted, 1)
            pe.wait_ge(asked, 2)
            pe.transpose(pe_out[0:1, P:2 * P], edge[:, 2:3], c.ident[:]).then_inc(shifted, 1)

def one_hots(dve, c, lo_b, hi_b, cols, lo_hot, hi_hot, done):
    dve.tensor_tensor(lo_hot, lo_b[:, cols].unsqueeze(2).to_broadcast([P, TILES, P]),
                      c.free_b[:, 0:P].unsqueeze(1).to_broadcast([P, TILES, P]), ALU.is_equal)
    dve.tensor_tensor(hi_hot, hi_b[:, cols].unsqueeze(2).to_broadcast([P, TILES, HI]),
                      c.free_b[:, 0:HI].unsqueeze(1).to_broadcast([P, TILES, HI]), ALU.is_equal).then_inc(done, 1)


def count(nc, c, name, lo_b, hi_b, info):
    with Scope(nc, f"count_{name}") as s:
        lo_hot = s.sb("lo_hot", [P, SLOTS, TILES, P], BF16)
        hi_hot = s.sb("hi_hot", [P, SLOTS, TILES, HI], BF16)
        zeros = s.sb("zeros", [P, P], BF16)
        ones_row = s.sb("ones_row", [P, HI])
        run = s.sb("run", [P, HI])
        pc = s.ps("counts", [P, 512])
        po = s.ps("offsets", [P, 512])
        hot, counted, line_sem = s.sem("hot"), s.sem("counted"), s.sem("line")
        zeroed, totals, offs = s.sem("zeroed"), s.sem("totals"), s.sem("offs")
        block = s.block()

        @block.vector
        def _(dve):
            dve.memset(zeros[:], 0.0).then_inc(zeroed, 1)

            def body(turn, first):
                for k in range(SLOTS):
                    if not first:
                        dve.wait_ge(counted, (turn - 1) * SLOTS + k + 1)
                    one_hots(dve, c, lo_b, hi_b, bass.ds(turn * TURN + k * TILES, TILES),
                             lo_hot[:, k], hi_hot[:, k], hot)

            loop(dve, TURNS, body)
            line = Line(dve, line_sem)
            dve.wait_ge(counted, TURNS * SLOTS)
            dve.tensor_copy(info.cnt[:], pc[:, 0:HI]).then_inc(totals, 1)
            line.do(dve.memset(ones_row[:], 1.0))
            dve.wait_ge(offs, 1)
            line.do(dve.tensor_copy(run[:], po[:, P:P + HI]))
            line.do(dve.tensor_tensor_scan(info.start[:], ones_row[:], run[:], 0.0, ALU.mult, ALU.add))
            line.do(dve.tensor_tensor(info.start[:], info.start[:], run[:], ALU.subtract))
            line.do(dve.tensor_tensor(info.start[:], info.start[:], po[:, 0:HI], ALU.add))
            line.do(dve.tensor_tensor(run[:], info.start[:], info.cnt[:], ALU.add))
            line.do(dve.tensor_scalar(run[:], run[:], -1.0, 0.0, ALU.add, ALU.max))
            line.do(dve.tensor_copy(info.end_i[:], run[:]))
            line.do(dve.tensor_scalar(info.used[:], info.cnt[:], 1.0, None, ALU.min))

        @block.tensor
        def _(pe):
            pe.wait_ge(zeroed, 1)
            pe.matmul(pc[:, 0:HI], zeros[:], zeros[:, 0:HI], start=True, stop=True)

            def body(turn, first):
                for k in range(SLOTS):
                    pe.wait_ge(hot, turn * SLOTS + k + 1)
                    for j in range(TILES):
                        mm = pe.matmul(pc[:, 0:HI], lo_hot[:, k, j, :], hi_hot[:, k, j, :],
                                       start=False, stop=True, skip_group_check=True)
                    mm.then_inc(counted, 1)

            loop(pe, TURNS, body)
            pe.wait_ge(totals, 1)
            pe.matmul(po[:, 0:HI], c.above[:], info.cnt[:], start=True, stop=True)
            pe.matmul(po[:, P:P + HI], c.ones[:], info.cnt[:], start=True, stop=True).then_inc(offs, 1)


def low_tiles(nc, c, lo_b, low_rows):
    with Scope(nc, "lows") as s:
        turned = s.sb("turned", [125, 25, P], BF16)
        flipped = s.ps("flipped", [P, 2, 1024], BF16)
        flips, copied, stored = s.sem("flips"), s.sem("copied"), s.sem("stored")
        block = s.block()

        @block.sync
        def _(sp):
            sp.wait_ge(copied, 25)
            sp.dma_start(low_rows.rearrange("(j k) e -> j (k e)", k=25),
                         turned[:].rearrange("j k e -> j (k e)")).then_inc(stored, 16)
            sp.wait_ge(stored, 16)

        @block.tensor
        def _(pe):
            for k in range(25):
                if k >= 2:
                    pe.wait_ge(copied, k - 1)
                pe.transpose(flipped[0:125, k % 2, 0:P], lo_b[:, k::25], c.ident_b[:]).then_inc(flips, 1)

        @block.scalar
        def _(act):
            for k in range(25):
                act.wait_ge(flips, k + 1)
                act.copy(turned[:, k, :], flipped[0:125, k % 2, 0:P]).then_inc(copied, 1)


def copy_edges(nc, k, attr2, attr8, rec):
    with Scope(nc, "copy") as s:
        two, eight = s.sb("two", [P, SLOTS, TURN, 2]), s.sb("eight", [P, SLOTS, TURN, 8])
        record = s.sb("record", [P, SLOTS, TURN, WORDS])
        turns = COLS // (SLOTS * TURN)
        landed, stored = s.sems("landed", SLOTS), s.sems("stored", SLOTS)
        built_a, built_v = s.sem("built_a"), s.sem("built_v")
        block = s.block()
        out = rec.rearrange("(p c) w -> p (c w)", p=P)

        @block.sync
        def _(sp):
            def body(turn, first):
                for i in range(SLOTS):
                    n = turn * SLOTS + i
                    if not first:
                        sp.wait_ge(built_v, n - SLOTS + 1)
                    sp.dma_start(two[:, i].rearrange("p c w -> p (c w)"), attr2.rearrange("(p c) w -> p (c w)", p=P)
                                 [:, bass.ds(n * (TURN * 2), TURN * 2)]).then_inc(landed[i], 16)
                    sp.dma_start(eight[:, i].rearrange("p c w -> p (c w)"), attr8.rearrange("(p c) w -> p (c w)", p=P)
                                 [:, bass.ds(n * (TURN * 8), TURN * 8)]).then_inc(landed[i], 16)

            loop(sp, turns, body)

        @block.vector
        def _(dve):
            def body(turn, first):
                for i in range(SLOTS):
                    cols = bass.ds((turn * SLOTS + i) * TURN, TURN)
                    if not first:
                        dve.wait_ge(stored[i], turn * 16)
                    dve.wait_ge(landed[i], turn * 32 + 32)
                    dve.tensor_copy(record[:, i, :, ATTR2:ATTR2 + 2], two[:, i])
                    dve.tensor_copy(record[:, i, :, ATTR8:ATTR8 + 8], eight[:, i])
                    dve.tensor_copy(record[:, i, :, WEIGHT], k.weight[:, cols])
                    dve.tensor_copy(record[:, i, :, DST_ROW], k.row[:, cols]).then_inc(built_v, 1)

            loop(dve, turns, body)

        @block.scalar
        def _(act):
            def body(turn, first):
                for i in range(SLOTS):
                    n = turn * SLOTS + i
                    if not first:
                        act.wait_ge(stored[i], turn * 16)
                    for word, col in ((SOURCE, k.source), (DST_LO, k.lo), (DST_HI, k.hi), (KIND, k.kind)):
                        ins = act.copy(record[:, i, :, word], col[:, bass.ds(n * TURN, TURN)])
                    ins.then_inc(built_a, 1)
                    act.wait_ge(built_v, n + 1)
                    act.wait_ge(built_a, n + 1)
                    act.dma_start(out[:, bass.ds(n * (TURN * WORDS), TURN * WORDS)],
                                  record[:, i].rearrange("p c w -> p (c w)")).then_inc(stored[i], 16)

            loop(act, turns, body)

        def until_stored(eng):
            for i in range(SLOTS):
                eng.wait_ge(stored[i], 16 * turns)

        @block.gpsimd
        def _(pool):
            until_stored(pool)

        @block.tensor
        def _(pe):
            until_stored(pe)


def sort_edges(nc, c, name, lo_b, hi_b, low_rows, info, words, columns, parts, rec):
    with Scope(nc, f"sort_{name}") as s:
        lo_hot = s.sb("lo_hot", [P, SLOTS, TILES, P], BF16)
        hi_hot = s.sb("hi_hot", [P, SLOTS, TILES, HI], BF16)
        lo_row = s.sb("lo_row", [P, SLOTS, TILES * P], BF16)
        lo_hot_t = s.sb("lo_hot_t", [P, SLOTS, TILES, P])
        before = s.sb("before", [P, SLOTS, TILES, P], BF16)
        place = s.sb("place", [P, TILES, P])
        picked = s.sb("picked", [P, TILES, HI])
        pos_f = s.sb("pos_f", [P, TILES])
        pos_i = s.sb("pos_i", [P, SLOTS, TILES], I32)
        record = s.sb("record", [P, SLOTS, TILES, words])
        staged = [s.sb(f"staged{w}", [P, SLOTS, TILES * n]) for w, n, _ in parts]
        pcount = s.ps("pcount", [P, 512])
        pread = s.ps("pread", [P, SLOTS, 512])
        hot, rows_in, parts_in = s.sem("hot"), s.sems("rows_in", SLOTS), s.sems("parts_in", SLOTS)
        hot_t, counter, added = s.sem("hot_t"), s.sem("counter"), s.sem("added")
        read, pick, pos, posd = s.sem("read"), s.sem("pick"), s.sem("pos"), s.sem("posd")
        built, scattered, zeroed, gate = s.sem("built"), s.sems("scattered", SLOTS), s.sem("zeroed"), s.sem("gate")
        block = s.block()

        @block.sync
        def _(sp):
            def body(turn, first):
                for k in range(SLOTS):
                    if not first:
                        sp.wait_ge(hot_t, (turn - 1) * SLOTS + k + 1)
                        sp.wait_ge(built, (turn - 1) * SLOTS + k + 1)
                    src = low_rows[bass.ds(turn * TURN + k * TILES, TILES), :]
                    sp.dma_start(lo_row[:, k, :], src.rearrange("t e -> (t e)").unsqueeze(0).to_broadcast([P, TILES * P])
                                 ).then_inc(rows_in[k], 16)
                    for (w, n, dram), st in zip(parts, staged):
                        sp.dma_start(st[:, k, :], dram.rearrange("(p c) w -> p (c w)", p=P)
                                     [:, bass.ds((turn * TURN + k * TILES) * n, TILES * n)]).then_inc(parts_in[k], 16)

            loop(sp, TURNS, body)

        @block.vector
        def _(dve):
            if words > columns[-1][0] + 1:
                dve.memset(record[:], 0.0)
            dve.memset(picked[:], 0.0).then_inc(zeroed, 1)

            def prepare(turn, first, k):
                if not first:
                    dve.wait_ge(read, (turn - 1) * SLOTS + k + 1)
                cols = bass.ds(turn * TURN + k * TILES, TILES)
                one_hots(dve, c, lo_b, hi_b, cols, lo_hot[:, k], hi_hot[:, k], hot)
                dve.wait_ge(rows_in[k], turn * 16 + 16)
                dve.tensor_scalar(lo_hot_t[:, k].rearrange("p t e -> p (t e)"), lo_row[:, k, :],
                                  c.lane[:, 0:1], None, ALU.is_equal)
                for j in range(TILES):
                    ins = dve.scalar_tensor_tensor(
                        out=before[:, k, j, :], in0=lo_row[:, k, j * P:(j + 1) * P],
                        scalar=lo_b[:, bass.ds(turn * TURN + k * TILES + j, 1)], in1=c.above_b[:],
                        op0=ALU.is_equal, op1=ALU.mult)
                ins.then_inc(hot_t, 1)

            def finish(turn, first, k):
                n = turn * SLOTS + k
                dve.wait_ge(read, n + 1)
                dve.tensor_tensor(picked[:], pread[:, k, 0:TILES * HI].rearrange("p (t h) -> p t h", t=TILES),
                                  hi_hot[:, k], ALU.mult).then_inc(pick, 1)
                dve.wait_ge(pick, n + 1)
                dve.tensor_reduce(pos_f[:], picked[:], AX.X, ALU.add).then_inc(pos, 1)
                dve.wait_ge(pos, n + 1)
                if not first:
                    dve.wait_ge(scattered[k], turn * (16 * TILES))
                dve.tensor_copy(pos_i[:, k, :], pos_f[:]).then_inc(posd, 1)

            def body(turn, first):
                for k in range(SLOTS):
                    prepare(turn, first, k)
                    if k >= 1:
                        finish(turn, first, k - 1)
                finish(turn, first, SLOTS - 1)

            loop(dve, TURNS, body)

        @block.tensor
        def _(pe):
            pe.matmul(pcount[:, 0:HI], c.ident[:], info.start[:], start=True, stop=True).then_inc(added, 1)

            def body(turn, first):
                for k in range(SLOTS):
                    pe.wait_ge(hot_t, turn * SLOTS + k + 1)
                    if not first:
                        pe.wait_ge(pick, (turn - 1) * SLOTS + k + 1)
                    for j in range(TILES):
                        tile = turn * TURN + k * TILES + j
                        pe.wait_ge(counter, tile + 1)
                        pe.matmul(pcount[:, 0:HI], lo_hot[:, k, j, :], hi_hot[:, k, j, :],
                                  start=False, stop=True, skip_group_check=True).then_inc(added, 1)
                        out = pread[:, k, j * HI:(j + 1) * HI]
                        pe.matmul(out, before[:, k, j, :], hi_hot[:, k, j, :], start=True, stop=False,
                                  skip_group_check=True)
                        mm = pe.matmul(out, lo_hot_t[:, k, j, :], place[:, j, 0:HI], start=False, stop=True,
                                       skip_group_check=True)
                    mm.then_inc(read, 1)

            loop(pe, TURNS, body)

        @block.scalar
        def _(act):
            act.wait_ge(zeroed, 1)
            act.wait_ge(added, 1)
            act.copy(place[:, 0, 0:HI], pcount[:, 0:HI]).then_inc(counter, 1)

            def build(turn, first, k):
                if not first:
                    act.wait_ge(scattered[k], turn * (16 * TILES))
                cols = bass.ds(turn * TURN + k * TILES, TILES)
                if parts:
                    act.wait_ge(parts_in[k], (turn + 1) * (16 * len(parts)))
                for (w, n, _), st in zip(parts, staged):
                    act.copy(record[:, k, :, w:w + n], st[:, k, :].rearrange("p (t n) -> p t n", n=n))
                for w, col in columns:
                    ins = act.copy(record[:, k, :, w], col[:, cols])
                ins.then_inc(built, 1)

            def body(turn, first):
                for k in range(SLOTS):
                    build(turn, first, k)
                    for j in range(TILES):
                        act.wait_ge(added, turn * TURN + k * TILES + j + 2)
                        act.copy(place[:, (j + 1) % TILES, 0:HI], pcount[:, 0:HI]).then_inc(counter, 1)

            loop(act, TURNS, body)

        @block.gpsimd
        def _(pool):
            def body(turn, first):
                for k in range(SLOTS):
                    pool.wait_ge(posd, turn * SLOTS + k + 1)
                    pool.sem_inc(gate, 1)
                    pool.wait_ge(built, turn * SLOTS + k + 1)
                    pool.sem_inc(gate, 1)
                    for j in range(TILES):
                        pool.indirect_dma_start(rec, bass.IndirectOffsetOnAxis(pos_i[:, k, j:j + 1], 0),
                                                record[:, k, j, :], None).then_inc(scattered[k], 16)

            loop(pool, TURNS, body)
            for k in range(SLOTS):
                pool.wait_ge(scattered[k], TURNS * 16 * TILES)


class Info:

    def __init__(self, sb, name):
        self.cnt, self.start, self.used = (sb(f"{name}_{n}", [P, HI]) for n in ("cnt", "start", "used"))
        self.end_i = sb(f"{name}_end", [P, HI], I32)


class Keys:

    def __init__(self, sb):
        self.weight, self.source, self.row = (sb(f"key_{n}", [P, COLS]) for n in ("weight", "source", "row"))
        self.lo, self.hi = sb("key_lo", [P, COLS], BF16), sb("key_hi", [P, COLS], BF16)
        self.kind = sb("key_kind", [P, COLS], I32)
        self.ordered = sb("ordered", [1, 1], I32)


class Constants:
    def __init__(self, sb):
        self.free, self.ident, self.above, self.down, self.up, self.ones = (
            sb(n, [P, P]) for n in ("free", "ident", "above", "down", "up", "ones"))
        self.free_b, self.ident_b, self.above_b = (sb(n, [P, P], BF16) for n in ("free_b", "ident_b", "above_b"))
        self.lane = sb("lane", [P, 1])
        self.wide = sb("wide", [P, WINDOW])

COLS_SLOT = 25
PASS_TURNS = COLS // (COLS_SLOT * SLOTS)
PAD = COLS_SLOT * SLOTS
BLOCK = 7
BLOCKS = HI // BLOCK
PIECE = 512
assert BLOCKS * BLOCK == HI and PASS_TURNS * COLS_SLOT * SLOTS == COLS


class Runs:

    def __init__(self, sb, name, info):
        self.info = info
        self.index = sb(f"{name}_index", [P, COLS + PAD], I32)
        self.weight = sb(f"{name}_weight", [P, COLS])
        self.goes_on = sb(f"{name}_goes_on", [P, COLS])
        self.first_lo = sb(f"{name}_first_lo", [P, P])
        self.first_hi = sb(f"{name}_first_hi", [P, HI])
        self.first_row = sb(f"{name}_first_row", [P, 1], I32)
        self.through = sb(f"{name}_through", [D, P])


def load_runs(nc, c, name, rec, runs, source):
    with Scope(nc, name) as s:
        recs = s.sb("recs", [P, SLOTS, COLS_SLOT, WORDS])
        row = s.sb("row", [P, COLS])
        ids, lo, hi = (s.sb(n, [P, COLS], I32) for n in ("ids", "lo", "hi"))
        firsts = s.sb("firsts", [P, WORDS])
        tmp = s.sb("tmp", [P, 8])
        alive = s.sb("alive", [P, D])
        psh = s.ps("shifted", [P, 512])
        landed, taken_a, taken_v = s.sems("landed", SLOTS), s.sem("taken_a"), s.sem("taken_v")
        first_in, line_sem, ends, shifted = s.sem("first_in"), s.sem("line"), s.sem("ends"), s.sem("shifted")
        block = s.block()
        view = rec.rearrange("(p c) w -> p (c w)", p=P)

        @block.sync
        def _(sp):
            sp.dma_start(firsts[:], view[:, 0:WORDS]).then_inc(first_in, 16)

            def body(turn, first):
                for k in range(SLOTS):
                    if not first:
                        sp.wait_ge(taken_a, (turn - 1) * SLOTS + k + 1)
                        sp.wait_ge(taken_v, (turn - 1) * SLOTS + k + 1)
                    at = (turn * SLOTS + k) * COLS_SLOT
                    sp.dma_start(recs[:, k].rearrange("p c w -> p (c w)"),
                                 view[:, bass.ds(at * WORDS, COLS_SLOT * WORDS)]).then_inc(landed[k], 16)

            loop(sp, PASS_TURNS, body)

        @block.scalar
        def _(act):
            def body(turn, first):
                for k in range(SLOTS):
                    cols = bass.ds((turn * SLOTS + k) * COLS_SLOT, COLS_SLOT)
                    act.wait_ge(landed[k], turn * 16 + 16)
                    act.copy(runs.weight[:, cols], recs[:, k, :, KIND]).then_inc(taken_a, 1)

            loop(act, PASS_TURNS, body)

        @block.vector
        def _(dve):
            def body(turn, first):
                for k in range(SLOTS):
                    cols = bass.ds((turn * SLOTS + k) * COLS_SLOT, COLS_SLOT)
                    dve.wait_ge(landed[k], turn * 16 + 16)
                    dve.tensor_scalar(source[:, cols], recs[:, k, :, SOURCE], -1.0, None, ALU.add)
                    dve.tensor_copy(row[:, cols], recs[:, k, :, DST_ROW]).then_inc(taken_v, 1)

            loop(dve, PASS_TURNS, body)
            line = Line(dve, line_sem)
            dve.wait_ge(taken_v, PASS_TURNS * SLOTS)
            dve.wait_ge(taken_a, PASS_TURNS * SLOTS)
            line.do(dve.tensor_copy(ids[:], source[:]))
            line.do(dve.tensor_scalar(lo[:], ids[:], 127, None, ALU.bitwise_and))
            line.do(dve.tensor_scalar(hi[:], ids[:], 7, None, ALU.arith_shift_right))
            line.do(dve.scalar_tensor_tensor(out=ids[:], in0=lo[:], scalar=float(HI), in1=hi[:],
                                             op0=ALU.mult, op1=ALU.add))
            line.do(dve.scalar_tensor_tensor(out=runs.index[:, 0:COLS], in0=ids[:], scalar=8.0, in1=runs.weight[:],
                                             op0=ALU.mult, op1=ALU.add))
            line.do(dve.tensor_copy(runs.index[:, COLS:COLS + PAD], runs.index[:, 0:PAD]))
            line.do(dve.tensor_tensor(runs.goes_on[:, 1:COLS], row[:, 1:COLS], row[:, 0:COLS - 1], ALU.is_equal))
            dve.tensor_scalar(tmp[:, 0:1], row[:, COLS - 1:COLS], 1.0, None, ALU.add).then_inc(ends, 1)
            line.do(dve.tensor_scalar(tmp[:, 1:2], row[:, 0:1], 1.0, None, ALU.add))
            dve.wait_ge(shifted, 1)
            line.do(dve.tensor_tensor(runs.goes_on[:, 0:1], tmp[:, 1:2], psh[:, 0:1], ALU.is_equal))
            dve.tensor_copy(tmp[:, 2:3], runs.goes_on[:, 0:1]).then_inc(ends, 1)
            line.do(dve.tensor_reduce(tmp[:, 3:4], runs.goes_on[:], AX.X, ALU.min))
            dve.tensor_copy(alive[:], tmp[:, 3:4].to_broadcast([P, D])).then_inc(ends, 1)
            dve.wait_ge(shifted, 3)
            line.do(dve.tensor_copy(runs.through[:], psh[0:D, 128:256]))
            line.do(dve.tensor_tensor(tmp[:, 4:5], tmp[:, 3:4], psh[:, 1:2], ALU.mult))
            line.do(dve.tensor_scalar(tmp[:, 5:6], tmp[:, 4:5], -1.0, 1.0, ALU.mult, ALU.add))
            line.do(dve.tensor_tensor(tmp[:, 6:7], tmp[:, 5:6], tmp[:, 2:3], ALU.mult))
            dve.wait_ge(first_in, 16)
            line.do(dve.tensor_copy(runs.first_row[:], firsts[:, DST_ROW:DST_ROW + 1]))
            line.do(dve.tensor_scalar(runs.first_lo[:], c.free[:], firsts[:, DST_LO:DST_LO + 1], None, ALU.is_equal))
            line.do(dve.tensor_scalar(runs.first_hi[:], c.free[:, 0:HI], firsts[:, DST_HI:DST_HI + 1], tmp[:, 6:7],
                                      ALU.is_equal, ALU.mult))

        @block.tensor
        def _(pe):
            pe.wait_ge(ends, 1)
            pe.matmul(psh[:, 0:1], c.down[:], tmp[:, 0:1], start=True, stop=True).then_inc(shifted, 1)
            pe.wait_ge(ends, 2)
            pe.matmul(psh[:, 1:2], c.up[:], tmp[:, 2:3], start=True, stop=True).then_inc(shifted, 1)
            pe.wait_ge(ends, 3)
            pe.matmul(psh[0:D, 128:256], alive[:], c.ident[:], start=True, stop=True).then_inc(shifted, 1)


class Carry:

    def __init__(self, s, width):
        self.width = width
        self.last = s.sb("last", [P, width])
        self.rows = s.sb("rows", [width, P + 1])
        self.spread = s.sb("spread", [P, HI, width])
        self.pt = s.ps("last_rows", [P, 512])
        self.fix = s.ps("fix", [P, 4 * PIECE])
        self.last_done, self.turned, self.scanned, self.back, self.laid, self.fixed = (
            s.sem(n) for n in ("last_done", "turned", "carry_scanned", "back", "laid", "fixed"))

    def tensor(self, pe, c, runs):
        w = self.width
        pe.wait_ge(self.last_done, 1)
        pe.transpose(self.pt[0:w, 0:P], self.last[:], c.ident[:]).then_inc(self.turned, 1)
        pe.wait_ge(self.scanned, 1)
        pe.matmul(self.pt[:, P:P + w], self.rows[:, 0:P], c.ident[0:w, 0:w], start=True, stop=True
                  ).then_inc(self.back, 1)
        pe.wait_ge(self.laid, 1)
        flat = self.spread[:].rearrange("p h f -> p (h f)")
        for at in range(0, HI * w, PIECE):
            to = min(at + PIECE, HI * w)
            mm = pe.matmul(self.fix[:, at:to], runs.first_lo[:], flat[:, at:to], start=True, stop=True)
        mm.then_inc(self.fixed, 1)

    def vector(self, dve, runs):
        w = self.width
        dve.wait_ge(self.turned, 1)
        dve.tensor_tensor_scan(self.rows[:, 1:P + 1], runs.through[0:w, :], self.pt[0:w, 0:P], 0.0,
                               ALU.mult, ALU.add).then_inc(self.scanned, 1)
        dve.wait_ge(self.back, 1)
        dve.tensor_tensor(self.spread[:], runs.first_hi[:].unsqueeze(2).to_broadcast([P, HI, w]),
                          self.pt[:, P:P + w].unsqueeze(1).to_broadcast([P, HI, w]), ALU.mult
                          ).then_inc(self.laid, 1)

    def add(self, dve, runs, ends, out, masked, done):
        w = self.width
        dve.tensor_tensor(out, ends, runs.info.used[:].unsqueeze(2).to_broadcast([P, HI, w]), ALU.mult
                          ).then_inc(masked, 1)
        dve.wait_ge(masked, 1)
        dve.wait_ge(self.fixed, 1)
        dve.tensor_tensor(out, out, self.fix[:, 0:HI * w].rearrange("p (h f) -> p h f", f=w), ALU.add
                          ).then_inc(done, 1)


def gather_ends(pool, runs, sums, ends, ends_in):
    for h in range(HI):
        pool.indirect_dma_start(ends[:, h, :], None, sums,
                                bass.IndirectOffsetOnAxis(runs.info.end_i[:, h:h + 1], 0)).then_inc(ends_in, 16)


def weighted_sums(nc, c, name, runs, table, sums, Y):
    with Scope(nc, name) as s:
        picked = s.sb("picked", [P, SLOTS, COLS_SLOT, D])
        staged = s.sb("staged", [P, SLOTS, COLS_SLOT], I32)
        message = s.sb("message", [P, COLS_SLOT, D])
        running = s.sb("running", [P, SLOTS, COLS_SLOT, D])
        ends = s.sb("ends", [P, HI, D])
        carry = Carry(s, D)
        staged_done, gathered = s.sems("staged_done", SLOTS), s.sems("gathered", SLOTS)
        weighed, scanned, kept, stored, free = (s.sem(n) for n in ("weighed", "scanned", "kept", "stored", "free"))
        ends_in, masked, y_done, gate = (s.sem(n) for n in ("ends_in", "masked", "y_done", "gate"))
        block = s.block()
        slots = PASS_TURNS * SLOTS
        flat = sums.rearrange("(p c) f -> p (c f)", p=P)

        @block.sync
        def _(sp):
            sp.sem_inc(free, SLOTS)
            with sp.Fori(0, PASS_TURNS) as turn:
                for k in range(SLOTS):
                    n = turn * SLOTS + k
                    sp.wait_ge(scanned, n + 1)
                    sp.dma_start(flat[:, bass.ds(n * (COLS_SLOT * D), COLS_SLOT * D)],
                                 running[:, k].rearrange("p c f -> p (c f)")).then_inc(stored, 16)
                    sp.wait_ge(stored, n * 16 + 16)
                    sp.sem_inc(free, 1)

        @block.gpsimd
        def _(pool):
            with pool.Fori(0, PASS_TURNS) as turn:
                for k in range(SLOTS):
                    pool.wait_ge(staged_done[k], turn + 1)
                    pool.sem_inc(gate, 1)
                    for j in range(COLS_SLOT):
                        pool.indirect_dma_start(picked[:, k, j, :], None, table,
                                                bass.IndirectOffsetOnAxis(staged[:, k, j:j + 1], 0)
                                                ).then_inc(gathered[k], 16)
            pool.wait_ge(stored, 16 * slots)
            pool.sem_inc(gate, 1)
            gather_ends(pool, runs, sums, ends, ends_in)

        @block.vector
        def _(dve):
            dve.memset(carry.rows[:], 0.0)
            for k in range(SLOTS):
                dve.tensor_copy(staged[:, k, :], runs.index[:, k * COLS_SLOT:(k + 1) * COLS_SLOT]
                                ).then_inc(staged_done[k], 1)
            dve.memset(carry.last[:], 0.0).then_inc(kept, 1)
            with dve.Fori(0, PASS_TURNS) as turn:
                for k in range(SLOTS):
                    n = turn * SLOTS + k
                    at = n * COLS_SLOT
                    dve.wait_ge(gathered[k], (turn + 1) * (16 * COLS_SLOT))
                    dve.tensor_tensor(message[:], picked[:, k],
                                      runs.weight[:, bass.ds(at, COLS_SLOT)].unsqueeze(2)
                                      .to_broadcast([P, COLS_SLOT, D]), ALU.mult).then_inc(weighed, 1)
                    dve.wait_ge(weighed, n + 1)
                    dve.tensor_copy(staged[:, k, :], runs.index[:, bass.ds(at + PAD, COLS_SLOT)]
                                    ).then_inc(staged_done[k], 1)
                    dve.wait_ge(kept, n + 1)
                    dve.wait_ge(free, n + 1)
                    for f in range(D):
                        ins = dve.tensor_tensor_scan(running[:, k, :, f], runs.goes_on[:, bass.ds(at, COLS_SLOT)],
                                                     message[:, :, f], carry.last[:, f:f + 1], ALU.mult, ALU.add)
                    ins.then_inc(scanned, 1)
                    dve.wait_ge(scanned, n + 1)
                    dve.tensor_copy(carry.last[:], running[:, k, COLS_SLOT - 1, :]).then_inc(kept, 1)
            dve.wait_ge(kept, slots + 1)
            dve.sem_inc(carry.last_done, 1)
            carry.vector(dve, runs)
            dve.wait_ge(ends_in, 16 * HI)
            carry.add(dve, runs, ends[:], Y[:], masked, y_done)
            dve.wait_ge(y_done, 1)

        @block.tensor
        def _(pe):
            carry.tensor(pe, c, runs)


T = 8


def type_counts(nc, c, name, runs, kinds, sums, counts):
    with Scope(nc, name) as s:
        hot = s.sb("hot", [P, COLS_SLOT, T])
        running = s.sb("running", [P, SLOTS, COLS_SLOT, T])
        ends = s.sb("ends", [P, HI, T])
        carry = Carry(s, T)
        hotted, scanned, kept, stored, free, ends_in, masked, counted, gate = (
            s.sem(n) for n in ("hotted", "scanned", "kept", "stored", "free", "ends_in", "masked", "counted", "gate"))
        block = s.block()
        flat = sums.rearrange("(p c) f -> p (c f)", p=P)

        @block.sync
        def _(sp):
            sp.sem_inc(free, SLOTS)
            with sp.Fori(0, PASS_TURNS) as turn:
                for k in range(SLOTS):
                    n = turn * SLOTS + k
                    sp.wait_ge(scanned, n + 1)
                    sp.dma_start(flat[:, bass.ds(n * (COLS_SLOT * T), COLS_SLOT * T)],
                                 running[:, k].rearrange("p c f -> p (c f)")).then_inc(stored, 16)
                    sp.wait_ge(stored, n * 16 + 16)
                    sp.sem_inc(free, 1)

        @block.gpsimd
        def _(pool):
            pool.wait_ge(stored, 16 * PASS_TURNS * SLOTS)
            pool.sem_inc(gate, 1)
            gather_ends(pool, runs, sums, ends, ends_in)

        @block.vector
        def _(dve):
            dve.memset(carry.rows[:], 0.0)
            dve.memset(carry.last[:], 0.0).then_inc(kept, 1)
            with dve.Fori(0, PASS_TURNS) as turn:
                for k in range(SLOTS):
                    n = turn * SLOTS + k
                    cols = bass.ds(n * COLS_SLOT, COLS_SLOT)
                    dve.tensor_tensor(hot[:], kinds[:, cols].unsqueeze(2).to_broadcast([P, COLS_SLOT, T]),
                                      c.free[:, 0:T].unsqueeze(1).to_broadcast([P, COLS_SLOT, T]), ALU.is_equal
                                      ).then_inc(hotted, 1)
                    dve.wait_ge(hotted, n + 1)
                    dve.wait_ge(kept, n + 1)
                    dve.wait_ge(free, n + 1)
                    for f in range(T):
                        ins = dve.tensor_tensor_scan(running[:, k, :, f], runs.goes_on[:, cols], hot[:, :, f],
                                                     carry.last[:, f:f + 1], ALU.mult, ALU.add)
                    ins.then_inc(scanned, 1)
                    dve.wait_ge(scanned, n + 1)
                    dve.tensor_copy(carry.last[:], running[:, k, COLS_SLOT - 1, :]).then_inc(kept, 1)
            dve.wait_ge(kept, PASS_TURNS * SLOTS + 1)
            dve.sem_inc(carry.last_done, 1)
            carry.vector(dve, runs)
            dve.wait_ge(ends_in, 16 * HI)
            carry.add(dve, runs, ends[:], counts[:], masked, counted)
            dve.wait_ge(counted, 1)

        @block.tensor
        def _(pe):
            carry.tensor(pe, c, runs)


def relation_norms(nc, c, runs, counts, filled):
    inverse_rows = nc.dram_tensor("inverse_rows", (ROWS, T), F32).ap()
    with Scope(nc, "norm") as s:
        inverse = s.sb("inverse", [P, HI, T])
        to_f, to_i = s.sb("to_f", [P, 3, HI]), s.sb("to_i", [P, HI], I32)
        zeros = s.sb("zeros", [P, 1000])
        gate, line_sem, zeroed, cleared, inverted, spread, out = (
            s.sem(n) for n in ("gate", "line", "zeroed", "cleared", "inverted", "spread", "out"))
        block = s.block()
        fill_flat = filled[0:N_EDGES, :].rearrange("(p c) f -> p (c f)", p=P)

        @block.scalar
        def _(act):
            act.wait_ge(zeroed, 1)
            for i in range(COLS * T // 1000):
                act.dma_start(fill_flat[:, i * 1000:(i + 1) * 1000], zeros[:]).then_inc(cleared, 16)
            act.wait_ge(inverted, 1)
            act.dma_start(inverse_rows.rearrange("(p h) t -> p (h t)", p=P),
                          inverse[:].rearrange("p h t -> p (h t)")).then_inc(out, 16)
            act.wait_ge(out, 16)

        @block.gpsimd
        def _(pool):
            pool.wait_ge(cleared, 16 * (COLS * T // 1000))
            pool.sem_inc(gate, 1)
            pool.wait_ge(inverted, 1)
            pool.sem_inc(gate, 1)
            for h in range(HI):
                pool.indirect_dma_start(filled, bass.IndirectOffsetOnAxis(to_i[:, h:h + 1], 0),
                                        inverse[:, h, :], None).then_inc(spread, 16)
            pool.wait_ge(spread, 16 * HI)

        @block.vector
        def _(dve):
            line = Line(dve, line_sem)
            dve.memset(zeros[:], 0.0).then_inc(zeroed, 1)
            line.do(dve.tensor_scalar(to_f[:, 0, :], c.lane[:].to_broadcast([P, HI]), float(HI), float(N_EDGES),
                                      ALU.mult, ALU.add))
            line.do(dve.tensor_tensor(to_f[:, 1, :], to_f[:, 0, :], c.free[:, 0:HI], ALU.add))
            line.do(dve.tensor_tensor(to_f[:, 2, :], runs.info.start[:], to_f[:, 1, :], ALU.subtract))
            line.do(dve.tensor_tensor(to_f[:, 0, :], to_f[:, 2, :], runs.info.used[:], ALU.mult))
            line.do(dve.tensor_tensor(to_i[:], to_f[:, 0, :], to_f[:, 1, :], ALU.add))
            line.do(dve.tensor_scalar(inverse[:], counts[:], 1.0, None, ALU.max))
            dve.reciprocal(inverse[:], inverse[:]).then_inc(inverted, 1)

    with Scope(nc, "fill") as s:
        given = s.sb("given", [P, SLOTS, COLS_SLOT, T])
        along = s.sb("along", [P, COLS_SLOT, T])
        hot = s.sb("hot", [P, COLS_SLOT, T])
        own = s.sb("own", [P, COLS_SLOT, T])
        norm = s.sb("norm", [P, COLS_SLOT])
        last = s.sb("last", [P, T])
        written = s.sem("written")
        landed = s.sems("landed", SLOTS)
        first_in, scanned, kept, hotted, used = (s.sem(n) for n in ("first_in", "scanned", "kept", "hotted", "used"))
        block = s.block()
        fill_flat = filled[0:N_EDGES, :].rearrange("(p c) f -> p (c f)", p=P)

        @block.gpsimd
        def _(pool):
            pool.indirect_dma_start(last[:], None, inverse_rows,
                                    bass.IndirectOffsetOnAxis(runs.first_row[:, 0:1], 0)).then_inc(first_in, 16)

        @block.sync
        def _(sp):
            def body(turn, first):
                for k in range(SLOTS):
                    if not first:
                        sp.wait_ge(scanned, (turn - 1) * SLOTS + k + 1)
                    n = turn * SLOTS + k
                    sp.dma_start(given[:, k].rearrange("p c f -> p (c f)"),
                                 fill_flat[:, bass.ds(n * (COLS_SLOT * T), COLS_SLOT * T)]).then_inc(landed[k], 16)

            loop(sp, PASS_TURNS, body)

        @block.vector
        def _(dve):
            dve.wait_ge(first_in, 16)
            dve.sem_inc(kept, 1)
            with dve.Fori(0, PASS_TURNS) as turn:
                for k in range(SLOTS):
                    n = turn * SLOTS + k
                    cols = bass.ds(n * COLS_SLOT, COLS_SLOT)
                    dve.wait_ge(landed[k], turn * 16 + 16)
                    dve.tensor_tensor(hot[:], runs.weight[:, cols].unsqueeze(2).to_broadcast([P, COLS_SLOT, T]),
                                      c.free[:, 0:T].unsqueeze(1).to_broadcast([P, COLS_SLOT, T]), ALU.is_equal)
                    dve.wait_ge(kept, n + 1)
                    for f in range(T):
                        ins = dve.tensor_tensor_scan(along[:, :, f], runs.goes_on[:, cols], given[:, k, :, f],
                                                     last[:, f:f + 1], ALU.mult, ALU.add)
                    ins.then_inc(scanned, 1)
                    dve.wait_ge(scanned, n + 1)
                    dve.tensor_copy(last[:], along[:, COLS_SLOT - 1, :]).then_inc(kept, 1)
                    dve.tensor_tensor(own[:], along[:], hot[:], ALU.mult).then_inc(hotted, 1)
                    dve.wait_ge(hotted, n + 1)
                    dve.tensor_reduce(norm[:], own[:], AX.X, ALU.add).then_inc(used, 1)
                    dve.wait_ge(used, n + 1)
                    dve.tensor_scalar(runs.weight[:, cols], norm[:], 1.0, None, ALU.mult).then_inc(written, 1)
                    dve.wait_ge(written, n + 1)


class Places:

    def __init__(self, sb):
        self.group = sb("group", [1, G_TURNS], I32)
        self.index = sb("g_index", [P, G_COLS + TURN], I32)
        self.b = sb("g_b", [P, G_COLS], BF16)
        self.a = sb("g_a", [P, G_COLS], BF16)


def group_places(nc, c, groups, counts, place, starts, G):
    with Scope(nc, "places") as s:
        hot, running, part = (s.sb(n, [P, COLS]) for n in ("hot", "running", "part"))
        pos, ones = s.sb("pos", [P, COLS]), s.sb("ones", [P, COLS])
        totals, sizes, turns, before, first, low = (s.sb(n, [P, T]) for n in ("totals", "sizes", "turns", "before", "first", "low"))
        turn_id, ended, group = s.sb("turn_id", [1, G_TURNS]), s.sb("ended", [1, G_TURNS]), s.sb("group", [1, G_TURNS])
        turn_i = s.sb("turn_i", [P, G_TURNS], I32)
        turns_i = s.sb("turns_i", [P, T], I32)
        run, lower = s.sb("run", [P, HI]), s.sb("lower", [P, HI])
        spare, start, used = s.sb("spare", [P, HI]), s.sb("start", [P, HI]), s.sb("used", [P, HI])
        node_start = s.sb("node_start", [P, HI, T], I32)
        p_sum = s.ps("p_sum", [P, PIECE])
        p_cnt = s.ps("p_cnt", [P, PIECE])
        line_sem, iotas, counted, summed, ready, looked, stored = (
            s.sem(n) for n in ("line", "iotas", "counted", "summed", "ready", "looked", "stored"))
        block = s.block()

        @block.gpsimd
        def _(pool):
            pool.iota(turn_i[:], pattern=[[1, G_TURNS]], base=0, channel_multiplier=0).then_inc(iotas, 1)

        @block.vector
        def _(dve):
            line = Line(dve, line_sem)
            line.do(dve.memset(ones[:], 1.0))
            line.do(dve.memset(pos[:], 0.0))
            line.do(dve.memset(totals[:], 0.0))
            for g in range(GROUPS):
                line.do(dve.tensor_scalar(hot[:], groups[:], float(g), None, ALU.is_equal))
                line.do(dve.tensor_tensor_scan(running[:], ones[:], hot[:], 0.0, ALU.mult, ALU.add))
                line.do(dve.tensor_copy(totals[:, g:g + 1], running[:, COLS - 1:COLS]))
                line.do(dve.scalar_tensor_tensor(out=part[:], in0=running[:], scalar=-1.0, in1=hot[:],
                                                 op0=ALU.add, op1=ALU.mult))
                line.do(dve.tensor_tensor(pos[:], pos[:], part[:], ALU.add))
            dve.sem_inc(counted, 1)
            dve.wait_ge(summed, 1)
            line.do(dve.tensor_copy(sizes[:], p_sum[:, 0:T]))
            line.do(dve.tensor_scalar(turns_i[:], sizes[:], 1.0 / PLACES, None, ALU.mult))
            line.do(dve.tensor_copy(turns[:], turns_i[:]))
            line.do(dve.tensor_scalar(turns[:], turns[:], -1.0, 0.0, ALU.add, ALU.max))
            for _ in range(3):
                line.do(dve.scalar_tensor_tensor(out=low[:], in0=turns[:], scalar=float(PLACES), in1=sizes[:],
                                                 op0=ALU.mult, op1=ALU.is_lt))
                line.do(dve.tensor_tensor(turns[:], turns[:], low[:], ALU.add))
            line.do(dve.tensor_tensor_scan(before[:], ones[:, 0:T], turns[:], 0.0, ALU.mult, ALU.add))
            line.do(dve.tensor_tensor(first[:], before[:], turns[:], ALU.subtract))
            line.do(dve.tensor_scalar(first[:], first[:], float(PLACES), None, ALU.mult))
            line.do(dve.tensor_tensor(low[:], first[:], p_sum[:, P:P + T], ALU.add))
            for g in range(GROUPS):
                line.do(dve.tensor_scalar(part[:], groups[:], float(g), low[:, g:g + 1], ALU.is_equal, ALU.mult))
                line.do(dve.tensor_tensor(pos[:], pos[:], part[:], ALU.add))
            line.do(dve.tensor_copy(place[:], pos[:]))

            dve.wait_ge(iotas, 1)
            line.do(dve.tensor_copy(turn_id[:], turn_i[0:1, :]))
            line.do(dve.memset(group[:], 0.0))
            for g in range(GROUPS - 1):
                line.do(dve.tensor_scalar(ended[:], turn_id[:], before[0:1, g:g + 1], None, ALU.is_ge))
                line.do(dve.tensor_tensor(group[:], group[:], ended[:], ALU.add))
            line.do(dve.tensor_copy(G.group[:], group[:]))

            line.do(dve.tensor_scalar(spare[:], c.lane[:].to_broadcast([P, HI]), float(HI),
                                      float(G_TURNS * PLACES), ALU.mult, ALU.add))
            line.do(dve.tensor_tensor(spare[:], spare[:], c.free[:, 0:HI], ALU.add))
            line.do(dve.memset(node_start[:], 0))
            for g in range(GROUPS):
                line.do(dve.tensor_scalar(run[:], counts[:, :, g], 1.0, None, ALU.mult))
                dve.sem_inc(ready, 1)
                dve.wait_ge(looked, g + 1)
                line.do(dve.tensor_copy(lower[:], p_cnt[:, P:P + HI]))
                line.do(dve.tensor_tensor_scan(start[:], ones[:, 0:HI], lower[:], 0.0, ALU.mult, ALU.add))
                line.do(dve.tensor_tensor(start[:], start[:], lower[:], ALU.subtract))
                line.do(dve.tensor_tensor(start[:], start[:], p_cnt[:, 0:HI], ALU.add))
                line.do(dve.scalar_tensor_tensor(out=start[:], in0=start[:], scalar=first[:, g:g + 1], in1=spare[:],
                                                 op0=ALU.add, op1=ALU.subtract))
                line.do(dve.tensor_scalar(used[:], run[:], 1.0, None, ALU.min))
                line.do(dve.tensor_tensor(start[:], start[:], used[:], ALU.mult))
                line.do(dve.tensor_tensor(node_start[:, :, g], start[:], spare[:], ALU.add))
                line.do(dve.tensor_scalar(spare[:], spare[:], float(ROWS), None, ALU.add))
            dve.sem_inc(ready, 1)

        @block.tensor
        def _(pe):
            pe.wait_ge(counted, 1)
            pe.matmul(p_sum[:, 0:T], c.ones[:], totals[:], start=True, stop=True)
            pe.matmul(p_sum[:, P:P + T], c.above[:], totals[:], start=True, stop=True).then_inc(summed, 1)
            for g in range(GROUPS):
                pe.wait_ge(ready, g + 1)
                pe.matmul(p_cnt[:, 0:HI], c.above[:], run[:], start=True, stop=True)
                pe.matmul(p_cnt[:, P:P + HI], c.ones[:], run[:], start=True, stop=True).then_inc(looked, 1)

        @block.sync
        def _(sp):
            sp.wait_ge(ready, GROUPS + 1)
            sp.dma_start(starts.rearrange("(h p) t -> p h t", p=P), node_start[:]).then_inc(stored, 16)
            sp.wait_ge(stored, 16)


def group_ids(nc, source, groups, scratch):
    with Scope(nc, "ids") as s:
        line_sem = s.sem("line")
        block = s.block()

        @block.vector
        def _(dve):
            line = Line(dve, line_sem)
            line.do(dve.tensor_copy(scratch[:], source[:]))
            line.do(dve.tensor_scalar(scratch[:], scratch[:], (8 * WINDOW).bit_length() - 1, None,
                                      ALU.arith_shift_right))
            line.do(dve.tensor_copy(groups[:], scratch[:]))


def clear_rows(nc, drams):
    with Scope(nc, "clear") as s:
        wide = 5280
        zeros = s.sb("zeros", [P, wide])
        zeroed, cleared = s.sem("zeroed"), s.sem("cleared")
        block = s.block()

        @block.vector
        def _(dve):
            dve.memset(zeros[:], 0.0).then_inc(zeroed, 1)

        @block.sync
        def _(sp):
            n = 0
            sp.wait_ge(zeroed, 1)
            for dram in drams:
                flat = dram.rearrange("(p c) w -> p (c w)", p=P)
                for at in range(0, flat.shape[1], wide):
                    to = min(at + wide, flat.shape[1])
                    sp.dma_start(flat[:, at:to], zeros[:, 0:to - at]).then_inc(cleared, 16)
                    n += 1
            sp.wait_ge(cleared, 16 * n)


def place_edges(nc, place, rec, grouped):
    with Scope(nc, "place") as s:
        record = s.sb("record", [P, SLOTS, COLS_SLOT, WORDS])
        at = s.sb("at", [P, SLOTS, COLS_SLOT], I32)
        landed, staged = s.sems("landed", SLOTS), s.sem("staged")
        scattered, gate = s.sems("scattered", SLOTS), s.sem("gate")
        block = s.block()
        view = rec.rearrange("(p c) w -> p (c w)", p=P)

        @block.sync
        def _(sp):
            def body(turn, first):
                for k in range(SLOTS):
                    if not first:
                        sp.wait_ge(scattered[k], turn * (16 * COLS_SLOT))
                    n = turn * SLOTS + k
                    sp.dma_start(record[:, k].rearrange("p c w -> p (c w)"),
                                 view[:, bass.ds(n * (COLS_SLOT * WORDS), COLS_SLOT * WORDS)]).then_inc(landed[k], 16)

            loop(sp, PASS_TURNS, body)

        @block.vector
        def _(dve):
            def body(turn, first):
                for k in range(SLOTS):
                    if not first:
                        dve.wait_ge(scattered[k], turn * (16 * COLS_SLOT))
                    dve.tensor_copy(at[:, k, :], place[:, bass.ds((turn * SLOTS + k) * COLS_SLOT, COLS_SLOT)]
                                    ).then_inc(staged, 1)

            loop(dve, PASS_TURNS, body)

        @block.gpsimd
        def _(pool):
            with pool.Fori(0, PASS_TURNS) as turn:
                for k in range(SLOTS):
                    pool.wait_ge(staged, turn * SLOTS + k + 1)
                    pool.sem_inc(gate, 1)
                    pool.wait_ge(landed[k], turn * 16 + 16)
                    pool.sem_inc(gate, 1)
                    for j in range(COLS_SLOT):
                        pool.indirect_dma_start(grouped, bass.IndirectOffsetOnAxis(at[:, k, j:j + 1], 0),
                                                record[:, k, j, :], None).then_inc(scattered[k], 16)
            for k in range(SLOTS):
                pool.wait_ge(scattered[k], PASS_TURNS * 16 * COLS_SLOT)


G_RING = 4
assert G_TURNS % G_RING == 0


def load_places(nc, grouped, G, weight, goes_on, first_node):
    with Scope(nc, "held") as s:
        recs = s.sb("recs", [P, G_RING, TURN, WORDS])
        source = s.sb("source", [P, G_COLS])
        ids, got = s.sb("ids", [P, G_COLS], I32), s.sb("got", [P, G_COLS], I32)
        landed, taken_a, taken_v, line_sem = s.sems("landed", G_RING), s.sem("taken_a"), s.sem("taken_v"), s.sem("line")
        block = s.block()
        view = grouped.rearrange("(t p c) w -> t p (c w)", p=P, c=TURN)

        @block.sync
        def _(sp):
            def body(it, first):
                for k in range(G_RING):
                    n = it * G_RING + k
                    if not first:
                        sp.wait_ge(taken_a, n - G_RING + 1)
                        sp.wait_ge(taken_v, n - G_RING + 1)
                    sp.dma_start(recs[:, k].rearrange("p c w -> p (c w)"),
                                 view[bass.ds(n, 1)].rearrange("t p w -> (t p) w")).then_inc(landed[k], 16)

            loop(sp, G_TURNS // G_RING, body)

        @block.scalar
        def _(act):
            def body(it, first):
                for k in range(G_RING):
                    cols = bass.ds((it * G_RING + k) * TURN, TURN)
                    act.wait_ge(landed[k], it * 16 + 16)
                    act.copy(weight[:, cols], recs[:, k, :, WEIGHT])
                    act.copy(source[:, cols], recs[:, k, :, SOURCE]).then_inc(taken_a, 1)

            loop(act, G_TURNS // G_RING, body)

        @block.vector
        def _(dve):
            def body(it, first):
                for k in range(G_RING):
                    n = it * G_RING + k
                    dve.wait_ge(landed[k], it * 16 + 16)
                    dve.tensor_copy(G.index[:, bass.ds(n * TURN, TURN)], recs[:, k, :, DST_ROW])
                    dve.tensor_tensor(goes_on[:, bass.ds(n * TURN + 1, TURN - 1)], recs[:, k, 1:TURN, DST_ROW],
                                      recs[:, k, 0:TURN - 1, DST_ROW], ALU.is_equal)
                    dve.scalar_tensor_tensor(out=first_node[:, bass.ds(n, 1)], in0=recs[:, k, 0:1, DST_HI],
                                             scalar=float(P), in1=recs[:, k, 0:1, DST_LO],
                                             op0=ALU.mult, op1=ALU.add).then_inc(taken_v, 1)

            loop(dve, G_TURNS // G_RING, body)
            line = Line(dve, line_sem)
            dve.wait_ge(taken_v, G_TURNS)
            dve.wait_ge(taken_a, G_TURNS)
            line.do(dve.tensor_copy(G.index[:, G_COLS:G_COLS + TURN], G.index[:, 0:TURN]))
            line.do(dve.tensor_scalar(ids[:], source[:], -1.0, None, ALU.add))
            line.do(dve.tensor_scalar(got[:], ids[:], 7, None, ALU.bitwise_and))
            line.do(dve.tensor_copy(G.a[:], got[:]))
            line.do(dve.tensor_scalar(source[:], source[:], 1.0, None, ALU.min))
            line.do(dve.tensor_scalar(source[:], source[:], 16.0, -16.0, ALU.mult, ALU.add))
            line.do(dve.tensor_tensor(G.a[:], G.a[:], source[:], ALU.add))
            line.do(dve.tensor_scalar(got[:], ids[:], 3, WINDOW - 1, ALU.arith_shift_right, ALU.bitwise_and))
            line.do(dve.tensor_copy(G.b[:], got[:]))


class Gathering:

    def __init__(self, s):
        self.zeros = s.sb("zeros", [P, PIECE], BF16)
        self.sums = s.ps("sums", [P, 4 * PIECE])
        self.moved = s.sb("moved", [P, B_ALL])
        self.pt = s.ps("turned_rows", [P, 2, PIECE])
        self.by_b = s.sb("by_b", [P, B_BLOCKS, 8 * D])
        self.blank, self.emptied, self.flips, self.copied, self.done = (
            s.sem(n) for n in ("blank", "emptied", "flips", "copied", "rows_done"))

    def clear(self, pe):
        for at in range(0, 4 * PIECE, PIECE):
            pe.matmul(self.sums[:, at:at + PIECE], self.zeros[:, 0:P], self.zeros[:], start=True, stop=True)

    def tensor(self, pe, c, r):
        pe.wait_ge(self.emptied, r * 4 + 4)
        for k in range(B_BLOCKS):
            n = min(P, B_ALL - k * P)
            if k >= 2:
                pe.wait_ge(self.copied, r * B_BLOCKS + (k - 1))
            pe.transpose(self.pt[0:n, k % 2, 0:P], self.moved[:, k * P:k * P + n], c.ident[:]).then_inc(self.flips, 1)

    def scalar(self, act, r):
        for at in range(0, B_ALL, PIECE):
            to = min(at + PIECE, B_ALL)
            act.copy(self.moved[:, at:to], self.sums[:, at:to]).then_inc(self.emptied, 1)
        for k in range(B_BLOCKS):
            n = min(P, B_ALL - k * P)
            act.wait_ge(self.flips, r * B_BLOCKS + k + 1)
            act.copy(self.by_b[0:n, k, :], self.pt[0:n, k % 2, 0:P]).then_inc(self.copied, 1)

    def rows(self, dram, width):
        full = B_ALL // P
        cut = full * P * 8
        return [(slice(0, P), slice(0, full), dram[0:cut].rearrange("(k p a) d -> p k (a d)", p=P, a=8)),
                (slice(0, B_ALL - full * P), slice(full, full + 1),
                 dram[cut:ROWS].rearrange("(k p a) d -> p k (a d)", k=1, a=8))]


def by_hi(dram):
    return dram.rearrange("(h p) d -> p h d", p=P)


def spread_slot(dve, message, a_hot, spread, b_val, b_hot, c, ready):
    n = message.shape[1]
    dve.tensor_tensor(spread, a_hot.unsqueeze(3).to_broadcast([P, n, 8, D]),
                      message.unsqueeze(2).to_broadcast([P, n, 8, D]), ALU.mult)
    for j in range(n):
        ins = dve.tensor_scalar(b_hot[:, j, :], c.wide[:], b_val[:, j:j + 1], None, ALU.is_equal)
    ins.then_inc(ready, 1)


def add_slot(pe, gathering, group, spread, b_hot, taken):
    for j in range(TILES):
        mm = pe.matmul(gathering.sums[:, bass.ds(group * WINDOW, WINDOW)],
                       spread[:, j].rearrange("p a d -> p (a d)"), b_hot[:, j, :],
                       start=False, stop=True, skip_group_check=True)
    mm.then_inc(taken, 1)


def powers(nc, c, G, weight, goes_on, first_node, starts, filled, node_rows, H, Y, rounds):
    with Scope(nc, "powers") as s:
        at_start = s.sb("at_start", [P, B_BLOCKS, 8, T], I32)
        given = s.sb("given", [P, G_RING, TURN, D])
        first = s.sb("first", [P, G_TURNS, D])
        along = s.sb("along", [P, TURN, D])
        message = s.sb("message", [P, TURN, D])
        a_hot = s.sb("a_hot", [P, TURN, 8])
        b_val = s.sb("b_val", [P, TURN])
        spread = s.sb("spread", [P, SLOTS, TILES, 8, D])
        b_hot = s.sb("b_hot", [P, SLOTS, TILES, WINDOW])
        g = Gathering(s)
        given_in = s.sems("given_in", G_RING)
        (y_in, starts_in, y_out, spread_out, first_in, groups_ready, firsts_ready, expanded, begun, mid, ready, taken,
         gate, last_in) = (s.sem(n) for n in (
            "y_in", "starts_in", "y_out", "spread_out", "first_in", "groups_ready", "firsts_ready", "expanded", "begun",
            "mid", "ready", "taken", "gate", "last_in"))
        block = s.block()
        places = filled[0:G_TURNS * PLACES, :].rearrange("(t p c) d -> t p (c d)", p=P, c=TURN)
        per_group = -(-G_TURNS // GROUPS)

        @block.sync
        def _(sp):
            for lanes, ks, dram in g.rows(starts, T):
                sp.dma_start(at_start[lanes, ks].rearrange("p k a t -> p k (a t)"), dram).then_inc(starts_in, 16)
            sp.dma_start(by_hi(node_rows), H[:]).then_inc(y_out, 16)
            sp.wait_ge(y_out, 16)
            for lanes, ks, dram in g.rows(node_rows, D):
                sp.dma_start(g.by_b[lanes, ks], dram).then_inc(y_in, 16)
            with sp.Fori(0, rounds) as r:
                with sp.Fori(0, G_TURNS // G_RING) as it:
                    for k in range(G_RING):
                        turn = it * G_RING + k
                        group = sp.value_load(G.group[0:1, bass.ds(turn, 1)], min_val=0, max_val=GROUPS - 1)
                        sp.wait_ge(groups_ready, r * GROUPS + group + 1)
                        sp.wait_ge(expanded, r * G_TURNS + turn + 1)
                        sp.dma_start(given[:, k].rearrange("p c d -> p (c d)"),
                                     places[bass.ds(turn, 1)].rearrange("t p w -> (t p) w")).then_inc(given_in[k], 16)
                sp.wait_ge(g.copied, r * B_BLOCKS + B_BLOCKS)
                for lanes, ks, dram in g.rows(node_rows, D):
                    sp.dma_start(dram, g.by_b[lanes, ks]).then_inc(y_in, 16)
            sp.wait_ge(y_in, 32 * (rounds + 1))
            sp.dma_start(Y[:], by_hi(node_rows)).then_inc(last_in, 16)
            sp.wait_ge(last_in, 16)

        @block.gpsimd
        def _(pool):
            pool.wait_ge(starts_in, 32)
            pool.sem_inc(gate, 1)
            with pool.Fori(0, rounds) as r:
                pool.wait_ge(y_in, r * 32 + 32)
                pool.sem_inc(gate, 1)
                for i in range(GROUPS):
                    for k in range(B_BLOCKS):
                        n = min(P, B_ALL - k * P)
                        for a in range(8):
                            pool.indirect_dma_start(filled, bass.IndirectOffsetOnAxis(at_start[0:n, k, a, i:i + 1], 0),
                                                    g.by_b[0:n, k, a * D:(a + 1) * D], None).then_inc(spread_out, 16)
                    upto = min((i + 1) * per_group, G_TURNS)
                    for turn in range(i * per_group, upto):
                        pool.indirect_dma_start(first[:, turn, :], None, node_rows,
                                                bass.IndirectOffsetOnAxis(first_node[:, turn:turn + 1], 0)
                                                ).then_inc(first_in, 16)
                    pool.wait_ge(spread_out, r * (16 * 8 * B_BLOCKS * GROUPS) + 16 * 8 * B_BLOCKS * (i + 1))
                    pool.sem_inc(groups_ready, 1)
                    pool.wait_ge(first_in, r * (16 * G_TURNS) + 16 * upto)
                    pool.sem_inc(firsts_ready, upto - i * per_group)

        @block.vector
        def _(dve):
            dve.memset(g.zeros[:], 0.0).then_inc(g.blank, 1)
            dve.sem_inc(expanded, G_RING)
            with dve.Fori(0, rounds) as r:
                with dve.Fori(0, G_TURNS // G_RING) as it:
                    for k in range(G_RING):
                        turn = it * G_RING + k
                        n = r * G_TURNS + turn
                        dve.wait_ge(given_in[k], r * (G_TURNS // G_RING * 16) + it * 16 + 16)
                        dve.wait_ge(firsts_ready, n + 1)
                        dve.tensor_scalar(along[:, 0, :], first[:, bass.ds(turn, 1), :].rearrange("p c d -> p (c d)"),
                                          1.0, None, ALU.mult).then_inc(begun, 1)
                        dve.wait_ge(begun, n + 1)
                        for f in range(D):
                            ins = dve.tensor_tensor_scan(
                                along[:, 1:TURN, f], goes_on[:, bass.ds(turn * TURN + 1, TURN - 1)],
                                given[:, k, 1:TURN, f], along[:, 0, f:f + 1], ALU.mult, ALU.add)
                        ins.then_inc(expanded, 1)
                        dve.tensor_tensor(a_hot[:], G.a[:, bass.ds(turn * TURN, TURN)].unsqueeze(2)
                                          .to_broadcast([P, TURN, 8]),
                                          c.free[:, 0:8].unsqueeze(1).to_broadcast([P, TURN, 8]), ALU.is_equal)
                        dve.tensor_scalar(b_val[:], G.b[:, bass.ds(turn * TURN, TURN)], 1.0, None, ALU.mult)
                        dve.wait_ge(expanded, n + G_RING + 1)
                        dve.tensor_tensor(message[:], along[:], weight[:, bass.ds(turn * TURN, TURN)].unsqueeze(2)
                                          .to_broadcast([P, TURN, D]), ALU.mult).then_inc(mid, 1)
                        dve.wait_ge(mid, n + 1)
                        for j in range(SLOTS):
                            dve.wait_ge(taken, n * SLOTS + j + 1)
                            cols = slice(j * TILES, (j + 1) * TILES)
                            spread_slot(dve, message[:, cols], a_hot[:, cols], spread[:, j], b_val[:, cols],
                                        b_hot[:, j], c, ready)
                        dve.wait_ge(ready, n * SLOTS + SLOTS)

        @block.tensor
        def _(pe):
            pe.wait_ge(g.blank, 1)
            pe.sem_inc(taken, SLOTS)
            with pe.Fori(0, rounds) as r:
                g.clear(pe)
                with pe.Fori(0, G_TURNS) as turn:
                    group = pe.value_load(G.group[0:1, bass.ds(turn, 1)], min_val=0, max_val=GROUPS - 1)
                    for j in range(SLOTS):
                        pe.wait_ge(ready, (r * G_TURNS + turn) * SLOTS + j + 1)
                        add_slot(pe, g, group, spread[:, j], b_hot[:, j], taken)
                g.tensor(pe, c, r)

        @block.scalar
        def _(act):
            with act.Fori(0, rounds) as r:
                act.wait_ge(taken, (r + 1) * (G_TURNS * SLOTS) + SLOTS)
                g.scalar(act, r)


def contracted_sums(nc, c, name, G, table, grouped, node_rows, Y, width, hats=False, silu_scale=None):
    with Scope(nc, name) as s:
        picked = s.sb("picked", [P, SLOTS, TILES, width, D])
        staged = s.sb("staged", [P, SLOTS, TILES], I32)
        recs = s.sb("recs", [P, SLOTS, TILES, WORDS])
        product = s.sb("product", [P, TILES, width, D])
        message = s.sb("message", [P, SLOTS, TILES, D])
        active = s.sb("active", [P, SLOTS, TILES, D]) if silu_scale is not None else message
        a_hot = s.sb("a_hot", [P, TILES, 8])
        b_val = s.sb("b_val", [P, TILES])
        spread = s.sb("spread", [P, SLOTS, TILES, 8, D])
        b_hot = s.sb("b_hot", [P, SLOTS, TILES, WINDOW])
        if hats:
            centers = s.sb("centers", [P, 5])
            far = s.sb("far", [P, TILES, 2, 4])
            hat = s.sb("hat", [P, SLOTS, TILES, 2, 4])
            coef = s.sb("coef", [P, TILES, 4, 4])
        g = Gathering(s)
        staged_done, gathered, recs_in = s.sems("staged_done", SLOTS), s.sems("gathered", SLOTS), s.sems("recs_in", SLOTS)
        times, summed, activated, set_up, farther, hatted, coefs, gate, mid, ready, taken, y_out, last_in = (
            s.sem(n) for n in ("times", "summed", "activated", "set_up", "farther", "hatted", "coefs", "gate", "mid",
                               "ready", "taken", "y_out", "last_in"))
        block = s.block()
        places = grouped.rearrange("(t p c) w -> t p (c w)", p=P, c=TURN)

        @block.sync
        def _(sp):
            def body(turn, first):
                for k in range(SLOTS):
                    if not first:
                        sp.wait_ge(summed, (turn - 1) * SLOTS + k + 1)
                        if hats:
                            sp.wait_ge(hatted, (turn - 1) * SLOTS + k + 1)
                    src = places[bass.ds(turn, 1), :, k * TILES * WORDS:(k + 1) * TILES * WORDS]
                    sp.dma_start(recs[:, k].rearrange("p c w -> p (c w)"), src.rearrange("t p w -> (t p) w")
                                 ).then_inc(recs_in[k], 16)

            loop(sp, G_TURNS, body)
            sp.wait_ge(g.copied, B_BLOCKS)
            for lanes, ks, dram in g.rows(node_rows, D):
                sp.dma_start(dram, g.by_b[lanes, ks]).then_inc(y_out, 16)
            sp.wait_ge(y_out, 32)
            sp.dma_start(Y[:], by_hi(node_rows)).then_inc(last_in, 16)
            sp.wait_ge(last_in, 16)

        @block.gpsimd
        def _(pool):
            with pool.Fori(0, G_TURNS) as turn:
                for k in range(SLOTS):
                    pool.wait_ge(staged_done[k], turn + 1)
                    pool.sem_inc(gate, 1)
                    for j in range(TILES):
                        pool.indirect_dma_start(picked[:, k, j].rearrange("p w d -> p (w d)"), None, table,
                                                bass.IndirectOffsetOnAxis(staged[:, k, j:j + 1], 0)
                                                ).then_inc(gathered[k], 16)

        @block.scalar
        def _(act):
            if hats:
                act.wait_ge(set_up, 1)

            def body(turn, first):
                for k in range(SLOTS):
                    n = turn * SLOTS + k
                    if hats:
                        act.wait_ge(recs_in[k], turn * 16 + 16)
                        if not first:
                            act.wait_ge(coefs, (turn - 1) * SLOTS + k + 1)
                        if not first or k:
                            act.wait_ge(hatted, n)
                        for v in range(4):
                            ins = act.activation(far[:, :, :, v], recs[:, k, :, ATTR2:ATTR2 + 2], ACT.Abs,
                                                 bias=centers[:, v:v + 1], scale=1.5)
                        ins.then_inc(farther, 1)
                        act.wait_ge(farther, n + 1)
                        act.activation(hat[:, k], far[:], ACT.Relu, bias=centers[:, 4:5], scale=-1.0
                                       ).then_inc(hatted, 1)
                    if silu_scale is not None:
                        act.wait_ge(summed, n + 1)
                        if not first:
                            act.wait_ge(ready, (turn - 1) * SLOTS + k + 1)
                        act.activation(active[:, k], message[:, k], ACT.Silu, scale=silu_scale
                                       ).then_inc(activated, 1)

            loop(act, G_TURNS, body)
            act.wait_ge(taken, G_TURNS * SLOTS)
            g.scalar(act, 0)

        @block.vector
        def _(dve):
            if hats:
                for v, at in enumerate((1.5, 0.5, -0.5, -1.5, 1.0)):
                    ins = dve.memset(centers[:, v:v + 1], at)
                ins.then_inc(set_up, 1)
            dve.memset(g.zeros[:], 0.0).then_inc(g.blank, 1)
            for k in range(SLOTS):
                dve.tensor_copy(staged[:, k, :], G.index[:, k * TILES:(k + 1) * TILES]).then_inc(staged_done[k], 1)

            def body(turn, first):
                for k in range(SLOTS):
                    n = turn * SLOTS + k
                    at = turn * TURN + k * TILES
                    dve.wait_ge(recs_in[k], turn * 16 + 16)
                    if hats:
                        dve.wait_ge(hatted, n + 1)
                        dve.tensor_tensor(coef[:], hat[:, k, :, 0, :].unsqueeze(3).to_broadcast([P, TILES, 4, 4]),
                                          hat[:, k, :, 1, :].unsqueeze(2).to_broadcast([P, TILES, 4, 4]),
                                          ALU.mult).then_inc(coefs, 1)
                        dve.wait_ge(coefs, n + 1)
                        co = coef[:].rearrange("p t a b -> p t (a b)")
                    else:
                        co = recs[:, k, :, ATTR8:ATTR8 + width]
                    dve.wait_ge(gathered[k], (turn + 1) * (16 * TILES))
                    if not first or k:
                        dve.wait_ge(ready, n)
                    dve.tensor_tensor(product[:], picked[:, k], co.unsqueeze(3).to_broadcast([P, TILES, width, D]),
                                      ALU.mult).then_inc(times, 1)
                    dve.wait_ge(times, n + 1)
                    dve.tensor_copy(staged[:, k, :], G.index[:, bass.ds(at + TURN, TILES)]
                                    ).then_inc(staged_done[k], 1)
                    dve.tensor_reduce(message[:, k], product[:].rearrange("p t w d -> p t d w"), AX.X, ALU.add
                                      ).then_inc(summed, 1)
                    dve.tensor_tensor(a_hot[:], G.a[:, bass.ds(at, TILES)].unsqueeze(2).to_broadcast([P, TILES, 8]),
                                      c.free[:, 0:8].unsqueeze(1).to_broadcast([P, TILES, 8]), ALU.is_equal)
                    dve.tensor_scalar(b_val[:], G.b[:, bass.ds(at, TILES)], 1.0, None, ALU.mult).then_inc(mid, 1)
                    dve.wait_ge(mid, n + 1)
                    dve.wait_ge(summed if silu_scale is None else activated, n + 1)
                    if not first:
                        dve.wait_ge(taken, (turn - 1) * SLOTS + k + 1)
                    spread_slot(dve, active[:, k], a_hot[:], spread[:, k], b_val[:], b_hot[:, k], c, ready)

            loop(dve, G_TURNS, body)

        @block.tensor
        def _(pe):
            pe.wait_ge(g.blank, 1)
            g.clear(pe)
            with pe.Fori(0, G_TURNS) as turn:
                group = pe.value_load(G.group[0:1, bass.ds(turn, 1)], min_val=0, max_val=GROUPS - 1)
                for k in range(SLOTS):
                    pe.wait_ge(ready, turn * SLOTS + k + 1)
                    add_slot(pe, g, group, spread[:, k], b_hot[:, k], taken)
            g.tensor(pe, c, 0)


def project(nc, c, name, src, weight, width, out=None, table=None):
    wide = BLOCK * width
    with Scope(nc, name) as s:
        diag = s.sb("diag", [BLOCK * D, BLOCK, width])
        turned = s.sb("turned", [BLOCK * D, 2, P])
        rows = s.sb("rows", [P, 2, wide]) if out is None else None
        pt = s.ps("turned_ps", [P, 2, PIECE])
        pp = s.ps("product", [P, 4, PIECE])
        zeroed, weights_in, flipped, copied, made, moved = (
            s.sem(n) for n in ("zeroed", "weights_in", "flipped", "copied", "made", "moved"))
        stored = s.sems("stored", 2)
        block = s.block()
        pieces = [(b, at, min(at + PIECE, wide)) for b in range(BLOCKS) for at in range(0, wide, PIECE)]
        per = len(pieces) // BLOCKS

        @block.sync
        def _(sp):
            sp.wait_ge(zeroed, 1)
            for j in range(BLOCK):
                to = diag[j * D:(j + 1) * D, j, :]
                if len(weight.shape) == 3:
                    to = to.rearrange("p (a d) -> p a d", d=D)
                sp.dma_start(to, weight).then_inc(weights_in, 16)
            if out is None:
                view = table.rearrange("(p h) w -> p (h w)", p=P)
                for b in range(BLOCKS):
                    sp.wait_ge(moved, (b + 1) * per)
                    sp.dma_start(view[:, b * wide:(b + 1) * wide], rows[:, b % 2, :]).then_inc(stored[b % 2], 16)
                for half in stored:
                    sp.wait_ge(half, 16 * (BLOCKS // 2))

        @block.vector
        def _(dve):
            dve.memset(diag[:], 0.0).then_inc(zeroed, 1)
            for b in range(BLOCKS):
                dve.wait_ge(flipped, b + 1)
                if b >= 2:
                    dve.wait_ge(made, (b - 1) * per)
                dve.tensor_copy(turned[:, b % 2, :], pt[0:BLOCK * D, b % 2, 0:P]).then_inc(copied, 1)

        @block.tensor
        def _(pe):
            def turn(b):
                if b >= 2:
                    pe.wait_ge(copied, b - 1)
                pe.transpose(pt[0:BLOCK * D, b % 2, 0:P],
                             src[:, b * BLOCK:(b + 1) * BLOCK, :].rearrange("p h d -> p (h d)"),
                             c.ident[:]).then_inc(flipped, 1)

            turn(0)
            pe.wait_ge(weights_in, 16 * BLOCK)
            flat = diag[:].rearrange("p h w -> p (h w)")
            for n, (b, at, to) in enumerate(pieces):
                if at == 0:
                    if b + 1 < BLOCKS:
                        turn(b + 1)
                    pe.wait_ge(copied, b + 1)
                if n >= 4:
                    pe.wait_ge(moved, n - 3)
                pe.matmul(pp[:, n % 4, 0:to - at], turned[:, b % 2, :], flat[:, at:to],
                          start=True, stop=True).then_inc(made, 1)

        @block.scalar
        def _(act):
            for n, (b, at, to) in enumerate(pieces):
                act.wait_ge(made, n + 1)
                if out is None:
                    if b >= 2 and at == 0:
                        act.wait_ge(stored[b % 2], 16 * (b // 2))
                    dest = rows[:, b % 2, at:to]
                else:
                    dest = out[:, b * BLOCK:(b + 1) * BLOCK, :].rearrange("p h w -> p (h w)")[:, at:to]
                act.copy(dest, pp[:, n % 4, 0:to - at]).then_inc(moved, 1)


def by_node(a):
    return a.unsqueeze(2).to_broadcast([P, HI, D])


def layernorm(nc, name, X, H):
    with Scope(nc, name) as s:
        mean, var, dev, inv = (s.sb(n, [P, HI]) for n in ("mean", "var", "dev", "inv"))
        square = s.sb("square", [P, HI, D])
        line_sem, spread, rooted = s.sem("line"), s.sem("spread"), s.sem("rooted")
        block = s.block()

        @block.vector
        def _(dve):
            line = Line(dve, line_sem)
            line.do(dve.tensor_reduce(mean[:], X[:], AX.X, ALU.add))
            line.do(dve.tensor_scalar(mean[:], mean[:], 1.0 / D, None, ALU.mult))
            line.do(dve.tensor_tensor(H[:], X[:], by_node(mean[:]), ALU.subtract))
            line.do(dve.tensor_tensor(square[:], H[:], H[:], ALU.mult))
            line.do(dve.tensor_reduce(var[:], square[:], AX.X, ALU.add))
            dve.tensor_scalar(var[:], var[:], 1.0 / D, 1e-5, ALU.mult, ALU.add).then_inc(spread, 1)
            dve.wait_ge(rooted, 1)
            line.do(dve.reciprocal(inv[:], dev[:]))
            line.do(dve.tensor_tensor(H[:], H[:], by_node(inv[:]), ALU.mult))
            line.do(dve.tensor_scalar(H[:], H[:], 0.0, None, ALU.max))

        @block.scalar
        def _(act):
            act.wait_ge(spread, 1)
            act.activation(dev[:], var[:], ACT.Sqrt).then_inc(rooted, 1)


def add_nodes(nc, name, out, terms, bias=None, relu=False):
    with Scope(nc, name) as s:
        wide = s.sb("wide", [P, D])
        bias_in, line_sem = s.sem("bias_in"), s.sem("line")
        block = s.block()

        @block.sync
        def _(sp):
            if bias is not None:
                sp.dma_start(wide[:], bias.unsqueeze(0).to_broadcast([P, D])).then_inc(bias_in, 16)
                sp.wait_ge(bias_in, 16)

        @block.vector
        def _(dve):
            line = Line(dve, line_sem)
            line.do(dve.tensor_tensor(out[:], terms[0][:], terms[1][:], ALU.add))
            for term in terms[2:]:
                line.do(dve.tensor_tensor(out[:], out[:], term[:], ALU.add))
            if bias is not None:
                dve.wait_ge(bias_in, 16)
                line.do(dve.tensor_tensor(out[:], out[:], wide[:].unsqueeze(1).to_broadcast([P, HI, D]), ALU.add))
            if relu:
                line.do(dve.tensor_scalar(out[:], out[:], 0.0, None, ALU.max))


def add_log_softmax(nc, name, X, Z):
    with Scope(nc, name) as s:
        top, total, log = (s.sb(n, [P, HI]) for n in ("top", "total", "log"))
        powers = s.sb("powers", [P, HI, D])
        line_sem, lowered, raised, totals, logs = (s.sem(n) for n in ("line", "lowered", "raised", "totals", "logs"))
        block = s.block()

        @block.vector
        def _(dve):
            line = Line(dve, line_sem)
            line.do(dve.tensor_reduce(top[:], Z[:], AX.X, ALU.max))
            dve.tensor_tensor(Z[:], Z[:], by_node(top[:]), ALU.subtract).then_inc(lowered, 1)
            dve.wait_ge(raised, 1)
            dve.tensor_reduce(total[:], powers[:], AX.X, ALU.add).then_inc(totals, 1)
            dve.wait_ge(logs, 1)
            line.do(dve.tensor_tensor(Z[:], Z[:], by_node(log[:]), ALU.subtract))
            line.do(dve.tensor_tensor(X[:], X[:], Z[:], ALU.add))

        @block.scalar
        def _(act):
            act.wait_ge(lowered, 1)
            act.activation(powers[:], Z[:], ACT.Exp).then_inc(raised, 1)
            act.wait_ge(totals, 1)
            act.activation(log[:], total[:], ACT.Ln).then_inc(logs, 1)


def update(nc, name, V, agg, U, scale):
    with Scope(nc, name) as s:
        line_sem, summed = s.sem("line"), s.sem("summed")
        block = s.block()

        @block.vector
        def _(dve):
            line = Line(dve, line_sem)
            v = V[:].rearrange("p n (h k) -> p (n h) k", k=D)
            a = agg[:].rearrange("p n h -> p (n h)").unsqueeze(2).to_broadcast([P, HI * D, D])
            line.do(dve.tensor_tensor(v, v, a, ALU.mult))
            dve.tensor_reduce(U[:], V[:].rearrange("p n (h k) -> p n k h", k=D), AX.X, ALU.add).then_inc(summed, 1)

        @block.scalar
        def _(act):
            act.wait_ge(summed, 1)
            act.activation(U[:], U[:], ACT.Silu, scale=scale).then_inc(line_sem, 1)


def finish(nc, X, H, U, scale, out):
    with Scope(nc, "finish") as s:
        line_sem, ready, stored = s.sem("line"), s.sem("ready"), s.sem("stored")
        block = s.block()

        @block.vector
        def _(dve):
            line = Line(dve, line_sem)
            line.do(dve.tensor_tensor(X[:], X[:], H[:], ALU.add))
            dve.scalar_tensor_tensor(out=X[:], in0=U[:], scalar=scale, in1=X[:], op0=ALU.mult, op1=ALU.add
                                     ).then_inc(ready, 1)

        @block.sync
        def _(sp):
            sp.wait_ge(ready, 1)
            sp.dma_start(out[0:FULL * P, :].rearrange("(h p) d -> p h d", p=P), X[:, 0:FULL, :]).then_inc(stored, 16)
            sp.dma_start(out[FULL * P:N_NODES, :], X[0:REST, FULL, :]).then_inc(stored, 16)
            sp.wait_ge(stored, 32)


def gnn_kernel(nc, x, src, dst, edge_attr_2, edge_attr_8, edge_type_8, edge_weight, L1_gnn_weight, L2_gnn_W1,
               L2_gnn_root1, L2_gnn_b1, L2_gnn_W2, L2_gnn_root2, L2_gnn_b2, L3_gnn_W_msg_tp, L3_gnn_W_msg_lin,
               L3_gnn_W_upd_tp, L3_gnn_W_upd_lin, out):
    def dram(name, shape, dt=F32):
        return nc.dram_tensor(name, shape, dt).ap()

    with ExitStack() as ctx:
        def sb(name, shape, dt=F32):
            return ctx.enter_context(nc.sbuf_tensor(name, shape, dt))

        c = Constants(sb)
        X, H, Y = (sb(n, [P, HI, D]) for n in "XHY")
        info = Info(sb, "dst")
        rec, grouped = dram("rec", (N_EDGES, WORDS)), dram("grouped", (G_TURNS * PLACES, WORDS))
        starts = dram("starts", (ROWS, T), I32)
        filled = dram("filled", (G_TURNS * PLACES + GROUPS * ROWS, D))
        type_filled = dram("type_filled", (N_EDGES + ROWS, T))
        type_sums = dram("type_sums", (N_EDGES, T))
        node_rows = dram("node_rows", (ROWS, D))
        constants(nc, c, x, X)
        clear_rows(nc, [grouped, filled[0:G_TURNS * PLACES, :]])

        with Scope(nc, "keys") as s:
            k = Keys(s.sb)
            low_rows = dram("low_rows", (COLS, P), BF16)
            digits(nc, c, src, dst, edge_weight, edge_type_8, k)
            count(nc, c, "dst", k.lo, k.hi, info)
            ordered = nc.values_load(k.ordered[0:1, 0:1], min_val=0, max_val=1)
            with nc.If(ordered == 1):
                copy_edges(nc, k, edge_attr_2, edge_attr_8, rec)
            with nc.Else():
                low_tiles(nc, c, k.lo, low_rows)
                sort_edges(nc, c, "dst", k.lo, k.hi, low_rows, info, WORDS,
                           [(WEIGHT, k.weight), (SOURCE, k.source), (DST_ROW, k.row), (DST_LO, k.lo), (DST_HI, k.hi),
                            (KIND, k.kind)], [(ATTR2, 2, edge_attr_2), (ATTR8, 8, edge_attr_8)], rec)

        with Scope(nc, "g") as gs:
            G = Places(gs.sb)
            with Scope(nc, "order") as s:
                runs = Runs(s.sb, "by_dst", info)
                source, groups = s.sb("source", [P, COLS]), s.sb("groups", [P, COLS])
                place = s.sb("place", [P, COLS], I32)
                counts = s.sb("counts", [P, HI, T])
                load_runs(nc, c, "runs", rec, runs, source)
                group_ids(nc, source, groups, place)
                type_counts(nc, c, "in_groups", runs, groups, type_sums, counts)
                group_places(nc, c, groups, counts, place, starts, G)
                place_edges(nc, place, rec, grouped)

            with Scope(nc, "l0") as s:
                weight = s.sb("weight", [P, G_COLS])
                goes_on = s.sb("goes_on", [P, G_COLS], BF16)
                first_node = s.sb("first_node", [P, G_TURNS], I32)
                load_places(nc, grouped, G, weight, goes_on, first_node)
                layernorm(nc, "ln0", X, H)
                powers(nc, c, G, weight, goes_on, first_node, starts, filled, node_rows, H, Y, 4)
            add_nodes(nc, "add0", X, [X, Y])

            layernorm(nc, "ln1", X, H)
            basis_rows = dram("L1_rows", (ROWS, 16 * D))
            project(nc, c, "basis", H, L1_gnn_weight.rearrange("u v i o -> i (u v) o"), 16 * D, table=basis_rows)
            contracted_sums(nc, c, "conv", G, basis_rows, grouped, node_rows, Y, 16, hats=True)
            add_nodes(nc, "add1", X, [X, Y])

            layernorm(nc, "ln2", X, H)
            with Scope(nc, "l2") as s:
                R = s.sb("R", [P, HI, D])
                runs = Runs(s.sb, "dst_runs", info)
                with Scope(nc, "l2_load") as t:
                    source, counts = t.sb("source", [P, COLS]), t.sb("counts", [P, HI, T])
                    load_runs(nc, c, "runs2", rec, runs, source)
                    type_counts(nc, c, "in_types", runs, runs.weight, type_sums, counts)
                    relation_norms(nc, c, runs, counts, type_filled)
                sums = dram("sums", (N_EDGES, D))
                typed_rows = dram("L2_rows", (ROWS, T * D))
                by_type = typed_rows.rearrange("n (r d) -> (n r) d", r=T)
                for n, (W, root, b) in enumerate(((L2_gnn_W1, L2_gnn_root1, L2_gnn_b1),
                                                  (L2_gnn_W2, L2_gnn_root2, L2_gnn_b2))):
                    project(nc, c, f"typed{n}", H, W.rearrange("r i o -> i r o"), T * D, table=typed_rows)
                    project(nc, c, f"root{n}", H, root, D, out=R)
                    weighted_sums(nc, c, f"relate{n}", runs, by_type, sums, Y)
                    add_nodes(nc, f"add2{n}", H, [Y, R], bias=b, relu=n == 0)
            add_log_softmax(nc, "softmax", X, H)

            layernorm(nc, "ln3", X, H)
            message_rows = dram("L3_rows", (ROWS, 8 * D))
            project(nc, c, "bilinear", H, L3_gnn_W_msg_tp, 8 * D, table=message_rows)
            contracted_sums(nc, c, "message", G, message_rows, grouped, node_rows, Y, 8, silu_scale=(8 * D) ** -0.5)
        with Scope(nc, "l3") as s:
            R = s.sb("R3", [P, HI, D])
            V = s.sb("V", [P, HI, D * D])
            project(nc, c, "mix", Y, L3_gnn_W_msg_lin, D, out=R)
            project(nc, c, "upd", H, L3_gnn_W_upd_tp, D * D, out=V)
            update(nc, "update", V, R, Y, D ** -0.5 / D)
            project(nc, c, "last", Y, L3_gnn_W_upd_lin, D, out=R)
            finish(nc, X, H, R, D ** -0.5, out)

_INS = ['x', 'src', 'dst', 'edge_attr_2', 'edge_attr_8', 'edge_type_8', 'edge_weight', 'node_vec1',
        'L1_gnn_weight', 'L2_gnn_W1', 'L2_gnn_root1', 'L2_gnn_b1', 'L2_gnn_W2', 'L2_gnn_root2', 'L2_gnn_b2',
        'L3_gnn_W_msg_tp', 'L3_gnn_W_msg_lin', 'L3_gnn_W_upd_tp', 'L3_gnn_W_upd_lin']


def kernel(**inputs):
    import numpy as _np
    import concourse.bacc as _bacc
    from concourse import mybir as _mybir
    from concourse.bass_utils import run_bass_kernel_spmd as _run

    nc = _bacc.Bacc("TRN2", target_bir_lowering=False, num_devices=1)
    arrays, args = {}, {}
    for name in _INS:
        if name == 'node_vec1':
            continue
        a = _np.ascontiguousarray(inputs[name])
        arrays[f"in_{name}"] = a
        args[name] = nc.dram_tensor(f"in_{name}", a.shape, _mybir.dt.from_np(a.dtype), kind="ExternalInput").ap()
    out = nc.dram_tensor("out_x", (N_NODES, D), F32, kind="ExternalOutput").ap()
    gnn_kernel(nc, out=out, **args)
    r = _run(nc, [arrays], core_ids=[0])
    return r.results[0]["out_x"]
```

```python
from contextlib import ExitStack

import concourse.bass as bass
from concourse import mybir

F32 = mybir.dt.float32
BF16 = mybir.dt.bfloat16
I32 = mybir.dt.int32
ALU = mybir.AluOpType
ACT = mybir.ActivationFunctionType
AX = mybir.AxisListType

P = 128
N_NODES = 12500
N_EDGES = 400000
D = 16
COLS = N_EDGES // P
HI = -(-N_NODES // P)
ROWS = P * HI
FULL = N_NODES // P
REST = N_NODES - FULL * P
TILES = 5
SLOTS = 5
TURN = TILES * SLOTS
TURNS = COLS // TURN
assert COLS == TURNS * TURN and P * COLS == N_EDGES and HI * TILES <= 512

WEIGHT, ATTR2, ATTR8, SOURCE, DST_ROW, DST_LO, DST_HI, KIND, WORDS = 0, 1, 3, 11, 12, 13, 14, 15, 16
WINDOW = 256
GROUPS = -(-N_NODES // (8 * WINDOW))
G_TURNS = TURNS + GROUPS
G_COLS = G_TURNS * TURN
PLACES = P * TURN
B_ALL = ROWS // 8
B_BLOCKS = -(-B_ALL // P)
BLANK = 5280


def loop(eng, turns, body):
    body(0, True)
    with eng.Fori(1, turns) as turn:
        body(turn, False)


class Line:

    def __init__(self, eng, sem):
        self.eng, self.sem, self.count = eng, sem, 0

    def do(self, ins):
        self.count += 1
        ins.then_inc(self.sem, 1)
        self.eng.wait_ge(self.sem, self.count)


class Scope:

    def __init__(self, nc, name):
        self.nc, self.name, self.stack, self.taken = nc, name, ExitStack(), []

    def __enter__(self):
        self.stack.__enter__()
        return self

    def __exit__(self, *e):
        self.stack.__exit__(*e)
        if self.taken:
            self.nc.clear_and_free_semaphores(self.taken)
            self.nc.all_engine_barrier()

    def sb(self, name, shape, dt=F32):
        return self.stack.enter_context(self.nc.sbuf_tensor(f"{self.name}_{name}", shape, dt))

    def ps(self, name, shape, dt=F32):
        return self.stack.enter_context(self.nc.psum_tensor(f"{self.name}_{name}", shape, dt))

    def sem(self, name):
        self.taken.append(self.nc.alloc_semaphore(f"{self.name}_{name}"))
        return self.taken[-1]

    def sems(self, name, n):
        return [self.sem(f"{name}{i}") for i in range(n)]

    def block(self):
        return self.stack.enter_context(self.nc.Block())


def constants(nc, c, x, X):
    with Scope(nc, "const") as s:
        iota_i = s.sb("iota_i", [P, WINDOW], I32)
        lane_i = s.sb("lane_i", [P, 1], I32)
        made, iotas, zeroed, x_in = s.sem("made"), s.sem("iotas"), s.sem("zeroed"), s.sem("x_in")
        block = s.block()

        @block.gpsimd
        def _(pool):
            pool.iota(iota_i[:], pattern=[[1, WINDOW]], base=0, channel_multiplier=0).then_inc(iotas, 1)
            pool.iota(lane_i[:], pattern=[[0, 1]], base=0, channel_multiplier=1).then_inc(iotas, 1)

        @block.vector
        def _(dve):
            line = Line(dve, made)
            dve.memset(X[:], 0.0).then_inc(zeroed, 1)
            dve.wait_ge(iotas, 2)
            line.do(dve.tensor_copy(c.free[:], iota_i[:, 0:P]))
            line.do(dve.tensor_copy(c.free_b[:], iota_i[:, 0:P]))
            line.do(dve.tensor_copy(c.wide[:], iota_i[:]))
            line.do(dve.tensor_copy(c.lane[:], lane_i[:]))
            line.do(dve.tensor_scalar(c.ident[:], c.free[:], c.lane[:, 0:1], None, ALU.is_equal))
            line.do(dve.tensor_copy(c.ident_b[:], c.ident[:]))
            line.do(dve.memset(c.ones[:], 1.0))
            line.do(dve.tensor_scalar(c.above[:], c.free[:], c.lane[:, 0:1], None, ALU.is_gt))
            line.do(dve.tensor_copy(c.above_b[:], c.above[:]))
            line.do(dve.tensor_scalar(c.down[:], c.free[:], -1.0, c.lane[:, 0:1], ALU.add, ALU.is_equal))
            line.do(dve.tensor_scalar(c.up[:], c.free[:], 1.0, c.lane[:, 0:1], ALU.add, ALU.is_equal))

        @block.sync
        def _(sp):
            sp.wait_ge(zeroed, 1)
            sp.dma_start(X[:, 0:FULL, :], x[0:FULL * P, :].rearrange("(h p) d -> p h d", p=P)).then_inc(x_in, 16)
            sp.dma_start(X[0:REST, FULL, :], x[FULL * P:N_NODES, :]).then_inc(x_in, 16)
            sp.wait_ge(x_in, 32)


def digits(nc, c, src, dst, weight, kind, k):
    with Scope(nc, "digits") as s:
        raw_s, raw_d = s.sb("raw_s", [P, COLS], I32), s.sb("raw_d", [P, COLS], I32)
        lo_i, hi_i = s.sb("lo_i", [P, COLS], I32), s.sb("hi_i", [P, COLS], I32)
        step = s.sb("step", [P, COLS])
        edge = s.sb("edge", [P, 4])
        least = s.sb("least", [1, 1])
        pe_out = s.ps("pe_out", [P, PIECE])
        loaded, line_sem, asked, shifted = (s.sem(n) for n in ("loaded", "line", "asked", "shifted"))
        block = s.block()

        def flat(dram):
            return dram.rearrange("(p c) -> p c", p=P)

        @block.sync
        def _(sp):
            sp.dma_start(raw_s[:], flat(src)).then_inc(loaded, 16)
            sp.dma_start(raw_d[:], flat(dst)).then_inc(loaded, 16)
            sp.dma_start(k.weight[:], flat(weight)).then_inc(loaded, 16)
            sp.dma_start(k.kind[:], flat(kind)).then_inc(loaded, 16)

        @block.vector
        def _(dve):
            line = Line(dve, line_sem)
            dve.wait_ge(loaded, 64)
            line.do(dve.tensor_scalar(k.source[:], raw_s[:], 1.0, None, ALU.add))
            line.do(dve.tensor_scalar(lo_i[:], raw_d[:], 127, None, ALU.bitwise_and))
            line.do(dve.tensor_scalar(hi_i[:], raw_d[:], 7, None, ALU.arith_shift_right))
            line.do(dve.tensor_copy(k.lo[:], lo_i[:]))
            line.do(dve.tensor_copy(k.hi[:], hi_i[:]))
            line.do(dve.scalar_tensor_tensor(out=k.row[:], in0=k.lo[:], scalar=float(HI), in1=k.hi[:],
                                             op0=ALU.mult, op1=ALU.add))
            line.do(dve.tensor_tensor(step[:, 0:COLS - 1], raw_d[:, 1:COLS], raw_d[:, 0:COLS - 1], ALU.subtract))
            dve.tensor_copy(edge[:, 0:1], raw_d[:, COLS - 1:COLS]).then_inc(asked, 1)
            dve.wait_ge(shifted, 1)
            line.do(dve.tensor_tensor(step[:, COLS - 1:COLS], raw_d[:, 0:1], pe_out[:, 0:1], ALU.subtract))
            line.do(dve.tensor_reduce(edge[:, 1:2], step[:], AX.X, ALU.min))
            dve.tensor_scalar(edge[:, 2:3], edge[:, 1:2], 0.0, None, ALU.is_ge).then_inc(asked, 1)
            dve.wait_ge(shifted, 2)
            line.do(dve.tensor_reduce(least[:], pe_out[0:1, P:2 * P], AX.X, ALU.min))
            line.do(dve.tensor_copy(k.ordered[:], least[:]))

        @block.tensor
        def _(pe):
            pe.wait_ge(asked, 1)
            pe.matmul(pe_out[:, 0:1], c.down[:], edge[:, 0:1], start=True, stop=True).then_inc(shifted, 1)
            pe.wait_ge(asked, 2)
            pe.transpose(pe_out[0:1, P:2 * P], edge[:, 2:3], c.ident[:]).then_inc(shifted, 1)


def one_hots(dve, c, lo_b, hi_b, cols, lo_hot, hi_hot, done):
    dve.tensor_tensor(lo_hot, lo_b[:, cols].unsqueeze(2).to_broadcast([P, TILES, P]),
                      c.free_b[:, 0:P].unsqueeze(1).to_broadcast([P, TILES, P]), ALU.is_equal)
    dve.tensor_tensor(hi_hot, hi_b[:, cols].unsqueeze(2).to_broadcast([P, TILES, HI]),
                      c.free_b[:, 0:HI].unsqueeze(1).to_broadcast([P, TILES, HI]), ALU.is_equal).then_inc(done, 1)


def count(nc, c, name, lo_b, hi_b, info, cleared_rows):
    with Scope(nc, f"count_{name}") as s:
        lo_hot = s.sb("lo_hot", [P, SLOTS, TILES, P], BF16)
        hi_hot = s.sb("hi_hot", [P, SLOTS, TILES, HI], BF16)
        zeros = s.sb("zeros", [P, P], BF16)
        blanks = s.sb("blanks", [P, BLANK])
        ones_row = s.sb("ones_row", [P, HI])
        run = s.sb("run", [P, HI])
        pc = s.ps("counts", [P, 512])
        po = s.ps("offsets", [P, 512])
        hot, counted, line_sem = s.sem("hot"), s.sem("counted"), s.sem("line")
        zeroed, totals, offs = s.sem("zeroed"), s.sem("totals"), s.sem("offs")
        blank, cleared = s.sem("blank"), s.sem("cleared")
        block = s.block()

        @block.sync
        def _(sp):
            sp.wait_ge(blank, 1)
            n = 0
            for dram in cleared_rows:
                flat = dram.rearrange("(p c) w -> p (c w)", p=P)
                for at in range(0, flat.shape[1], BLANK):
                    to = min(at + BLANK, flat.shape[1])
                    sp.dma_start(flat[:, at:to], blanks[:, 0:to - at]).then_inc(cleared, 16)
                    n += 1
            sp.wait_ge(cleared, 16 * n)

        @block.vector
        def _(dve):
            dve.memset(blanks[:], 0.0).then_inc(blank, 1)
            dve.memset(zeros[:], 0.0).then_inc(zeroed, 1)

            def body(turn, first):
                for k in range(SLOTS):
                    if not first:
                        dve.wait_ge(counted, (turn - 1) * SLOTS + k + 1)
                    one_hots(dve, c, lo_b, hi_b, bass.ds(turn * TURN + k * TILES, TILES),
                             lo_hot[:, k], hi_hot[:, k], hot)

            loop(dve, TURNS, body)
            line = Line(dve, line_sem)
            dve.wait_ge(counted, TURNS * SLOTS)
            dve.tensor_copy(info.cnt[:], pc[:, 0:HI]).then_inc(totals, 1)
            line.do(dve.memset(ones_row[:], 1.0))
            dve.wait_ge(offs, 1)
            line.do(dve.tensor_copy(run[:], po[:, P:P + HI]))
            line.do(dve.tensor_tensor_scan(info.start[:], ones_row[:], run[:], 0.0, ALU.mult, ALU.add))
            line.do(dve.tensor_tensor(info.start[:], info.start[:], run[:], ALU.subtract))
            line.do(dve.tensor_tensor(info.start[:], info.start[:], po[:, 0:HI], ALU.add))
            line.do(dve.tensor_tensor(run[:], info.start[:], info.cnt[:], ALU.add))
            line.do(dve.tensor_scalar(run[:], run[:], -1.0, 0.0, ALU.add, ALU.max))
            line.do(dve.tensor_copy(info.end_i[:], run[:]))
            line.do(dve.tensor_scalar(info.used[:], info.cnt[:], 1.0, None, ALU.min))

        @block.tensor
        def _(pe):
            pe.wait_ge(zeroed, 1)
            pe.matmul(pc[:, 0:HI], zeros[:], zeros[:, 0:HI], start=True, stop=True)

            def body(turn, first):
                for k in range(SLOTS):
                    pe.wait_ge(hot, turn * SLOTS + k + 1)
                    for j in range(TILES):
                        mm = pe.matmul(pc[:, 0:HI], lo_hot[:, k, j, :], hi_hot[:, k, j, :],
                                       start=False, stop=True, skip_group_check=True)
                    mm.then_inc(counted, 1)

            loop(pe, TURNS, body)
            pe.wait_ge(totals, 1)
            pe.matmul(po[:, 0:HI], c.above[:], info.cnt[:], start=True, stop=True)
            pe.matmul(po[:, P:P + HI], c.ones[:], info.cnt[:], start=True, stop=True).then_inc(offs, 1)


def low_tiles(nc, c, lo_b, low_rows):
    with Scope(nc, "lows") as s:
        turned = s.sb("turned", [125, 25, P], BF16)
        flipped = s.ps("flipped", [P, 2, 1024], BF16)
        flips, copied, stored = s.sem("flips"), s.sem("copied"), s.sem("stored")
        block = s.block()

        @block.sync
        def _(sp):
            sp.wait_ge(copied, 25)
            sp.dma_start(low_rows.rearrange("(j k) e -> j (k e)", k=25),
                         turned[:].rearrange("j k e -> j (k e)")).then_inc(stored, 16)
            sp.wait_ge(stored, 16)

        @block.tensor
        def _(pe):
            for k in range(25):
                if k >= 2:
                    pe.wait_ge(copied, k - 1)
                pe.transpose(flipped[0:125, k % 2, 0:P], lo_b[:, k::25], c.ident_b[:]).then_inc(flips, 1)

        @block.scalar
        def _(act):
            for k in range(25):
                act.wait_ge(flips, k + 1)
                act.copy(turned[:, k, :], flipped[0:125, k % 2, 0:P]).then_inc(copied, 1)


def copy_edges(nc, k, attr2, attr8, rec):
    with Scope(nc, "copy") as s:
        two, eight = s.sb("two", [P, SLOTS, TURN, 2]), s.sb("eight", [P, SLOTS, TURN, 8])
        record = s.sb("record", [P, SLOTS, TURN, WORDS])
        turns = COLS // (SLOTS * TURN)
        landed, stored = s.sems("landed", SLOTS), s.sems("stored", SLOTS)
        built_a, built_v = s.sem("built_a"), s.sem("built_v")
        block = s.block()
        out = rec.rearrange("(p c) w -> p (c w)", p=P)

        @block.sync
        def _(sp):
            def body(turn, first):
                for i in range(SLOTS):
                    n = turn * SLOTS + i
                    if not first:
                        sp.wait_ge(built_v, n - SLOTS + 1)
                    sp.dma_start(two[:, i].rearrange("p c w -> p (c w)"), attr2.rearrange("(p c) w -> p (c w)", p=P)
                                 [:, bass.ds(n * (TURN * 2), TURN * 2)]).then_inc(landed[i], 16)
                    sp.dma_start(eight[:, i].rearrange("p c w -> p (c w)"), attr8.rearrange("(p c) w -> p (c w)", p=P)
                                 [:, bass.ds(n * (TURN * 8), TURN * 8)]).then_inc(landed[i], 16)

            loop(sp, turns, body)

        @block.vector
        def _(dve):
            def body(turn, first):
                for i in range(SLOTS):
                    cols = bass.ds((turn * SLOTS + i) * TURN, TURN)
                    if not first:
                        dve.wait_ge(stored[i], turn * 16)
                    dve.wait_ge(landed[i], turn * 32 + 32)
                    dve.tensor_copy(record[:, i, :, ATTR2:ATTR2 + 2], two[:, i])
                    dve.tensor_copy(record[:, i, :, ATTR8:ATTR8 + 8], eight[:, i])
                    dve.tensor_copy(record[:, i, :, WEIGHT], k.weight[:, cols])
                    dve.tensor_copy(record[:, i, :, DST_ROW], k.row[:, cols]).then_inc(built_v, 1)

            loop(dve, turns, body)

        @block.scalar
        def _(act):
            def body(turn, first):
                for i in range(SLOTS):
                    n = turn * SLOTS + i
                    if not first:
                        act.wait_ge(stored[i], turn * 16)
                    for word, col in ((SOURCE, k.source), (DST_LO, k.lo), (DST_HI, k.hi), (KIND, k.kind)):
                        ins = act.copy(record[:, i, :, word], col[:, bass.ds(n * TURN, TURN)])
                    ins.then_inc(built_a, 1)
                    act.wait_ge(built_v, n + 1)
                    act.wait_ge(built_a, n + 1)
                    act.dma_start(out[:, bass.ds(n * (TURN * WORDS), TURN * WORDS)],
                                  record[:, i].rearrange("p c w -> p (c w)")).then_inc(stored[i], 16)

            loop(act, turns, body)

        def until_stored(eng):
            for i in range(SLOTS):
                eng.wait_ge(stored[i], 16 * turns)

        @block.gpsimd
        def _(pool):
            until_stored(pool)

        @block.tensor
        def _(pe):
            until_stored(pe)


def sort_edges(nc, c, name, lo_b, hi_b, low_rows, info, words, columns, parts, rec):
    with Scope(nc, f"sort_{name}") as s:
        lo_hot = s.sb("lo_hot", [P, SLOTS, TILES, P], BF16)
        hi_hot = s.sb("hi_hot", [P, SLOTS, TILES, HI], BF16)
        lo_row = s.sb("lo_row", [P, SLOTS, TILES * P], BF16)
        lo_hot_t = s.sb("lo_hot_t", [P, SLOTS, TILES, P])
        before = s.sb("before", [P, SLOTS, TILES, P], BF16)
        place = s.sb("place", [P, TILES, P])
        picked = s.sb("picked", [P, TILES, HI])
        pos_f = s.sb("pos_f", [P, TILES])
        pos_i = s.sb("pos_i", [P, SLOTS, TILES], I32)
        record = s.sb("record", [P, SLOTS, TILES, words])
        staged = [s.sb(f"staged{w}", [P, SLOTS, TILES * n]) for w, n, _ in parts]
        pcount = s.ps("pcount", [P, 512])
        pread = s.ps("pread", [P, SLOTS, 512])
        hot, rows_in, parts_in = s.sem("hot"), s.sems("rows_in", SLOTS), s.sems("parts_in", SLOTS)
        hot_t, counter, added = s.sem("hot_t"), s.sem("counter"), s.sem("added")
        read, pick, pos, posd = s.sem("read"), s.sem("pick"), s.sem("pos"), s.sem("posd")
        built, scattered, zeroed, gate = s.sem("built"), s.sems("scattered", SLOTS), s.sem("zeroed"), s.sem("gate")
        block = s.block()

        @block.sync
        def _(sp):
            def body(turn, first):
                for k in range(SLOTS):
                    if not first:
                        sp.wait_ge(hot_t, (turn - 1) * SLOTS + k + 1)
                        sp.wait_ge(built, (turn - 1) * SLOTS + k + 1)
                    src = low_rows[bass.ds(turn * TURN + k * TILES, TILES), :]
                    sp.dma_start(lo_row[:, k, :], src.rearrange("t e -> (t e)").unsqueeze(0).to_broadcast([P, TILES * P])
                                 ).then_inc(rows_in[k], 16)
                    for (w, n, dram), st in zip(parts, staged):
                        sp.dma_start(st[:, k, :], dram.rearrange("(p c) w -> p (c w)", p=P)
                                     [:, bass.ds((turn * TURN + k * TILES) * n, TILES * n)]).then_inc(parts_in[k], 16)

            loop(sp, TURNS, body)

        @block.vector
        def _(dve):
            dve.memset(picked[:], 0.0).then_inc(zeroed, 1)

            def prepare(turn, first, k):
                if not first:
                    dve.wait_ge(read, (turn - 1) * SLOTS + k + 1)
                cols = bass.ds(turn * TURN + k * TILES, TILES)
                one_hots(dve, c, lo_b, hi_b, cols, lo_hot[:, k], hi_hot[:, k], hot)
                dve.wait_ge(rows_in[k], turn * 16 + 16)
                dve.tensor_scalar(lo_hot_t[:, k].rearrange("p t e -> p (t e)"), lo_row[:, k, :],
                                  c.lane[:, 0:1], None, ALU.is_equal)
                for j in range(TILES):
                    ins = dve.scalar_tensor_tensor(
                        out=before[:, k, j, :], in0=lo_row[:, k, j * P:(j + 1) * P],
                        scalar=lo_b[:, bass.ds(turn * TURN + k * TILES + j, 1)], in1=c.above_b[:],
                        op0=ALU.is_equal, op1=ALU.mult)
                ins.then_inc(hot_t, 1)

            def finish(turn, first, k):
                n = turn * SLOTS + k
                dve.wait_ge(read, n + 1)
                dve.tensor_tensor(picked[:], pread[:, k, 0:TILES * HI].rearrange("p (t h) -> p t h", t=TILES),
                                  hi_hot[:, k], ALU.mult).then_inc(pick, 1)
                dve.wait_ge(pick, n + 1)
                dve.tensor_reduce(pos_f[:], picked[:], AX.X, ALU.add).then_inc(pos, 1)
                dve.wait_ge(pos, n + 1)
                if not first:
                    dve.wait_ge(scattered[k], turn * (16 * TILES))
                dve.tensor_copy(pos_i[:, k, :], pos_f[:]).then_inc(posd, 1)

            def body(turn, first):
                for k in range(SLOTS):
                    prepare(turn, first, k)
                    if k >= 1:
                        finish(turn, first, k - 1)
                finish(turn, first, SLOTS - 1)

            loop(dve, TURNS, body)

        @block.tensor
        def _(pe):
            pe.matmul(pcount[:, 0:HI], c.ident[:], info.start[:], start=True, stop=True).then_inc(added, 1)

            def body(turn, first):
                for k in range(SLOTS):
                    pe.wait_ge(hot_t, turn * SLOTS + k + 1)
                    if not first:
                        pe.wait_ge(pick, (turn - 1) * SLOTS + k + 1)
                    for j in range(TILES):
                        tile = turn * TURN + k * TILES + j
                        pe.wait_ge(counter, tile + 1)
                        pe.matmul(pcount[:, 0:HI], lo_hot[:, k, j, :], hi_hot[:, k, j, :],
                                  start=False, stop=True, skip_group_check=True).then_inc(added, 1)
                        out = pread[:, k, j * HI:(j + 1) * HI]
                        pe.matmul(out, before[:, k, j, :], hi_hot[:, k, j, :], start=True, stop=False,
                                  skip_group_check=True)
                        mm = pe.matmul(out, lo_hot_t[:, k, j, :], place[:, j, 0:HI], start=False, stop=True,
                                       skip_group_check=True)
                    mm.then_inc(read, 1)

            loop(pe, TURNS, body)

        @block.scalar
        def _(act):
            act.wait_ge(zeroed, 1)
            act.wait_ge(added, 1)
            act.copy(place[:, 0, 0:HI], pcount[:, 0:HI]).then_inc(counter, 1)

            def build(turn, first, k):
                if not first:
                    act.wait_ge(scattered[k], turn * (16 * TILES))
                cols = bass.ds(turn * TURN + k * TILES, TILES)
                if parts:
                    act.wait_ge(parts_in[k], (turn + 1) * (16 * len(parts)))
                for (w, n, _), st in zip(parts, staged):
                    act.copy(record[:, k, :, w:w + n], st[:, k, :].rearrange("p (t n) -> p t n", n=n))
                for w, col in columns:
                    ins = act.copy(record[:, k, :, w], col[:, cols])
                ins.then_inc(built, 1)

            def body(turn, first):
                for k in range(SLOTS):
                    build(turn, first, k)
                    for j in range(TILES):
                        act.wait_ge(added, turn * TURN + k * TILES + j + 2)
                        act.copy(place[:, (j + 1) % TILES, 0:HI], pcount[:, 0:HI]).then_inc(counter, 1)

            loop(act, TURNS, body)

        @block.gpsimd
        def _(pool):
            def body(turn, first):
                for k in range(SLOTS):
                    pool.wait_ge(posd, turn * SLOTS + k + 1)
                    pool.sem_inc(gate, 1)
                    pool.wait_ge(built, turn * SLOTS + k + 1)
                    pool.sem_inc(gate, 1)
                    for j in range(TILES):
                        pool.indirect_dma_start(rec, bass.IndirectOffsetOnAxis(pos_i[:, k, j:j + 1], 0),
                                                record[:, k, j, :], None).then_inc(scattered[k], 16)

            loop(pool, TURNS, body)
            for k in range(SLOTS):
                pool.wait_ge(scattered[k], TURNS * 16 * TILES)


class Info:

    def __init__(self, sb, name):
        self.cnt, self.start, self.used = (sb(f"{name}_{n}", [P, HI]) for n in ("cnt", "start", "used"))
        self.end_i = sb(f"{name}_end", [P, HI], I32)


class Keys:

    def __init__(self, sb):
        self.weight, self.source, self.row = (sb(f"key_{n}", [P, COLS]) for n in ("weight", "source", "row"))
        self.lo, self.hi = sb("key_lo", [P, COLS], BF16), sb("key_hi", [P, COLS], BF16)
        self.kind = sb("key_kind", [P, COLS], I32)
        self.ordered = sb("ordered", [1, 1], I32)


class Constants:
    def __init__(self, sb):
        self.free, self.ident, self.above, self.down, self.up, self.ones = (
            sb(n, [P, P]) for n in ("free", "ident", "above", "down", "up", "ones"))
        self.free_b, self.ident_b, self.above_b = (sb(n, [P, P], BF16) for n in ("free_b", "ident_b", "above_b"))
        self.lane = sb("lane", [P, 1])
        self.wide = sb("wide", [P, WINDOW])


COLS_SLOT = 25
PASS_TURNS = COLS // (COLS_SLOT * SLOTS)
PAD = COLS_SLOT * SLOTS
BLOCK = 7
BLOCKS = HI // BLOCK
PIECE = 512
assert BLOCKS * BLOCK == HI and PASS_TURNS * COLS_SLOT * SLOTS == COLS


class Runs:

    def __init__(self, sb, name, info):
        self.info = info
        self.index = sb(f"{name}_index", [P, COLS + PAD], I32)
        self.weight = sb(f"{name}_weight", [P, COLS])
        self.goes_on = sb(f"{name}_goes_on", [P, COLS])
        self.first_lo = sb(f"{name}_first_lo", [P, P])
        self.first_hi = sb(f"{name}_first_hi", [P, HI])
        self.first_row = sb(f"{name}_first_row", [P, 1], I32)
        self.through = sb(f"{name}_through", [D, P])


def load_runs(nc, c, name, rec, runs, source):
    with Scope(nc, name) as s:
        recs = s.sb("recs", [P, SLOTS, COLS_SLOT, WORDS])
        row = s.sb("row", [P, COLS])
        ids, lo, hi = (s.sb(n, [P, COLS], I32) for n in ("ids", "lo", "hi"))
        firsts = s.sb("firsts", [P, WORDS])
        tmp = s.sb("tmp", [P, 8])
        alive = s.sb("alive", [P, D])
        psh = s.ps("shifted", [P, 512])
        landed, taken_a, taken_v = s.sems("landed", SLOTS), s.sem("taken_a"), s.sem("taken_v")
        first_in, line_sem, ends, shifted = s.sem("first_in"), s.sem("line"), s.sem("ends"), s.sem("shifted")
        block = s.block()
        view = rec.rearrange("(p c) w -> p (c w)", p=P)

        @block.sync
        def _(sp):
            sp.dma_start(firsts[:], view[:, 0:WORDS]).then_inc(first_in, 16)

            def body(turn, first):
                for k in range(SLOTS):
                    if not first:
                        sp.wait_ge(taken_a, (turn - 1) * SLOTS + k + 1)
                        sp.wait_ge(taken_v, (turn - 1) * SLOTS + k + 1)
                    at = (turn * SLOTS + k) * COLS_SLOT
                    sp.dma_start(recs[:, k].rearrange("p c w -> p (c w)"),
                                 view[:, bass.ds(at * WORDS, COLS_SLOT * WORDS)]).then_inc(landed[k], 16)

            loop(sp, PASS_TURNS, body)

        @block.scalar
        def _(act):
            def body(turn, first):
                for k in range(SLOTS):
                    cols = bass.ds((turn * SLOTS + k) * COLS_SLOT, COLS_SLOT)
                    act.wait_ge(landed[k], turn * 16 + 16)
                    act.copy(runs.weight[:, cols], recs[:, k, :, KIND]).then_inc(taken_a, 1)

            loop(act, PASS_TURNS, body)

        @block.vector
        def _(dve):
            def body(turn, first):
                for k in range(SLOTS):
                    cols = bass.ds((turn * SLOTS + k) * COLS_SLOT, COLS_SLOT)
                    dve.wait_ge(landed[k], turn * 16 + 16)
                    dve.tensor_scalar(source[:, cols], recs[:, k, :, SOURCE], -1.0, None, ALU.add)
                    dve.tensor_copy(row[:, cols], recs[:, k, :, DST_ROW]).then_inc(taken_v, 1)

            loop(dve, PASS_TURNS, body)
            line = Line(dve, line_sem)
            dve.wait_ge(taken_v, PASS_TURNS * SLOTS)
            dve.wait_ge(taken_a, PASS_TURNS * SLOTS)
            line.do(dve.tensor_copy(ids[:], source[:]))
            line.do(dve.tensor_scalar(lo[:], ids[:], 127, None, ALU.bitwise_and))
            line.do(dve.tensor_scalar(hi[:], ids[:], 7, None, ALU.arith_shift_right))
            line.do(dve.scalar_tensor_tensor(out=ids[:], in0=lo[:], scalar=float(HI), in1=hi[:],
                                             op0=ALU.mult, op1=ALU.add))
            line.do(dve.scalar_tensor_tensor(out=runs.index[:, 0:COLS], in0=ids[:], scalar=8.0, in1=runs.weight[:],
                                             op0=ALU.mult, op1=ALU.add))
            line.do(dve.tensor_copy(runs.index[:, COLS:COLS + PAD], runs.index[:, 0:PAD]))
            line.do(dve.tensor_tensor(runs.goes_on[:, 1:COLS], row[:, 1:COLS], row[:, 0:COLS - 1], ALU.is_equal))
            dve.tensor_scalar(tmp[:, 0:1], row[:, COLS - 1:COLS], 1.0, None, ALU.add).then_inc(ends, 1)
            line.do(dve.tensor_scalar(tmp[:, 1:2], row[:, 0:1], 1.0, None, ALU.add))
            dve.wait_ge(shifted, 1)
            line.do(dve.tensor_tensor(runs.goes_on[:, 0:1], tmp[:, 1:2], psh[:, 0:1], ALU.is_equal))
            dve.tensor_copy(tmp[:, 2:3], runs.goes_on[:, 0:1]).then_inc(ends, 1)
            line.do(dve.tensor_reduce(tmp[:, 3:4], runs.goes_on[:], AX.X, ALU.min))
            dve.tensor_copy(alive[:], tmp[:, 3:4].to_broadcast([P, D])).then_inc(ends, 1)
            dve.wait_ge(shifted, 3)
            line.do(dve.tensor_copy(runs.through[:], psh[0:D, 128:256]))
            line.do(dve.tensor_tensor(tmp[:, 4:5], tmp[:, 3:4], psh[:, 1:2], ALU.mult))
            line.do(dve.tensor_scalar(tmp[:, 5:6], tmp[:, 4:5], -1.0, 1.0, ALU.mult, ALU.add))
            line.do(dve.tensor_tensor(tmp[:, 6:7], tmp[:, 5:6], tmp[:, 2:3], ALU.mult))
            dve.wait_ge(first_in, 16)
            line.do(dve.tensor_copy(runs.first_row[:], firsts[:, DST_ROW:DST_ROW + 1]))
            line.do(dve.tensor_scalar(runs.first_lo[:], c.free[:], firsts[:, DST_LO:DST_LO + 1], None, ALU.is_equal))
            line.do(dve.tensor_scalar(runs.first_hi[:], c.free[:, 0:HI], firsts[:, DST_HI:DST_HI + 1], tmp[:, 6:7],
                                      ALU.is_equal, ALU.mult))

        @block.tensor
        def _(pe):
            pe.wait_ge(ends, 1)
            pe.matmul(psh[:, 0:1], c.down[:], tmp[:, 0:1], start=True, stop=True).then_inc(shifted, 1)
            pe.wait_ge(ends, 2)
            pe.matmul(psh[:, 1:2], c.up[:], tmp[:, 2:3], start=True, stop=True).then_inc(shifted, 1)
            pe.wait_ge(ends, 3)
            pe.matmul(psh[0:D, 128:256], alive[:], c.ident[:], start=True, stop=True).then_inc(shifted, 1)


class Carry:

    def __init__(self, s, width):
        self.width = width
        self.last = s.sb("last", [P, width])
        self.rows = s.sb("rows", [width, P + 1])
        self.spread = s.sb("spread", [P, HI, width])
        self.pt = s.ps("last_rows", [P, 512])
        self.fix = s.ps("fix", [P, 4 * PIECE])
        self.last_done, self.turned, self.scanned, self.back, self.laid, self.fixed = (
            s.sem(n) for n in ("last_done", "turned", "carry_scanned", "back", "laid", "fixed"))

    def tensor(self, pe, c, runs):
        w = self.width
        pe.wait_ge(self.last_done, 1)
        pe.transpose(self.pt[0:w, 0:P], self.last[:], c.ident[:]).then_inc(self.turned, 1)
        pe.wait_ge(self.scanned, 1)
        pe.matmul(self.pt[:, P:P + w], self.rows[:, 0:P], c.ident[0:w, 0:w], start=True, stop=True
                  ).then_inc(self.back, 1)
        pe.wait_ge(self.laid, 1)
        flat = self.spread[:].rearrange("p h f -> p (h f)")
        for at in range(0, HI * w, PIECE):
            to = min(at + PIECE, HI * w)
            mm = pe.matmul(self.fix[:, at:to], runs.first_lo[:], flat[:, at:to], start=True, stop=True)
        mm.then_inc(self.fixed, 1)

    def vector(self, dve, runs):
        w = self.width
        dve.wait_ge(self.turned, 1)
        dve.tensor_tensor_scan(self.rows[:, 1:P + 1], runs.through[0:w, :], self.pt[0:w, 0:P], 0.0,
                               ALU.mult, ALU.add).then_inc(self.scanned, 1)
        dve.wait_ge(self.back, 1)
        dve.tensor_tensor(self.spread[:], runs.first_hi[:].unsqueeze(2).to_broadcast([P, HI, w]),
                          self.pt[:, P:P + w].unsqueeze(1).to_broadcast([P, HI, w]), ALU.mult
                          ).then_inc(self.laid, 1)

    def add(self, dve, runs, ends, out, masked, done):
        w = self.width
        dve.tensor_tensor(out, ends, runs.info.used[:].unsqueeze(2).to_broadcast([P, HI, w]), ALU.mult
                          ).then_inc(masked, 1)
        dve.wait_ge(masked, 1)
        dve.wait_ge(self.fixed, 1)
        dve.tensor_tensor(out, out, self.fix[:, 0:HI * w].rearrange("p (h f) -> p h f", f=w), ALU.add
                          ).then_inc(done, 1)


def gather_ends(pool, runs, sums, ends, ends_in):
    for h in range(HI):
        pool.indirect_dma_start(ends[:, h, :], None, sums,
                                bass.IndirectOffsetOnAxis(runs.info.end_i[:, h:h + 1], 0)).then_inc(ends_in, 16)


def weighted_sums(nc, c, name, runs, table, sums, Y, inverses=None):
    with Scope(nc, name) as s:
        picked = s.sb("picked", [P, SLOTS, COLS_SLOT, D])
        staged = s.sb("staged", [P, SLOTS, COLS_SLOT], I32)
        message = s.sb("message", [P, COLS_SLOT, D])
        running = s.sb("running", [P, SLOTS, COLS_SLOT, D])
        ends = s.sb("ends", [P, HI, D])
        carry = Carry(s, D)
        staged_done, gathered = s.sems("staged_done", SLOTS), s.sems("gathered", SLOTS)
        weighed, scanned, kept, stored, free = (s.sem(n) for n in ("weighed", "scanned", "kept", "stored", "free"))
        ends_in, masked, y_done, gate = (s.sem(n) for n in ("ends_in", "masked", "y_done", "gate"))
        norms = Norms(s, inverses, runs) if inverses is not None else None
        block = s.block()
        slots = PASS_TURNS * SLOTS
        flat = sums.rearrange("(p c) f -> p (c f)", p=P)

        @block.sync
        def _(sp):
            sp.sem_inc(free, SLOTS)
            with sp.Fori(0, PASS_TURNS) as turn:
                for k in range(SLOTS):
                    n = turn * SLOTS + k
                    sp.wait_ge(scanned, n + 1)
                    sp.dma_start(flat[:, bass.ds(n * (COLS_SLOT * D), COLS_SLOT * D)],
                                 running[:, k].rearrange("p c f -> p (c f)")).then_inc(stored, 16)
                    sp.wait_ge(stored, n * 16 + 16)
                    sp.sem_inc(free, 1)

        if norms is not None:
            @block.scalar
            def _(act):
                norms.scalar(act)

        @block.gpsimd
        def _(pool):
            if norms is not None:
                norms.first(pool)
            with pool.Fori(0, PASS_TURNS) as turn:
                for k in range(SLOTS):
                    pool.wait_ge(staged_done[k], turn + 1)
                    pool.sem_inc(gate, 1)
                    for j in range(COLS_SLOT):
                        pool.indirect_dma_start(picked[:, k, j, :], None, table,
                                                bass.IndirectOffsetOnAxis(staged[:, k, j:j + 1], 0)
                                                ).then_inc(gathered[k], 16)
            pool.wait_ge(stored, 16 * slots)
            pool.sem_inc(gate, 1)
            gather_ends(pool, runs, sums, ends, ends_in)

        @block.vector
        def _(dve):
            dve.memset(carry.rows[:], 0.0)
            for k in range(SLOTS):
                dve.tensor_copy(staged[:, k, :], runs.index[:, k * COLS_SLOT:(k + 1) * COLS_SLOT]
                                ).then_inc(staged_done[k], 1)
            if norms is not None:
                norms.begin(dve)
            dve.memset(carry.last[:], 0.0).then_inc(kept, 1)
            with dve.Fori(0, PASS_TURNS) as turn:
                for k in range(SLOTS):
                    n = turn * SLOTS + k
                    at = n * COLS_SLOT
                    if norms is not None:
                        norms.slot(dve, c, turn, k)
                    dve.wait_ge(gathered[k], (turn + 1) * (16 * COLS_SLOT))
                    dve.tensor_tensor(message[:], picked[:, k],
                                      runs.weight[:, bass.ds(at, COLS_SLOT)].unsqueeze(2)
                                      .to_broadcast([P, COLS_SLOT, D]), ALU.mult).then_inc(weighed, 1)
                    dve.wait_ge(weighed, n + 1)
                    dve.tensor_copy(staged[:, k, :], runs.index[:, bass.ds(at + PAD, COLS_SLOT)]
                                    ).then_inc(staged_done[k], 1)
                    dve.wait_ge(kept, n + 1)
                    dve.wait_ge(free, n + 1)
                    for f in range(D):
                        ins = dve.tensor_tensor_scan(running[:, k, :, f], runs.goes_on[:, bass.ds(at, COLS_SLOT)],
                                                     message[:, :, f], carry.last[:, f:f + 1], ALU.mult, ALU.add)
                    ins.then_inc(scanned, 1)
                    dve.wait_ge(scanned, n + 1)
                    dve.tensor_copy(carry.last[:], running[:, k, COLS_SLOT - 1, :]).then_inc(kept, 1)
            dve.wait_ge(kept, slots + 1)
            dve.sem_inc(carry.last_done, 1)
            carry.vector(dve, runs)
            dve.wait_ge(ends_in, 16 * HI)
            carry.add(dve, runs, ends[:], Y[:], masked, y_done)
            dve.wait_ge(y_done, 1)

        @block.tensor
        def _(pe):
            carry.tensor(pe, c, runs)


T = 8


class Counting:

    def __init__(self, s, runs, kinds, sums):
        self.runs, self.kinds, self.sums = runs, kinds, sums
        self.hot = s.sb("kind_hot", [P, COLS_SLOT, T])
        self.running = s.sb("counts_so_far", [P, SLOTS, COLS_SLOT, T])
        self.ends = s.sb("ends", [P, HI, T])
        self.carry = Carry(s, T)
        self.hotted, self.scanned, self.kept, self.stored, self.free, self.ends_in, self.masked, self.counted, \
            self.ends_gate = (s.sem(f"counting_{n}") for n in ("hotted", "scanned", "kept", "stored", "free", "ends_in", "masked",
                                                 "counted", "ends_gate"))

    def scalar(self, act):
        flat = self.sums.rearrange("(p c) f -> p (c f)", p=P)
        act.sem_inc(self.free, SLOTS)
        with act.Fori(0, PASS_TURNS) as turn:
            for k in range(SLOTS):
                n = turn * SLOTS + k
                act.wait_ge(self.scanned, n + 1)
                act.dma_start(flat[:, bass.ds(n * (COLS_SLOT * T), COLS_SLOT * T)],
                              self.running[:, k].rearrange("p c f -> p (c f)")).then_inc(self.stored, 16)
                act.wait_ge(self.stored, n * 16 + 16)
                act.sem_inc(self.free, 1)

    def gather(self, pool):
        pool.wait_ge(self.stored, 16 * PASS_TURNS * SLOTS)
        pool.sem_inc(self.ends_gate, 1)
        gather_ends(pool, self.runs, self.sums, self.ends, self.ends_in)

    def begin(self, dve):
        dve.memset(self.carry.rows[:], 0.0)
        dve.memset(self.carry.last[:], 0.0).then_inc(self.kept, 1)

    def slot(self, dve, c, turn, k):
        n = turn * SLOTS + k
        cols = bass.ds(n * COLS_SLOT, COLS_SLOT)
        dve.tensor_tensor(self.hot[:], self.kinds[:, cols].unsqueeze(2).to_broadcast([P, COLS_SLOT, T]),
                          c.free[:, 0:T].unsqueeze(1).to_broadcast([P, COLS_SLOT, T]), ALU.is_equal
                          ).then_inc(self.hotted, 1)
        dve.wait_ge(self.hotted, n + 1)
        dve.wait_ge(self.kept, n + 1)
        dve.wait_ge(self.free, n + 1)
        for f in range(T):
            ins = dve.tensor_tensor_scan(self.running[:, k, :, f], self.runs.goes_on[:, cols], self.hot[:, :, f],
                                         self.carry.last[:, f:f + 1], ALU.mult, ALU.add)
        ins.then_inc(self.scanned, 1)
        dve.wait_ge(self.scanned, n + 1)
        dve.tensor_copy(self.carry.last[:], self.running[:, k, COLS_SLOT - 1, :]).then_inc(self.kept, 1)

    def last(self, dve):
        dve.wait_ge(self.kept, PASS_TURNS * SLOTS + 1)
        dve.sem_inc(self.carry.last_done, 1)
        self.carry.vector(dve, self.runs)

    def end(self, dve, counts):
        dve.wait_ge(self.ends_in, 16 * HI)
        self.carry.add(dve, self.runs, self.ends[:], counts[:], self.masked, self.counted)
        dve.wait_ge(self.counted, 1)


class Inverses:

    def __init__(self, nc, sb):
        self.filled = nc.dram_tensor("type_filled", (N_EDGES + ROWS, T), F32).ap()
        self.rows = nc.dram_tensor("inverse_rows", (ROWS, T), F32).ap()
        self.values = sb("inverses", [P, HI, T])
        self.to = sb("inverses_to", [P, HI], I32)

    def make(self, nc, c, runs, counts):
        with Scope(nc, "inverses") as s:
            to_f = s.sb("to_f", [P, 3, HI])
            line_sem, inverted, out = s.sem("line"), s.sem("inverted"), s.sem("out")
            block = s.block()

            @block.scalar
            def _(act):
                act.wait_ge(inverted, 1)
                act.dma_start(self.rows.rearrange("(p h) t -> p (h t)", p=P),
                              self.values[:].rearrange("p h t -> p (h t)")).then_inc(out, 16)
                act.wait_ge(out, 16)

            @block.vector
            def _(dve):
                line = Line(dve, line_sem)
                line.do(dve.tensor_scalar(to_f[:, 0, :], c.lane[:].to_broadcast([P, HI]), float(HI), float(N_EDGES),
                                          ALU.mult, ALU.add))
                line.do(dve.tensor_tensor(to_f[:, 1, :], to_f[:, 0, :], c.free[:, 0:HI], ALU.add))
                line.do(dve.tensor_tensor(to_f[:, 2, :], runs.info.start[:], to_f[:, 1, :], ALU.subtract))
                line.do(dve.tensor_tensor(to_f[:, 0, :], to_f[:, 2, :], runs.info.used[:], ALU.mult))
                line.do(dve.tensor_tensor(self.to[:], to_f[:, 0, :], to_f[:, 1, :], ALU.add))
                line.do(dve.tensor_scalar(self.values[:], counts[:], 1.0, None, ALU.max))
                dve.reciprocal(self.values[:], self.values[:]).then_inc(inverted, 1)

    def spread(self, pool, spread_out):
        for h in range(HI):
            pool.indirect_dma_start(self.filled, bass.IndirectOffsetOnAxis(self.to[:, h:h + 1], 0),
                                    self.values[:, h, :], None).then_inc(spread_out, 16)
        pool.wait_ge(spread_out, 16 * HI)


class Norms:

    def __init__(self, s, inverses, runs):
        self.inverses, self.runs = inverses, runs
        self.given = s.sb("given", [P, SLOTS, COLS_SLOT, T])
        self.along, self.hot, self.own = (s.sb(n, [P, COLS_SLOT, T]) for n in ("along", "hot", "own"))
        self.norm, self.last = s.sb("norm", [P, COLS_SLOT]), s.sb("inverse_last", [P, T])
        self.landed = s.sems("norm_landed", SLOTS)
        self.first_in, self.scanned, self.kept, self.hotted, self.used, self.written = (
            s.sem(f"norm_{n}") for n in ("first_in", "scanned", "kept", "hotted", "used", "written"))

    def scalar(self, act):
        flat = self.inverses.filled[0:N_EDGES, :].rearrange("(p c) f -> p (c f)", p=P)

        def body(turn, first):
            for k in range(SLOTS):
                n = turn * SLOTS + k
                if not first:
                    act.wait_ge(self.scanned, (turn - 1) * SLOTS + k + 1)
                act.dma_start(self.given[:, k].rearrange("p c f -> p (c f)"),
                              flat[:, bass.ds(n * (COLS_SLOT * T), COLS_SLOT * T)]).then_inc(self.landed[k], 16)

        loop(act, PASS_TURNS, body)

    def first(self, pool):
        pool.indirect_dma_start(self.last[:], None, self.inverses.rows,
                                bass.IndirectOffsetOnAxis(self.runs.first_row[:, 0:1], 0)).then_inc(self.first_in, 16)

    def begin(self, dve):
        dve.wait_ge(self.first_in, 16)
        dve.sem_inc(self.kept, 1)

    def slot(self, dve, c, turn, k):
        n = turn * SLOTS + k
        cols = bass.ds(n * COLS_SLOT, COLS_SLOT)
        weight = self.runs.weight
        dve.wait_ge(self.landed[k], turn * 16 + 16)
        dve.tensor_tensor(self.hot[:], weight[:, cols].unsqueeze(2).to_broadcast([P, COLS_SLOT, T]),
                          c.free[:, 0:T].unsqueeze(1).to_broadcast([P, COLS_SLOT, T]), ALU.is_equal)
        dve.wait_ge(self.kept, n + 1)
        for f in range(T):
            ins = dve.tensor_tensor_scan(self.along[:, :, f], self.runs.goes_on[:, cols], self.given[:, k, :, f],
                                         self.last[:, f:f + 1], ALU.mult, ALU.add)
        ins.then_inc(self.scanned, 1)
        dve.wait_ge(self.scanned, n + 1)
        dve.tensor_copy(self.last[:], self.along[:, COLS_SLOT - 1, :]).then_inc(self.kept, 1)
        dve.tensor_tensor(self.own[:], self.along[:], self.hot[:], ALU.mult).then_inc(self.hotted, 1)
        dve.wait_ge(self.hotted, n + 1)
        dve.tensor_reduce(self.norm[:], self.own[:], AX.X, ALU.add).then_inc(self.used, 1)
        dve.wait_ge(self.used, n + 1)
        dve.tensor_scalar(weight[:, cols], self.norm[:], 1.0, None, ALU.mult).then_inc(self.written, 1)
        dve.wait_ge(self.written, n + 1)


class Places:

    def __init__(self, sb):
        self.group = sb("group", [1, G_TURNS], I32)
        self.index = sb("g_index", [P, G_COLS + TURN], I32)
        self.b = sb("g_b", [P, G_COLS], BF16)
        self.a = sb("g_a", [P, G_COLS], BF16)


def group_places(nc, c, runs, groups, sums, counts, place, starts, G):
    with Scope(nc, "places") as s:
        hot, running, part = (s.sb(n, [P, COLS]) for n in ("hot", "running", "part"))
        pos, ones = s.sb("pos", [P, COLS]), s.sb("ones", [P, HI])
        totals, sizes, turns, before, first, low = (s.sb(n, [P, T]) for n in ("totals", "sizes", "turns", "before", "first", "low"))
        turn_id, ended, group = s.sb("turn_id", [1, G_TURNS]), s.sb("ended", [1, G_TURNS]), s.sb("group", [1, G_TURNS])
        turn_i = s.sb("turn_i", [P, G_TURNS], I32)
        turns_i = s.sb("turns_i", [P, T], I32)
        run, lower = s.sb("run", [P, HI]), s.sb("lower", [P, HI])
        spare, start, used = s.sb("spare", [P, HI]), s.sb("start", [P, HI]), s.sb("used", [P, HI])
        node_start = s.sb("node_start", [P, HI, T], I32)
        p_sum = s.ps("p_sum", [P, PIECE])
        p_cnt = s.ps("p_cnt", [P, PIECE])
        line_sem, iotas, counted, summed, ready, looked, stored = (
            s.sem(n) for n in ("line", "iotas", "counted", "summed", "ready", "looked", "stored"))
        counting = Counting(s, runs, groups, sums)
        block = s.block()

        @block.scalar
        def _(act):
            counting.scalar(act)

        @block.gpsimd
        def _(pool):
            pool.iota(turn_i[:], pattern=[[1, G_TURNS]], base=0, channel_multiplier=0).then_inc(iotas, 1)
            counting.gather(pool)

        @block.vector
        def _(dve):
            counting.begin(dve)
            with dve.Fori(0, PASS_TURNS) as turn:
                for k in range(SLOTS):
                    counting.slot(dve, c, turn, k)
            counting.last(dve)
            line = Line(dve, line_sem)
            line.do(dve.memset(ones[:], 1.0))
            line.do(dve.memset(pos[:], 0.0))
            line.do(dve.memset(totals[:], 0.0))
            for g in range(GROUPS):
                line.do(dve.tensor_scalar(hot[:], groups[:], float(g), None, ALU.is_equal))
                line.do(dve.tensor_tensor_scan(running[:], ones[:, 0:1].to_broadcast([P, COLS]), hot[:], 0.0, ALU.mult, ALU.add))
                line.do(dve.tensor_copy(totals[:, g:g + 1], running[:, COLS - 1:COLS]))
                line.do(dve.scalar_tensor_tensor(out=part[:], in0=running[:], scalar=-1.0, in1=hot[:],
                                                 op0=ALU.add, op1=ALU.mult))
                line.do(dve.tensor_tensor(pos[:], pos[:], part[:], ALU.add))
            dve.sem_inc(counted, 1)
            dve.wait_ge(summed, 1)
            line.do(dve.tensor_copy(sizes[:], p_sum[:, 0:T]))
            line.do(dve.tensor_scalar(turns_i[:], sizes[:], 1.0 / PLACES, None, ALU.mult))
            line.do(dve.tensor_copy(turns[:], turns_i[:]))
            line.do(dve.tensor_scalar(turns[:], turns[:], -1.0, 0.0, ALU.add, ALU.max))
            for _ in range(3):
                line.do(dve.scalar_tensor_tensor(out=low[:], in0=turns[:], scalar=float(PLACES), in1=sizes[:],
                                                 op0=ALU.mult, op1=ALU.is_lt))
                line.do(dve.tensor_tensor(turns[:], turns[:], low[:], ALU.add))
            line.do(dve.tensor_tensor_scan(before[:], ones[:, 0:T], turns[:], 0.0, ALU.mult, ALU.add))
            line.do(dve.tensor_tensor(first[:], before[:], turns[:], ALU.subtract))
            line.do(dve.tensor_scalar(first[:], first[:], float(PLACES), None, ALU.mult))
            line.do(dve.tensor_tensor(low[:], first[:], p_sum[:, P:P + T], ALU.add))
            for g in range(GROUPS):
                line.do(dve.tensor_scalar(part[:], groups[:], float(g), low[:, g:g + 1], ALU.is_equal, ALU.mult))
                line.do(dve.tensor_tensor(pos[:], pos[:], part[:], ALU.add))
            line.do(dve.tensor_copy(place[:, 0:COLS], pos[:]))
            line.do(dve.memset(place[:, COLS:COLS + PAD], 0))

            dve.wait_ge(iotas, 1)
            line.do(dve.tensor_copy(turn_id[:], turn_i[0:1, :]))
            line.do(dve.memset(group[:], 0.0))
            for g in range(GROUPS - 1):
                line.do(dve.tensor_scalar(ended[:], turn_id[:], before[0:1, g:g + 1], None, ALU.is_ge))
                line.do(dve.tensor_tensor(group[:], group[:], ended[:], ALU.add))
            line.do(dve.tensor_copy(G.group[:], group[:]))

            line.do(dve.tensor_scalar(spare[:], c.lane[:].to_broadcast([P, HI]), float(HI),
                                      float(G_TURNS * PLACES), ALU.mult, ALU.add))
            line.do(dve.tensor_tensor(spare[:], spare[:], c.free[:, 0:HI], ALU.add))
            line.do(dve.memset(node_start[:], 0))
            counting.end(dve, counts)
            for g in range(GROUPS):
                line.do(dve.tensor_scalar(run[:], counts[:, :, g], 1.0, None, ALU.mult))
                dve.sem_inc(ready, 1)
                dve.wait_ge(looked, g + 1)
                line.do(dve.tensor_copy(lower[:], p_cnt[:, P:P + HI]))
                line.do(dve.tensor_tensor_scan(start[:], ones[:, 0:HI], lower[:], 0.0, ALU.mult, ALU.add))
                line.do(dve.tensor_tensor(start[:], start[:], lower[:], ALU.subtract))
                line.do(dve.tensor_tensor(start[:], start[:], p_cnt[:, 0:HI], ALU.add))
                line.do(dve.scalar_tensor_tensor(out=start[:], in0=start[:], scalar=first[:, g:g + 1], in1=spare[:],
                                                 op0=ALU.add, op1=ALU.subtract))
                line.do(dve.tensor_scalar(used[:], run[:], 1.0, None, ALU.min))
                line.do(dve.tensor_tensor(start[:], start[:], used[:], ALU.mult))
                line.do(dve.tensor_tensor(node_start[:, :, g], start[:], spare[:], ALU.add))
                line.do(dve.tensor_scalar(spare[:], spare[:], float(ROWS), None, ALU.add))
            dve.sem_inc(ready, 1)

        @block.tensor
        def _(pe):
            counting.carry.tensor(pe, c, runs)
            pe.wait_ge(counted, 1)
            pe.matmul(p_sum[:, 0:T], c.ones[:], totals[:], start=True, stop=True)
            pe.matmul(p_sum[:, P:P + T], c.above[:], totals[:], start=True, stop=True).then_inc(summed, 1)
            for g in range(GROUPS):
                pe.wait_ge(ready, g + 1)
                pe.matmul(p_cnt[:, 0:HI], c.above[:], run[:], start=True, stop=True)
                pe.matmul(p_cnt[:, P:P + HI], c.ones[:], run[:], start=True, stop=True).then_inc(looked, 1)

        @block.sync
        def _(sp):
            sp.wait_ge(ready, GROUPS + 1)
            sp.dma_start(starts.rearrange("(h p) t -> p h t", p=P), node_start[:]).then_inc(stored, 16)
            sp.wait_ge(stored, 16)


def group_ids(nc, source, groups, scratch):
    with Scope(nc, "ids") as s:
        line_sem = s.sem("line")
        block = s.block()

        @block.vector
        def _(dve):
            line = Line(dve, line_sem)
            whole = scratch[:, 0:COLS]
            line.do(dve.tensor_copy(whole, source[:]))
            line.do(dve.tensor_scalar(whole, whole, (8 * WINDOW).bit_length() - 1, None,
                                      ALU.arith_shift_right))
            line.do(dve.tensor_copy(groups[:], whole))


def place_edges(nc, c, place, rec, grouped, runs, kinds, sums, counts):
    with Scope(nc, "place") as s:
        record = s.sb("record", [P, SLOTS, COLS_SLOT, WORDS])
        at = s.sb("at", [P, SLOTS, COLS_SLOT], I32)
        landed, staged = s.sems("landed", SLOTS), s.sem("staged")
        scattered, gate = s.sems("scattered", SLOTS), s.sem("gate")
        counting = Counting(s, runs, kinds, sums)
        block = s.block()
        view = rec.rearrange("(p c) w -> p (c w)", p=P)

        @block.sync
        def _(sp):
            def body(turn, first):
                for k in range(SLOTS):
                    if not first:
                        sp.wait_ge(scattered[k], turn * (16 * COLS_SLOT))
                    n = turn * SLOTS + k
                    sp.dma_start(record[:, k].rearrange("p c w -> p (c w)"),
                                 view[:, bass.ds(n * (COLS_SLOT * WORDS), COLS_SLOT * WORDS)]).then_inc(landed[k], 16)

            loop(sp, PASS_TURNS, body)

        @block.scalar
        def _(act):
            counting.scalar(act)

        @block.vector
        def _(dve):
            counting.begin(dve)
            for k in range(SLOTS):
                dve.tensor_copy(at[:, k, :], place[:, k * COLS_SLOT:(k + 1) * COLS_SLOT]).then_inc(staged, 1)
            with dve.Fori(0, PASS_TURNS) as turn:
                for k in range(SLOTS):
                    counting.slot(dve, c, turn, k)
                    dve.wait_ge(scattered[k], (turn + 1) * (16 * COLS_SLOT))
                    dve.tensor_copy(at[:, k, :], place[:, bass.ds((turn * SLOTS + k) * COLS_SLOT + PAD, COLS_SLOT)]
                                    ).then_inc(staged, 1)
            counting.last(dve)
            counting.end(dve, counts)

        @block.tensor
        def _(pe):
            counting.carry.tensor(pe, c, runs)

        @block.gpsimd
        def _(pool):
            with pool.Fori(0, PASS_TURNS) as turn:
                for k in range(SLOTS):
                    pool.wait_ge(staged, turn * SLOTS + k + 1)
                    pool.sem_inc(gate, 1)
                    pool.wait_ge(landed[k], turn * 16 + 16)
                    pool.sem_inc(gate, 1)
                    for j in range(COLS_SLOT):
                        pool.indirect_dma_start(grouped, bass.IndirectOffsetOnAxis(at[:, k, j:j + 1], 0),
                                                record[:, k, j, :], None).then_inc(scattered[k], 16)
            for k in range(SLOTS):
                pool.wait_ge(scattered[k], PASS_TURNS * 16 * COLS_SLOT)
            counting.gather(pool)


G_RING = 4
PAIR = 2
assert G_TURNS % G_RING == 0 and G_RING % PAIR == 0


def load_places(nc, grouped, G, weight, goes_on, first_node):
    with Scope(nc, "held") as s:
        recs = s.sb("recs", [P, G_RING, TURN, WORDS])
        source = s.sb("source", [P, G_COLS])
        ids, got = s.sb("ids", [P, G_COLS], I32), s.sb("got", [P, G_COLS], I32)
        landed, taken_a, taken_v, line_sem = s.sems("landed", G_RING), s.sem("taken_a"), s.sem("taken_v"), s.sem("line")
        block = s.block()
        view = grouped.rearrange("(t p c) w -> t p (c w)", p=P, c=TURN)

        @block.sync
        def _(sp):
            def body(it, first):
                for k in range(G_RING):
                    n = it * G_RING + k
                    if not first:
                        sp.wait_ge(taken_a, n - G_RING + 1)
                        sp.wait_ge(taken_v, n - G_RING + 1)
                    sp.dma_start(recs[:, k].rearrange("p c w -> p (c w)"),
                                 view[bass.ds(n, 1)].rearrange("t p w -> (t p) w")).then_inc(landed[k], 16)

            loop(sp, G_TURNS // G_RING, body)

        @block.scalar
        def _(act):
            def body(it, first):
                for k in range(G_RING):
                    cols = bass.ds((it * G_RING + k) * TURN, TURN)
                    act.wait_ge(landed[k], it * 16 + 16)
                    act.copy(weight[:, cols], recs[:, k, :, WEIGHT])
                    act.copy(source[:, cols], recs[:, k, :, SOURCE]).then_inc(taken_a, 1)

            loop(act, G_TURNS // G_RING, body)

        @block.vector
        def _(dve):
            def body(it, first):
                for k in range(G_RING):
                    n = it * G_RING + k
                    dve.wait_ge(landed[k], it * 16 + 16)
                    dve.tensor_copy(G.index[:, bass.ds(n * TURN, TURN)], recs[:, k, :, DST_ROW])
                    dve.tensor_tensor(goes_on[:, bass.ds(n * TURN + 1, TURN - 1)], recs[:, k, 1:TURN, DST_ROW],
                                      recs[:, k, 0:TURN - 1, DST_ROW], ALU.is_equal)
                    dve.scalar_tensor_tensor(out=first_node[:, bass.ds(n, 1)], in0=recs[:, k, 0:1, DST_HI],
                                             scalar=float(P), in1=recs[:, k, 0:1, DST_LO],
                                             op0=ALU.mult, op1=ALU.add).then_inc(taken_v, 1)

            loop(dve, G_TURNS // G_RING, body)
            line = Line(dve, line_sem)
            dve.wait_ge(taken_v, G_TURNS)
            dve.wait_ge(taken_a, G_TURNS)
            line.do(dve.memset(goes_on[:, 0::TURN], 0.0))
            line.do(dve.tensor_copy(G.index[:, G_COLS:G_COLS + TURN], G.index[:, 0:TURN]))
            line.do(dve.tensor_scalar(ids[:], source[:], -1.0, None, ALU.add))
            line.do(dve.tensor_scalar(got[:], ids[:], 7, None, ALU.bitwise_and))
            line.do(dve.tensor_copy(G.a[:], got[:]))
            line.do(dve.tensor_scalar(source[:], source[:], 1.0, None, ALU.min))
            line.do(dve.tensor_scalar(source[:], source[:], 16.0, -16.0, ALU.mult, ALU.add))
            line.do(dve.tensor_tensor(G.a[:], G.a[:], source[:], ALU.add))
            line.do(dve.tensor_scalar(got[:], ids[:], 3, WINDOW - 1, ALU.arith_shift_right, ALU.bitwise_and))
            line.do(dve.tensor_copy(G.b[:], got[:]))


class Gathering:

    def __init__(self, s):
        self.zeros = s.sb("zeros", [P, PIECE], BF16)
        self.sums = s.ps("sums", [P, 4 * PIECE])
        self.moved = s.sb("moved", [P, B_ALL])
        self.pt = s.ps("turned_rows", [P, 2, PIECE])
        self.by_b = s.sb("by_b", [P, B_BLOCKS, 8 * D])
        self.blank, self.emptied, self.flips, self.copied, self.done = (
            s.sem(n) for n in ("blank", "emptied", "flips", "copied", "rows_done"))

    def clear(self, pe):
        for at in range(0, 4 * PIECE, PIECE):
            pe.matmul(self.sums[:, at:at + PIECE], self.zeros[:, 0:P], self.zeros[:], start=True, stop=True)

    def tensor(self, pe, c, r):
        pe.wait_ge(self.emptied, r * 4 + 4)
        for k in range(B_BLOCKS):
            n = min(P, B_ALL - k * P)
            if k >= 2:
                pe.wait_ge(self.copied, r * B_BLOCKS + (k - 1))
            pe.transpose(self.pt[0:n, k % 2, 0:P], self.moved[:, k * P:k * P + n], c.ident[:]).then_inc(self.flips, 1)

    def scalar(self, act, r):
        for at in range(0, B_ALL, PIECE):
            to = min(at + PIECE, B_ALL)
            act.copy(self.moved[:, at:to], self.sums[:, at:to]).then_inc(self.emptied, 1)
        for k in range(B_BLOCKS):
            n = min(P, B_ALL - k * P)
            act.wait_ge(self.flips, r * B_BLOCKS + k + 1)
            act.copy(self.by_b[0:n, k, :], self.pt[0:n, k % 2, 0:P]).then_inc(self.copied, 1)

    def rows(self, dram):
        full = B_ALL // P
        cut = full * P * 8
        return [(slice(0, P), slice(0, full), dram[0:cut].rearrange("(k p a) d -> p k (a d)", p=P, a=8)),
                (slice(0, B_ALL - full * P), slice(full, full + 1),
                 dram[cut:ROWS].rearrange("(k p a) d -> p k (a d)", k=1, a=8))]


def by_hi(dram):
    return dram.rearrange("(h p) d -> p h d", p=P)


def spread_slot(dve, message, a_hot, spread, b_val, b_hot, c, ready):
    n = message.shape[1]
    dve.tensor_tensor(spread, a_hot.unsqueeze(3).to_broadcast([P, n, 8, D]),
                      message.unsqueeze(2).to_broadcast([P, n, 8, D]), ALU.mult)
    for j in range(n):
        ins = dve.tensor_scalar(b_hot[:, j, :], c.wide[:], b_val[:, j:j + 1], None, ALU.is_equal)
    ins.then_inc(ready, 1)


def add_slot(pe, gathering, group, spread, b_hot, taken):
    for j in range(TILES):
        mm = pe.matmul(gathering.sums[:, bass.ds(group * WINDOW, WINDOW)],
                       spread[:, j].rearrange("p a d -> p (a d)"), b_hot[:, j, :],
                       start=False, stop=True, skip_group_check=True)
    mm.then_inc(taken, 1)


def powers(nc, c, G, weight, goes_on, first_node, starts, filled, node_rows, H, Y, rounds,
           inverses):
    with Scope(nc, "powers") as s:
        at_start = s.sb("at_start", [P, B_BLOCKS, 8, T], I32)
        given = s.sb("given", [P, G_RING, TURN, D])
        first = s.sb("first", [P, G_TURNS, D])
        along = s.sb("along", [P, PAIR * TURN, D])
        message = s.sb("message", [P, PAIR * TURN, D])
        a_hot = s.sb("a_hot", [P, PAIR * TURN, 8])
        b_val = s.sb("b_val", [P, PAIR * TURN])
        spread = s.sb("spread", [P, SLOTS, TILES, 8, D])
        b_hot = s.sb("b_hot", [P, SLOTS, TILES, WINDOW])
        g = Gathering(s)
        given_in = s.sems("given_in", G_RING)
        (y_in, starts_in, y_out, spread_out, first_in, groups_ready, firsts_ready, expanded, begun, mid, ready, taken,
         gate, last_in, inverses_out) = (s.sem(n) for n in (
            "y_in", "starts_in", "y_out", "spread_out", "first_in", "groups_ready", "firsts_ready", "expanded", "begun",
            "mid", "ready", "taken", "gate", "last_in", "inverses_out"))
        block = s.block()
        places = filled[0:G_TURNS * PLACES, :].rearrange("(t p c) d -> t p (c d)", p=P, c=TURN)
        per_group = -(-G_TURNS // GROUPS)

        @block.sync
        def _(sp):
            for lanes, ks, dram in g.rows(starts):
                sp.dma_start(at_start[lanes, ks].rearrange("p k a t -> p k (a t)"), dram).then_inc(starts_in, 16)
            sp.dma_start(by_hi(node_rows), H[:]).then_inc(y_out, 16)
            sp.wait_ge(y_out, 16)
            for lanes, ks, dram in g.rows(node_rows):
                sp.dma_start(g.by_b[lanes, ks], dram).then_inc(y_in, 16)
            with sp.Fori(0, rounds) as r:
                with sp.Fori(0, G_TURNS // G_RING) as it:
                    for k in range(G_RING):
                        turn = it * G_RING + k
                        group = sp.value_load(G.group[0:1, bass.ds(turn, 1)], min_val=0, max_val=GROUPS - 1)
                        sp.wait_ge(groups_ready, r * GROUPS + group + 1)
                        sp.wait_ge(expanded, r * G_TURNS + turn + 1)
                        sp.dma_start(given[:, k].rearrange("p c d -> p (c d)"),
                                     places[bass.ds(turn, 1)].rearrange("t p w -> (t p) w")).then_inc(given_in[k], 16)
                sp.wait_ge(g.copied, r * B_BLOCKS + B_BLOCKS)
                for lanes, ks, dram in g.rows(node_rows):
                    sp.dma_start(dram, g.by_b[lanes, ks]).then_inc(y_in, 16)
            sp.wait_ge(y_in, 32 * (rounds + 1))
            sp.dma_start(Y[:], by_hi(node_rows)).then_inc(last_in, 16)
            sp.wait_ge(last_in, 16)

        @block.gpsimd
        def _(pool):
            pool.wait_ge(starts_in, 32)
            pool.sem_inc(gate, 1)
            with pool.Fori(0, rounds) as r:
                pool.wait_ge(y_in, r * 32 + 32)
                pool.sem_inc(gate, 1)
                for i in range(GROUPS):
                    for k in range(B_BLOCKS):
                        n = min(P, B_ALL - k * P)
                        for a in range(8):
                            pool.indirect_dma_start(filled, bass.IndirectOffsetOnAxis(at_start[0:n, k, a, i:i + 1], 0),
                                                    g.by_b[0:n, k, a * D:(a + 1) * D], None).then_inc(spread_out, 16)
                    upto = min((i + 1) * per_group, G_TURNS)
                    for turn in range(i * per_group, upto):
                        pool.indirect_dma_start(first[:, turn, :], None, node_rows,
                                                bass.IndirectOffsetOnAxis(first_node[:, turn:turn + 1], 0)
                                                ).then_inc(first_in, 16)
                    pool.wait_ge(spread_out, r * (16 * 8 * B_BLOCKS * GROUPS) + 16 * 8 * B_BLOCKS * (i + 1))
                    pool.sem_inc(groups_ready, 1)
                    pool.wait_ge(first_in, r * (16 * G_TURNS) + 16 * upto)
                    pool.sem_inc(firsts_ready, upto - i * per_group)
            inverses.spread(pool, inverses_out)

        @block.vector
        def _(dve):
            dve.memset(g.zeros[:], 0.0).then_inc(g.blank, 1)
            dve.sem_inc(expanded, G_RING)
            with dve.Fori(0, rounds) as r:
                with dve.Fori(0, G_TURNS // G_RING) as it:
                    for h in range(G_RING // PAIR):
                        pair = it * (G_RING // PAIR) + h
                        n = r * (G_TURNS // PAIR) + pair
                        ks = slice(h * PAIR, (h + 1) * PAIR)
                        cols = bass.ds(pair * (PAIR * TURN), PAIR * TURN)
                        for given_sem in given_in[ks]:
                            dve.wait_ge(given_sem, r * (G_TURNS // G_RING * 16) + it * 16 + 16)
                        dve.wait_ge(firsts_ready, (n + 1) * PAIR)
                        dve.tensor_scalar(given[:, ks, 0, :], first[:, bass.ds(pair * PAIR, PAIR), :],
                                          1.0, None, ALU.mult).then_inc(begun, 1)
                        dve.wait_ge(begun, n + 1)
                        rows = given[:, ks].rearrange("p k c f -> p (k c) f")
                        for f in range(D):
                            ins = dve.tensor_tensor_scan(along[:, :, f], goes_on[:, cols], rows[:, :, f], 0.0,
                                                         ALU.mult, ALU.add)
                        ins.then_inc(expanded, PAIR)
                        dve.tensor_tensor(a_hot[:], G.a[:, cols].unsqueeze(2).to_broadcast([P, PAIR * TURN, 8]),
                                          c.free[:, 0:8].unsqueeze(1).to_broadcast([P, PAIR * TURN, 8]), ALU.is_equal)
                        dve.tensor_scalar(b_val[:], G.b[:, cols], 1.0, None, ALU.mult)
                        dve.wait_ge(expanded, (n + 1) * PAIR + G_RING)
                        dve.tensor_tensor(message[:], along[:], weight[:, cols].unsqueeze(2)
                                          .to_broadcast([P, PAIR * TURN, D]), ALU.mult).then_inc(mid, 1)
                        dve.wait_ge(mid, n + 1)
                        for j in range(PAIR * SLOTS):
                            dve.wait_ge(taken, n * (PAIR * SLOTS) + j + 1)
                            at = slice(j * TILES, (j + 1) * TILES)
                            spread_slot(dve, message[:, at], a_hot[:, at], spread[:, j % SLOTS], b_val[:, at],
                                        b_hot[:, j % SLOTS], c, ready)
                        dve.wait_ge(ready, (n + 1) * (PAIR * SLOTS))

        @block.tensor
        def _(pe):
            pe.wait_ge(g.blank, 1)
            pe.sem_inc(taken, SLOTS)
            with pe.Fori(0, rounds) as r:
                g.clear(pe)
                with pe.Fori(0, G_TURNS) as turn:
                    group = pe.value_load(G.group[0:1, bass.ds(turn, 1)], min_val=0, max_val=GROUPS - 1)
                    for j in range(SLOTS):
                        pe.wait_ge(ready, (r * G_TURNS + turn) * SLOTS + j + 1)
                        add_slot(pe, g, group, spread[:, j], b_hot[:, j], taken)
                g.tensor(pe, c, r)

        @block.scalar
        def _(act):
            with act.Fori(0, rounds) as r:
                act.wait_ge(taken, (r + 1) * (G_TURNS * SLOTS) + SLOTS)
                g.scalar(act, r)


def contracted_sums(nc, c, name, G, table, grouped, node_rows, Y, width, hats=False, silu_scale=None):
    with Scope(nc, name) as s:
        picked = s.sb("picked", [P, SLOTS, TILES, width, D])
        staged = s.sb("staged", [P, SLOTS, TILES], I32)
        recs = s.sb("recs", [P, SLOTS, TILES, WORDS])
        product = s.sb("product", [P, TILES, width, D])
        message = s.sb("message", [P, SLOTS, TILES, D])
        active = s.sb("active", [P, SLOTS, TILES, D]) if silu_scale is not None else message
        a_hot = s.sb("a_hot", [P, TILES, 8])
        b_val = s.sb("b_val", [P, TILES])
        spread = s.sb("spread", [P, SLOTS, TILES, 8, D])
        b_hot = s.sb("b_hot", [P, SLOTS, TILES, WINDOW])
        if hats:
            centers = s.sb("centers", [P, 5])
            far = s.sb("far", [P, TILES, 2, 4])
            hat = s.sb("hat", [P, SLOTS, TILES, 2, 4])
            coef = s.sb("coef", [P, TILES, 4, 4])
        g = Gathering(s)
        staged_done, gathered, recs_in = s.sems("staged_done", SLOTS), s.sems("gathered", SLOTS), s.sems("recs_in", SLOTS)
        times, summed, activated, set_up, farther, hatted, coefs, gate, mid, ready, taken, y_out, last_in = (
            s.sem(n) for n in ("times", "summed", "activated", "set_up", "farther", "hatted", "coefs", "gate", "mid",
                               "ready", "taken", "y_out", "last_in"))
        block = s.block()
        places = grouped.rearrange("(t p c) w -> t p (c w)", p=P, c=TURN)

        @block.sync
        def _(sp):
            def body(turn, first):
                for k in range(SLOTS):
                    if not first:
                        sp.wait_ge(summed, (turn - 1) * SLOTS + k + 1)
                        if hats:
                            sp.wait_ge(hatted, (turn - 1) * SLOTS + k + 1)
                    src = places[bass.ds(turn, 1), :, k * TILES * WORDS:(k + 1) * TILES * WORDS]
                    sp.dma_start(recs[:, k].rearrange("p c w -> p (c w)"), src.rearrange("t p w -> (t p) w")
                                 ).then_inc(recs_in[k], 16)

            loop(sp, G_TURNS, body)
            sp.wait_ge(g.copied, B_BLOCKS)
            for lanes, ks, dram in g.rows(node_rows):
                sp.dma_start(dram, g.by_b[lanes, ks]).then_inc(y_out, 16)
            sp.wait_ge(y_out, 32)
            sp.dma_start(Y[:], by_hi(node_rows)).then_inc(last_in, 16)
            sp.wait_ge(last_in, 16)

        @block.gpsimd
        def _(pool):
            with pool.Fori(0, G_TURNS) as turn:
                for k in range(SLOTS):
                    pool.wait_ge(staged_done[k], turn + 1)
                    pool.sem_inc(gate, 1)
                    for j in range(TILES):
                        pool.indirect_dma_start(picked[:, k, j].rearrange("p w d -> p (w d)"), None, table,
                                                bass.IndirectOffsetOnAxis(staged[:, k, j:j + 1], 0)
                                                ).then_inc(gathered[k], 16)

        @block.scalar
        def _(act):
            if hats:
                act.wait_ge(set_up, 1)

            def body(turn, first):
                for k in range(SLOTS):
                    n = turn * SLOTS + k
                    if hats:
                        act.wait_ge(recs_in[k], turn * 16 + 16)
                        if not first:
                            act.wait_ge(coefs, (turn - 1) * SLOTS + k + 1)
                        if not first or k:
                            act.wait_ge(hatted, n)
                        for v in range(4):
                            ins = act.activation(far[:, :, :, v], recs[:, k, :, ATTR2:ATTR2 + 2], ACT.Abs,
                                                 bias=centers[:, v:v + 1], scale=1.5)
                        ins.then_inc(farther, 1)
                        act.wait_ge(farther, n + 1)
                        act.activation(hat[:, k], far[:], ACT.Relu, bias=centers[:, 4:5], scale=-1.0
                                       ).then_inc(hatted, 1)
                    if silu_scale is not None:
                        act.wait_ge(summed, n + 1)
                        if not first:
                            act.wait_ge(ready, (turn - 1) * SLOTS + k + 1)
                        act.activation(active[:, k], message[:, k], ACT.Silu, scale=silu_scale
                                       ).then_inc(activated, 1)

            loop(act, G_TURNS, body)
            act.wait_ge(taken, G_TURNS * SLOTS)
            g.scalar(act, 0)

        @block.vector
        def _(dve):
            if hats:
                for v, at in enumerate((1.5, 0.5, -0.5, -1.5, 1.0)):
                    ins = dve.memset(centers[:, v:v + 1], at)
                ins.then_inc(set_up, 1)
            dve.memset(g.zeros[:], 0.0).then_inc(g.blank, 1)
            for k in range(SLOTS):
                dve.tensor_copy(staged[:, k, :], G.index[:, k * TILES:(k + 1) * TILES]).then_inc(staged_done[k], 1)

            def body(turn, first):
                for k in range(SLOTS):
                    n = turn * SLOTS + k
                    at = turn * TURN + k * TILES
                    dve.wait_ge(recs_in[k], turn * 16 + 16)
                    if hats:
                        dve.wait_ge(hatted, n + 1)
                        dve.tensor_tensor(coef[:], hat[:, k, :, 0, :].unsqueeze(3).to_broadcast([P, TILES, 4, 4]),
                                          hat[:, k, :, 1, :].unsqueeze(2).to_broadcast([P, TILES, 4, 4]),
                                          ALU.mult).then_inc(coefs, 1)
                        dve.wait_ge(coefs, n + 1)
                        co = coef[:].rearrange("p t a b -> p t (a b)")
                    else:
                        co = recs[:, k, :, ATTR8:ATTR8 + width]
                    dve.wait_ge(gathered[k], (turn + 1) * (16 * TILES))
                    if not first or k:
                        dve.wait_ge(ready, n)
                    dve.tensor_tensor(product[:], picked[:, k], co.unsqueeze(3).to_broadcast([P, TILES, width, D]),
                                      ALU.mult).then_inc(times, 1)
                    dve.wait_ge(times, n + 1)
                    dve.tensor_copy(staged[:, k, :], G.index[:, bass.ds(at + TURN, TILES)]
                                    ).then_inc(staged_done[k], 1)
                    dve.tensor_reduce(message[:, k], product[:].rearrange("p t w d -> p t d w"), AX.X, ALU.add
                                      ).then_inc(summed, 1)
                    dve.tensor_tensor(a_hot[:], G.a[:, bass.ds(at, TILES)].unsqueeze(2).to_broadcast([P, TILES, 8]),
                                      c.free[:, 0:8].unsqueeze(1).to_broadcast([P, TILES, 8]), ALU.is_equal)
                    dve.tensor_scalar(b_val[:], G.b[:, bass.ds(at, TILES)], 1.0, None, ALU.mult).then_inc(mid, 1)
                    dve.wait_ge(mid, n + 1)
                    dve.wait_ge(summed if silu_scale is None else activated, n + 1)
                    if not first:
                        dve.wait_ge(taken, (turn - 1) * SLOTS + k + 1)
                    spread_slot(dve, active[:, k], a_hot[:], spread[:, k], b_val[:], b_hot[:, k], c, ready)

            loop(dve, G_TURNS, body)

        @block.tensor
        def _(pe):
            pe.wait_ge(g.blank, 1)
            g.clear(pe)
            with pe.Fori(0, G_TURNS) as turn:
                group = pe.value_load(G.group[0:1, bass.ds(turn, 1)], min_val=0, max_val=GROUPS - 1)
                for k in range(SLOTS):
                    pe.wait_ge(ready, turn * SLOTS + k + 1)
                    add_slot(pe, g, group, spread[:, k], b_hot[:, k], taken)
            g.tensor(pe, c, 0)


def project(nc, c, name, src, weight, width, out=None, table=None):
    wide = BLOCK * width
    with Scope(nc, name) as s:
        diag = s.sb("diag", [BLOCK * D, BLOCK, width])
        turned = s.sb("turned", [BLOCK * D, 2, P])
        rows = s.sb("rows", [P, 2, wide]) if out is None else None
        pt = s.ps("turned_ps", [P, 2, PIECE])
        pp = s.ps("product", [P, 4, PIECE])
        zeroed, weights_in, flipped, copied, made, moved = (
            s.sem(n) for n in ("zeroed", "weights_in", "flipped", "copied", "made", "moved"))
        stored = s.sems("stored", 2)
        block = s.block()
        pieces = [(b, at, min(at + PIECE, wide)) for b in range(BLOCKS) for at in range(0, wide, PIECE)]
        per = len(pieces) // BLOCKS

        @block.sync
        def _(sp):
            sp.wait_ge(zeroed, 1)
            for j in range(BLOCK):
                to = diag[j * D:(j + 1) * D, j, :]
                if len(weight.shape) == 3:
                    to = to.rearrange("p (a d) -> p a d", d=D)
                sp.dma_start(to, weight).then_inc(weights_in, 16)
            if out is None:
                view = table.rearrange("(p h) w -> p (h w)", p=P)
                for b in range(BLOCKS):
                    sp.wait_ge(moved, (b + 1) * per)
                    sp.dma_start(view[:, b * wide:(b + 1) * wide], rows[:, b % 2, :]).then_inc(stored[b % 2], 16)
                for half in stored:
                    sp.wait_ge(half, 16 * (BLOCKS // 2))

        @block.vector
        def _(dve):
            dve.memset(diag[:], 0.0).then_inc(zeroed, 1)
            for b in range(BLOCKS):
                dve.wait_ge(flipped, b + 1)
                if b >= 2:
                    dve.wait_ge(made, (b - 1) * per)
                dve.tensor_copy(turned[:, b % 2, :], pt[0:BLOCK * D, b % 2, 0:P]).then_inc(copied, 1)

        @block.tensor
        def _(pe):
            def turn(b):
                if b >= 2:
                    pe.wait_ge(copied, b - 1)
                pe.transpose(pt[0:BLOCK * D, b % 2, 0:P],
                             src[:, b * BLOCK:(b + 1) * BLOCK, :].rearrange("p h d -> p (h d)"),
                             c.ident[:]).then_inc(flipped, 1)

            turn(0)
            pe.wait_ge(weights_in, 16 * BLOCK)
            flat = diag[:].rearrange("p h w -> p (h w)")
            for n, (b, at, to) in enumerate(pieces):
                if at == 0:
                    if b + 1 < BLOCKS:
                        turn(b + 1)
                    pe.wait_ge(copied, b + 1)
                if n >= 4:
                    pe.wait_ge(moved, n - 3)
                pe.matmul(pp[:, n % 4, 0:to - at], turned[:, b % 2, :], flat[:, at:to],
                          start=True, stop=True).then_inc(made, 1)

        @block.scalar
        def _(act):
            for n, (b, at, to) in enumerate(pieces):
                act.wait_ge(made, n + 1)
                if out is None:
                    if b >= 2 and at == 0:
                        act.wait_ge(stored[b % 2], 16 * (b // 2))
                    dest = rows[:, b % 2, at:to]
                else:
                    dest = out[:, b * BLOCK:(b + 1) * BLOCK, :].rearrange("p h w -> p (h w)")[:, at:to]
                act.copy(dest, pp[:, n % 4, 0:to - at]).then_inc(moved, 1)


def by_node(a):
    return a.unsqueeze(2).to_broadcast([P, HI, D])


def layernorm(nc, name, X, H):
    with Scope(nc, name) as s:
        mean, var, dev, inv = (s.sb(n, [P, HI]) for n in ("mean", "var", "dev", "inv"))
        square = s.sb("square", [P, HI, D])
        line_sem, spread, rooted = s.sem("line"), s.sem("spread"), s.sem("rooted")
        block = s.block()

        @block.vector
        def _(dve):
            line = Line(dve, line_sem)
            line.do(dve.tensor_reduce(mean[:], X[:], AX.X, ALU.add))
            line.do(dve.tensor_scalar(mean[:], mean[:], 1.0 / D, None, ALU.mult))
            line.do(dve.tensor_tensor(H[:], X[:], by_node(mean[:]), ALU.subtract))
            line.do(dve.tensor_tensor(square[:], H[:], H[:], ALU.mult))
            line.do(dve.tensor_reduce(var[:], square[:], AX.X, ALU.add))
            dve.tensor_scalar(var[:], var[:], 1.0 / D, 1e-5, ALU.mult, ALU.add).then_inc(spread, 1)
            dve.wait_ge(rooted, 1)
            line.do(dve.reciprocal(inv[:], dev[:]))
            line.do(dve.tensor_tensor(H[:], H[:], by_node(inv[:]), ALU.mult))
            line.do(dve.tensor_scalar(H[:], H[:], 0.0, None, ALU.max))

        @block.scalar
        def _(act):
            act.wait_ge(spread, 1)
            act.activation(dev[:], var[:], ACT.Sqrt).then_inc(rooted, 1)


def add_nodes(nc, name, out, terms, bias=None, relu=False):
    with Scope(nc, name) as s:
        wide = s.sb("wide", [P, D])
        bias_in, line_sem = s.sem("bias_in"), s.sem("line")
        block = s.block()

        @block.sync
        def _(sp):
            if bias is not None:
                sp.dma_start(wide[:], bias.unsqueeze(0).to_broadcast([P, D])).then_inc(bias_in, 16)
                sp.wait_ge(bias_in, 16)

        @block.vector
        def _(dve):
            line = Line(dve, line_sem)
            line.do(dve.tensor_tensor(out[:], terms[0][:], terms[1][:], ALU.add))
            for term in terms[2:]:
                line.do(dve.tensor_tensor(out[:], out[:], term[:], ALU.add))
            if bias is not None:
                dve.wait_ge(bias_in, 16)
                line.do(dve.tensor_tensor(out[:], out[:], wide[:].unsqueeze(1).to_broadcast([P, HI, D]), ALU.add))
            if relu:
                line.do(dve.tensor_scalar(out[:], out[:], 0.0, None, ALU.max))


def add_log_softmax(nc, name, X, Z):
    with Scope(nc, name) as s:
        top, total, log = (s.sb(n, [P, HI]) for n in ("top", "total", "log"))
        powers = s.sb("powers", [P, HI, D])
        line_sem, lowered, raised, totals, logs = (s.sem(n) for n in ("line", "lowered", "raised", "totals", "logs"))
        block = s.block()

        @block.vector
        def _(dve):
            line = Line(dve, line_sem)
            line.do(dve.tensor_reduce(top[:], Z[:], AX.X, ALU.max))
            dve.tensor_tensor(Z[:], Z[:], by_node(top[:]), ALU.subtract).then_inc(lowered, 1)
            dve.wait_ge(raised, 1)
            dve.tensor_reduce(total[:], powers[:], AX.X, ALU.add).then_inc(totals, 1)
            dve.wait_ge(logs, 1)
            line.do(dve.tensor_tensor(Z[:], Z[:], by_node(log[:]), ALU.subtract))
            line.do(dve.tensor_tensor(X[:], X[:], Z[:], ALU.add))

        @block.scalar
        def _(act):
            act.wait_ge(lowered, 1)
            act.activation(powers[:], Z[:], ACT.Exp).then_inc(raised, 1)
            act.wait_ge(totals, 1)
            act.activation(log[:], total[:], ACT.Ln).then_inc(logs, 1)


def update(nc, name, V, agg, U, scale):
    with Scope(nc, name) as s:
        line_sem, summed = s.sem("line"), s.sem("summed")
        block = s.block()

        @block.vector
        def _(dve):
            line = Line(dve, line_sem)
            v = V[:].rearrange("p n (h k) -> p (n h) k", k=D)
            a = agg[:].rearrange("p n h -> p (n h)").unsqueeze(2).to_broadcast([P, HI * D, D])
            line.do(dve.tensor_tensor(v, v, a, ALU.mult))
            dve.tensor_reduce(U[:], V[:].rearrange("p n (h k) -> p n k h", k=D), AX.X, ALU.add).then_inc(summed, 1)

        @block.scalar
        def _(act):
            act.wait_ge(summed, 1)
            act.activation(U[:], U[:], ACT.Silu, scale=scale).then_inc(line_sem, 1)


def finish(nc, X, H, U, scale, out):
    with Scope(nc, "finish") as s:
        line_sem, ready, stored = s.sem("line"), s.sem("ready"), s.sem("stored")
        block = s.block()

        @block.vector
        def _(dve):
            line = Line(dve, line_sem)
            line.do(dve.tensor_tensor(X[:], X[:], H[:], ALU.add))
            dve.scalar_tensor_tensor(out=X[:], in0=U[:], scalar=scale, in1=X[:], op0=ALU.mult, op1=ALU.add
                                     ).then_inc(ready, 1)

        @block.sync
        def _(sp):
            sp.wait_ge(ready, 1)
            sp.dma_start(out[0:FULL * P, :].rearrange("(h p) d -> p h d", p=P), X[:, 0:FULL, :]).then_inc(stored, 16)
            sp.dma_start(out[FULL * P:N_NODES, :], X[0:REST, FULL, :]).then_inc(stored, 16)
            sp.wait_ge(stored, 32)


def gnn_kernel(nc, x, src, dst, edge_attr_2, edge_attr_8, edge_type_8, edge_weight, L1_gnn_weight, L2_gnn_W1,
               L2_gnn_root1, L2_gnn_b1, L2_gnn_W2, L2_gnn_root2, L2_gnn_b2, L3_gnn_W_msg_tp, L3_gnn_W_msg_lin,
               L3_gnn_W_upd_tp, L3_gnn_W_upd_lin, out):
    def dram(name, shape, dt=F32):
        return nc.dram_tensor(name, shape, dt).ap()

    with ExitStack() as ctx:
        def sb(name, shape, dt=F32):
            return ctx.enter_context(nc.sbuf_tensor(name, shape, dt))

        c = Constants(sb)
        X, H, Y = (sb(n, [P, HI, D]) for n in "XHY")
        info = Info(sb, "dst")
        rec, grouped = dram("rec", (N_EDGES, WORDS)), dram("grouped", (G_TURNS * PLACES, WORDS))
        starts = dram("starts", (ROWS, T), I32)
        filled = dram("filled", (G_TURNS * PLACES + GROUPS * ROWS, D))
        type_sums = dram("type_sums", (N_EDGES, T))
        node_rows = dram("node_rows", (ROWS, D))
        inverses = Inverses(nc, sb)
        constants(nc, c, x, X)

        with Scope(nc, "keys") as s:
            k = Keys(s.sb)
            low_rows = dram("low_rows", (COLS, P), BF16)
            digits(nc, c, src, dst, edge_weight, edge_type_8, k)
            count(nc, c, "dst", k.lo, k.hi, info, 
                  [grouped, filled[0:G_TURNS * PLACES, :], inverses.filled[0:N_EDGES, :]])
            ordered = nc.values_load(k.ordered[0:1, 0:1], min_val=0, max_val=1)
            with nc.If(ordered == 1):
                copy_edges(nc, k, edge_attr_2, edge_attr_8, rec)
            with nc.Else():
                low_tiles(nc, c, k.lo, low_rows)
                sort_edges(nc, c, "dst", k.lo, k.hi, low_rows, info, WORDS,
                           [(WEIGHT, k.weight), (SOURCE, k.source), (DST_ROW, k.row), (DST_LO, k.lo), (DST_HI, k.hi),
                            (KIND, k.kind)], [(ATTR2, 2, edge_attr_2), (ATTR8, 8, edge_attr_8)], rec)

        with Scope(nc, "g") as gs:
            G = Places(gs.sb)
            runs = Runs(gs.sb, "by_dst", info)
            with Scope(nc, "order") as s:
                source, groups = s.sb("source", [P, COLS]), s.sb("groups", [P, COLS])
                place = s.sb("place", [P, COLS + PAD], I32)
                counts = s.sb("counts", [P, HI, T])
                load_runs(nc, c, "runs", rec, runs, source)
                group_ids(nc, source, groups, place)
                group_places(nc, c, runs, groups, type_sums, counts, place, starts, G)
                place_edges(nc, c, place, rec, grouped, runs, runs.weight, type_sums, counts)
                inverses.make(nc, c, runs, counts)

            with Scope(nc, "l0") as s:
                weight = s.sb("weight", [P, G_COLS])
                goes_on = s.sb("goes_on", [P, G_COLS], BF16)
                first_node = s.sb("first_node", [P, G_TURNS], I32)
                load_places(nc, grouped, G, weight, goes_on, first_node)
                layernorm(nc, "ln0", X, H)
                powers(nc, c, G, weight, goes_on, first_node, starts, filled, node_rows, H, Y, 4,
                       inverses)
            add_nodes(nc, "add0", X, [X, Y])

            layernorm(nc, "ln1", X, H)
            basis_rows = dram("L1_rows", (ROWS, 16 * D))
            project(nc, c, "basis", H, L1_gnn_weight.rearrange("u v i o -> i (u v) o"), 16 * D, table=basis_rows)
            contracted_sums(nc, c, "conv", G, basis_rows, grouped, node_rows, Y, 16, hats=True)
            add_nodes(nc, "add1", X, [X, Y])

            layernorm(nc, "ln2", X, H)
            with Scope(nc, "l2") as s:
                R = s.sb("R", [P, HI, D])
                sums = dram("sums", (N_EDGES, D))
                typed_rows = dram("L2_rows", (ROWS, T * D))
                by_type = typed_rows.rearrange("n (r d) -> (n r) d", r=T)
                for n, (W, root, b) in enumerate(((L2_gnn_W1, L2_gnn_root1, L2_gnn_b1),
                                                  (L2_gnn_W2, L2_gnn_root2, L2_gnn_b2))):
                    project(nc, c, f"typed{n}", H, W.rearrange("r i o -> i r o"), T * D, table=typed_rows)
                    project(nc, c, f"root{n}", H, root, D, out=R)
                    weighted_sums(nc, c, f"relate{n}", runs, by_type, sums, Y, inverses if n == 0 else None)
                    add_nodes(nc, f"add2{n}", H, [Y, R], bias=b, relu=n == 0)
            add_log_softmax(nc, "softmax", X, H)

            layernorm(nc, "ln3", X, H)
            message_rows = dram("L3_rows", (ROWS, 8 * D))
            project(nc, c, "bilinear", H, L3_gnn_W_msg_tp, 8 * D, table=message_rows)
            contracted_sums(nc, c, "message", G, message_rows, grouped, node_rows, Y, 8, silu_scale=(8 * D) ** -0.5)
        with Scope(nc, "l3") as s:
            R = s.sb("R3", [P, HI, D])
            V = s.sb("V", [P, HI, D * D])
            project(nc, c, "mix", Y, L3_gnn_W_msg_lin, D, out=R)
            project(nc, c, "upd", H, L3_gnn_W_upd_tp, D * D, out=V)
            update(nc, "update", V, R, Y, D ** -0.5 / D)
            project(nc, c, "last", Y, L3_gnn_W_upd_lin, D, out=R)
            finish(nc, X, H, R, D ** -0.5, out)

_INS = ['x', 'src', 'dst', 'edge_attr_2', 'edge_attr_8', 'edge_type_8', 'edge_weight', 'node_vec1',
        'L1_gnn_weight', 'L2_gnn_W1', 'L2_gnn_root1', 'L2_gnn_b1', 'L2_gnn_W2', 'L2_gnn_root2', 'L2_gnn_b2',
        'L3_gnn_W_msg_tp', 'L3_gnn_W_msg_lin', 'L3_gnn_W_upd_tp', 'L3_gnn_W_upd_lin']


def kernel(**inputs):
    import numpy as _np
    import concourse.bacc as _bacc
    from concourse import mybir as _mybir
    from concourse.bass_utils import run_bass_kernel_spmd as _run

    nc = _bacc.Bacc("TRN2", target_bir_lowering=False, num_devices=1)
    arrays, args = {}, {}
    for name in _INS:
        if name == 'node_vec1':
            continue
        a = _np.ascontiguousarray(inputs[name])
        arrays[f"in_{name}"] = a
        args[name] = nc.dram_tensor(f"in_{name}", a.shape, _mybir.dt.from_np(a.dtype), kind="ExternalInput").ap()
    out = nc.dram_tensor("out_x", (N_NODES, D), F32, kind="ExternalOutput").ap()
    gnn_kernel(nc, out=out, **args)
    r = _run(nc, [arrays], core_ids=[0])
    return r.results[0]["out_x"]
```
